# Optimizing a Trainium2 kernel written in Bass

```python
import numpy as np
import jax
import jax.numpy as jnp

def _softmax(x, axis=-1):
    return jax.nn.softmax(x, axis=axis)

def _gelu(x):
    return jax.nn.gelu(x, approximate=True)

def _silu(x):
    return jax.nn.silu(x)

def _sigmoid(x):
    return jax.nn.sigmoid(x)

def _layernorm(x, axis=-1, eps=1e-05):
    m = jnp.mean(x, axis=axis, keepdims=True)
    v = jnp.var(x, axis=axis, keepdims=True)
    return (x - m) / jnp.sqrt(v + eps)

def _scatter_add(tgt, idx, src, axis=0):
    return tgt.at[idx].add(src)

def _segment_sum(src, seg, n):
    return jax.ops.segment_sum(src, seg, n)
kernel_name = 'mk_adaln_d1_jaxref_r8_4ef512'

def setup_inputs(seed: int=0):
    np.random.seed(seed)
    _w = jnp.asarray

    def _L0_attn_setup():
        import jax, jax.numpy as jnp
        import numpy as np
        B, N, D_IN, D_OUT, HEADS = (4, 512, 128, 128, 16)
        D_HEAD = D_OUT // HEADS
        key = jax.random.key(seed)
        ks = jax.random.split(key, 5)
        x = jax.random.normal(ks[0], (B, N, D_IN), dtype=jnp.float32)
        s_in = 1.0 / np.sqrt(D_IN)
        s_out = 1.0 / np.sqrt(D_OUT)
        Wq = jax.random.normal(ks[1], (D_IN, D_OUT), dtype=jnp.float32) * s_in
        Wk = jax.random.normal(ks[2], (D_IN, D_OUT), dtype=jnp.float32) * s_in
        Wv = jax.random.normal(ks[3], (D_IN, D_OUT), dtype=jnp.float32) * s_in
        Wo = jax.random.normal(ks[4], (D_OUT, D_OUT), dtype=jnp.float32) * s_out
        bo = jnp.zeros((D_OUT,), dtype=jnp.float32)
        return {'x': x, 'Wq': Wq, 'Wk': Wk, 'Wv': Wv, 'Wo': Wo, 'bo': bo}
    _L0_attn_in = _L0_attn_setup()

    def _L0_ffn_setup():
        import jax, jax.numpy as jnp
        import numpy as np
        DIM, HEADS, FFN, E = (128, 16, 512, 8)
        B, S = (2, 128)
        EPS = 1e-05

        def _ln(x, g, b):
            mu = jnp.mean(x, axis=-1, keepdims=True)
            var = jnp.mean((x - mu) ** 2, axis=-1, keepdims=True)
            return (x - mu) * jax.lax.rsqrt(var + EPS) * g + b
        key = jax.random.key(seed)
        ks = jax.random.split(key, 20)
        sd = 0.02
        d, f = (DIM, FFN)
        return {'x': jax.random.normal(ks[0], (B, S, d), jnp.float32), 'ln1_g': jnp.ones((d,), jnp.float32), 'ln1_b': jnp.zeros((d,), jnp.float32), 'Wqkv': jax.random.normal(ks[1], (d, 3 * d), jnp.float32) * sd, 'bqkv': jnp.zeros((3 * d,), jnp.float32), 'Wo': jax.random.normal(ks[2], (d, d), jnp.float32) * sd, 'bo': jnp.zeros((d,), jnp.float32), 'ln2_g': jnp.ones((d,), jnp.float32), 'ln2_b': jnp.zeros((d,), jnp.float32), 'gate_w': jax.random.normal(ks[3], (d, E), jnp.float32) * sd, 'W1': jax.random.normal(ks[4], (E, d, f), jnp.float32) * sd, 'b1': jnp.zeros((E, f), jnp.float32), 'W2': jax.random.normal(ks[5], (E, f, d), jnp.float32) * sd, 'b2': jnp.zeros((E, d), jnp.float32), 'rW1': jax.random.normal(ks[6], (d, f), jnp.float32) * sd, 'rb1': jnp.zeros((f,), jnp.float32), 'rW2': jax.random.normal(ks[7], (f, d), jnp.float32) * sd, 'rb2': jnp.zeros((d,), jnp.float32), 'coef_w': jax.random.normal(ks[8], (d, 2), jnp.float32) * sd, 'coef_b': jnp.zeros((2,), jnp.float32)}
    _L0_ffn_in = _L0_ffn_setup()
    _L0_c = _w((lambda *s: np.random.randn(*s).astype(np.float32) * 0.05)(32, 128))
    _L0_wmod = _w((lambda *s: np.random.randn(*s).astype(np.float32) * 0.05)(128, 6 * 128) * 128 ** (-0.5))
    _d = {'L0_attn_x': _L0_attn_in['x'], 'L0_attn_Wq': _L0_attn_in['Wq'], 'L0_attn_Wk': _L0_attn_in['Wk'], 'L0_attn_Wv': _L0_attn_in['Wv'], 'L0_attn_Wo': _L0_attn_in['Wo'], 'L0_attn_bo': _L0_attn_in['bo'], 'L0_ffn_ln1_g': _L0_ffn_in['ln1_g'], 'L0_ffn_ln1_b': _L0_ffn_in['ln1_b'], 'L0_ffn_Wqkv': _L0_ffn_in['Wqkv'], 'L0_ffn_bqkv': _L0_ffn_in['bqkv'], 'L0_ffn_Wo': _L0_ffn_in['Wo'], 'L0_ffn_bo': _L0_ffn_in['bo'], 'L0_ffn_ln2_g': _L0_ffn_in['ln2_g'], 'L0_ffn_ln2_b': _L0_ffn_in['ln2_b'], 'L0_ffn_gate_w': _L0_ffn_in['gate_w'], 'L0_ffn_W1': _L0_ffn_in['W1'], 'L0_ffn_b1': _L0_ffn_in['b1'], 'L0_ffn_W2': _L0_ffn_in['W2'], 'L0_ffn_b2': _L0_ffn_in['b2'], 'L0_ffn_rW1': _L0_ffn_in['rW1'], 'L0_ffn_rb1': _L0_ffn_in['rb1'], 'L0_ffn_rW2': _L0_ffn_in['rW2'], 'L0_ffn_rb2': _L0_ffn_in['rb2'], 'L0_ffn_coef_w': _L0_ffn_in['coef_w'], 'L0_ffn_coef_b': _L0_ffn_in['coef_b'], 'L0_c': _L0_c, 'L0_wmod': _L0_wmod}
    _x0 = _d['L0_attn_x']
    _d['L0_attn_x'] = jax.random.normal(jax.random.fold_in(jax.random.key(seed), 1), (32, 256, 128), dtype=_x0.dtype)
    del _x0
    return _d

def reference(L0_attn_x, L0_attn_Wq, L0_attn_Wk, L0_attn_Wv, L0_attn_Wo, L0_attn_bo, L0_ffn_ln1_g, L0_ffn_ln1_b, L0_ffn_Wqkv, L0_ffn_bqkv, L0_ffn_Wo, L0_ffn_bo, L0_ffn_ln2_g, L0_ffn_ln2_b, L0_ffn_gate_w, L0_ffn_W1, L0_ffn_b1, L0_ffn_W2, L0_ffn_b2, L0_ffn_rW1, L0_ffn_rb1, L0_ffn_rW2, L0_ffn_rb2, L0_ffn_coef_w, L0_ffn_coef_b, L0_c, L0_wmod):

    def _L0_attn_ref(x, Wq, Wk, Wv, Wo, bo):
        import jax, jax.numpy as jnp
        import numpy as np
        B, N, D_IN, D_OUT, HEADS = (4, 512, 128, 128, 16)
        D_HEAD = D_OUT // HEADS
        q = jax.nn.softmax(jnp.einsum('bni,io->bno', x, Wq), axis=-1)
        k = jax.nn.softmax(jnp.einsum('bni,io->bno', x, Wk), axis=-2)
        v = jnp.einsum('bni,io->bno', x, Wv)
        scale = 1.0 / np.sqrt(D_HEAD).astype(np.float32)
        ctx = jnp.einsum('bnd,bne->bde', k, v) * scale
        y = jnp.einsum('bnd,bde->bne', q, ctx) / jnp.float32(D_OUT)
        return jnp.einsum('bnd,de->bne', y, Wo) + bo

    def _L0_ffn_ref(x, ln1_g, ln1_b, Wqkv, bqkv, Wo, bo, ln2_g, ln2_b, gate_w, W1, b1, W2, b2, rW1, rb1, rW2, rb2, coef_w, coef_b):
        import jax, jax.numpy as jnp
        import numpy as np
        DIM, HEADS, FFN, E = (128, 16, 512, 8)
        B, S = (2, 128)
        EPS = 1e-05

        def _ln(x, g, b):
            mu = jnp.mean(x, axis=-1, keepdims=True)
            var = jnp.mean((x - mu) ** 2, axis=-1, keepdims=True)
            return (x - mu) * jax.lax.rsqrt(var + EPS) * g + b
        b, s, d = x.shape
        h, dh = (HEADS, d // HEADS)
        xn = _ln(x, ln1_g, ln1_b)
        qkv = xn @ Wqkv + bqkv
        q, k, v = jnp.split(qkv, 3, axis=-1)
        q = q.reshape(b, s, h, dh)
        k = k.reshape(b, s, h, dh)
        v = v.reshape(b, s, h, dh)
        scores = jnp.einsum('bqhd,bkhd->bhqk', q, k) / jnp.sqrt(jnp.float32(dh))
        attn = jax.nn.softmax(scores, axis=-1)
        ctx = jnp.einsum('bhqk,bkhd->bqhd', attn, v).reshape(b, s, d)
        x = x + ctx @ Wo + bo
        xn2 = _ln(x, ln2_g, ln2_b)
        xt = xn2.reshape(b * s, d)
        probs = jax.nn.softmax(xt @ gate_w, axis=-1)
        gate_val = jnp.max(probs, axis=-1, keepdims=True)
        expert_idx = jnp.argmax(probs, axis=-1)
        oh = jax.nn.one_hot(expert_idx, E, dtype=xt.dtype)
        xe = jnp.einsum('te,td->etd', oh, xt)
        he = jax.nn.gelu(jnp.einsum('etd,edf->etf', xe, W1) + b1[:, None, :], approximate=False)
        ye = jnp.einsum('etf,efd->etd', he, W2) + b2[:, None, :]
        moe_out = jnp.einsum('te,etd->td', oh, ye) * gate_val
        rm = jax.nn.gelu(xt @ rW1 + rb1, approximate=False) @ rW2 + rb2
        coef = jax.nn.softmax(xt @ coef_w + coef_b, axis=-1)
        ff = moe_out * coef[:, 0:1] + rm * coef[:, 1:2]
        return x + ff.reshape(b, s, d)
    x = L0_attn_x
    mod = (_silu(L0_c) @ L0_wmod).reshape(L0_c.shape[0], 6, 1, -1)
    sa, ca, ga, sb, cb, gb = (mod[:, 0], mod[:, 1], mod[:, 2], mod[:, 3], mod[:, 4], mod[:, 5])
    ga = (2 * (ga >= 0) - 1) * jnp.maximum(jnp.abs(ga), 0.25)
    gb = (2 * (gb >= 0) - 1) * jnp.maximum(jnp.abs(gb), 0.25)
    h = _layernorm(x, axis=-1) * (1 + ca) + sa
    x = x + ga * _L0_attn_ref(h, L0_attn_Wq, L0_attn_Wk, L0_attn_Wv, L0_attn_Wo, L0_attn_bo)
    h = _layernorm(x, axis=-1) * (1 + cb) + sb
    x = x + gb * _L0_ffn_ref(h, L0_ffn_ln1_g, L0_ffn_ln1_b, L0_ffn_Wqkv, L0_ffn_bqkv, L0_ffn_Wo, L0_ffn_bo, L0_ffn_ln2_g, L0_ffn_ln2_b, L0_ffn_gate_w, L0_ffn_W1, L0_ffn_b1, L0_ffn_W2, L0_ffn_b2, L0_ffn_rW1, L0_ffn_rb1, L0_ffn_rW2, L0_ffn_rb2, L0_ffn_coef_w, L0_ffn_coef_b)
    return x

_drawn_inputs = setup_inputs


def setup_inputs(seed=0):
    import zlib

    import numpy as np

    out = dict(_drawn_inputs(seed))
    spreads = {'L0_attn_bo': (0.0, 0.324),
     'L0_ffn_ln1_g': (1.0, 0.6),
     'L0_ffn_ln1_b': (0.0, 0.8),
     'L0_ffn_bqkv': (0.0, 0.8),
     'L0_ffn_bo': (0.0, 0.332),
     'L0_ffn_ln2_g': (1.0, 0.6),
     'L0_ffn_ln2_b': (0.0, 0.8),
     'L0_ffn_b1': (0.0, 0.8),
     'L0_ffn_b2': (0.0, 0.8),
     'L0_ffn_rb1': (0.0, 0.8),
     'L0_ffn_rb2': (0.0, 0.706),
     'L0_ffn_coef_b': (0.0, 0.8)}
    factors = {'L0_attn_Wq': 8.0,
     'L0_attn_Wk': 8.0,
     'L0_attn_Wv': 8.0,
     'L0_attn_Wo': 8.0,
     'L0_ffn_Wqkv': 8.0,
     'L0_ffn_Wo': 8.0,
     'L0_ffn_gate_w': 8.0,
     'L0_ffn_W1': 8.0,
     'L0_ffn_W2': 8.0,
     'L0_ffn_rW1': 8.0,
     'L0_ffn_rW2': 7.719,
     'L0_ffn_coef_w': 8.0}
    for name, (base, spread) in spreads.items():
        noise = np.random.default_rng([zlib.crc32(name.encode()), seed]).standard_normal(out[name].shape)
        drawn = base * np.exp(spread * noise) if base else spread * noise
        out[name] = jnp.asarray(drawn.astype(out[name].dtype))
    for name, factor in factors.items():
        out[name] = (out[name] * factor).astype(out[name].dtype)
    return out
```

```python
from contextlib import ExitStack

import concourse.bass as bass
from concourse import mybir

ALU = mybir.AluOpType
ACT = mybir.ActivationFunctionType
AX = mybir.AxisListType
F32 = mybir.dt.float32
BF16 = mybir.dt.bfloat16
U32 = mybir.dt.uint32

P = 128
B, S, D = 32, 256, 128
TPB = S // P
TILES = B * TPB
HEADS, DH = 16, 8
FFN, E = 512, 8
FC = FFN // P
EPS = 1e-5
ATT_SCALE = float(DH) ** -0.5
LIN_SCALE = float(DH) ** -0.5 / D
PARTS = 3
QK_ROWS = PARTS * PARTS * DH
ALL_ROWS = QK_ROWS + PARTS
NBUF = 3
HALF = HEADS // 2
VW = DH + 1
VA_COLS = HEADS * VW + 32 - VW
MAX_TILES = TILES + E - 1
SLOTS = MAX_TILES * P
ROW = D + 2
NVEC = 6 + (E + 1) * FC
GT = 4
GB = GT // TPB
GROUPS = TILES // GT
WB1 = FFN + FC * P
WB2 = WB1 + FC
WCOLS = WB2 + D
NL = E + 2

LOAD, FRONT, SPREAD, MAX, EXP, BACK = range(6)
JOBS = [
    ("x_T", FRONT, 0), ("max_T_hi", EXP, 0), ("qv", FRONT, 1), ("ctx_rows0", BACK, 1), ("k", FRONT, 2),
    ("ctx_rows1", BACK, 2), ("ctx_T", BACK, 3), ("qk_T", FRONT, 4), ("lin_ctx", FRONT, 5),
    ("att_out", BACK, 5), ("lin_m", FRONT, 6), ("lin_out", FRONT, 7), ("max_T_lo", MAX, 8),
    ("moe_in_T", BACK, 9), ("logits", BACK, 10), ("h_T", FRONT, 14), ("qk", FRONT, 15), ("v", FRONT, 15),
]
JOB = {name: n for n, (name, _, _) in enumerate(JOBS)}
PIPE = B + BACK
MAIN_FROM = BACK + 1
MAIN_TO = MAIN_FROM + (B - MAIN_FROM) // NBUF * NBUF


def done_iterations(t, stage):
    return min(max(t - stage, 0), B) if isinstance(t, int) else t - stage


def active(t, stage):
    return 0 <= t - stage < B if isinstance(t, int) else True


def bank_uses(t, job):
    n = 0
    for k in range(job % 2, len(JOBS), 2):
        n = n + done_iterations(t, JOBS[k][1])
        if k < job and active(t, JOBS[k][1]):
            n = n + 1
    return n


def wait(eng, sem, value):
    if not isinstance(value, int) or value > 0:
        eng.wait_ge(sem, value)


def adaln_block(nc, x_d, c_d, wmod_d, wqkv_lin_d, wo_lin_d, bo_lin_d, vec_d, wqkv_d, bqk_d, bv_d, wo_d, bo_d,
                wlog_d, blog_d, w1_d, b1_d, w2_d, b2_d, out_d):
    with ExitStack() as ctx:
        def sb(name, shape, dt=F32):
            return ctx.enter_context(nc.sbuf_tensor(name, shape, dt))

        def sem(name):
            return ctx.enter_context(nc.semaphore(name))

        mod_dram = nc.dram_tensor("mod_rows", [B, 4, D], F32, kind="Internal").ap()
        split_dram = nc.dram_tensor("split_qk", [2, PARTS, P, S], BF16, kind="Internal").ap()
        sorted_dram = nc.dram_tensor("sorted_tokens", [SLOTS, ROW], F32, kind="Internal").ap()
        moe_dram = nc.dram_tensor("moe_out", [B * S + SLOTS, D], F32, kind="Internal").ap()

        res = sb("res", [P, TILES, D])
        keep = sb("keep", [P, TILES, D])
        moe_in_T = sb("moe_in_T", [P, B * S])
        big = sb("big", [P, NBUF * HEADS * S])
        w_shared = sb("w_shared", [P, WCOLS])
        logit = sb("logit", [P, TILES, NL])
        ident = sb("ident", [P, P])
        vecs_T = sb("vecs_T", [P, 48])
        BIGH = NBUF * HEADS * S // 2
        q_all = big[:, 0:BIGH].bitcast(BF16).rearrange("p (n h s) -> p n h s", n=NBUF, h=HEADS)
        k_all = big[:, BIGH:2 * BIGH].bitcast(BF16).rearrange("p (n h s) -> p n h s", n=NBUF, h=HEADS)
        w_exp = big[:, 0:E * WCOLS].rearrange("p (e n) -> p e n", e=E)
        slots0 = big[:, 0:MAX_TILES * ROW].rearrange("p (t n) -> p t n", n=ROW)
        staged = big[:, E * WCOLS:(E + 2) * WCOLS].rearrange("p (n w) -> p n w", n=2)

        w_qv = sb("w_qv", [P, 2 * D])
        w_k = sb("w_k", [P, D])
        w_lo = sb("w_lo", [P, D])
        w_qkv = sb("w_qkv", [P, 3 * D])
        w_ao = sb("w_ao", [P, D])
        w_log = sb("w_log", [P, NL])
        b_lo = sb("b_lo", [P, D])
        b_v = sb("b_v", [P, D])
        b_ao = sb("b_ao", [P, D])
        b_log = sb("b_log", [P, NL])
        half_neg = sb("half_neg", [P, TPB])
        modT = sb("modT", [P, 2, B])
        rows_in = sb("rows_in", [NVEC, P])
        tile_first = sb("tile_first", [P, TILES])
        tile_no = sb("tile_no", [P, MAX_TILES])
        order = sb("order", [P, E])
        token_meta = sb("token_meta", [P, TILES, 2])

        st_a, st_b, st_c, st_d = (sb(f"st_{x}", [P, TPB, 6]) for x in "abcd")
        mv_a, mv_b, mv_c, mv_d = (sb(f"mv_{x}", [P, TPB, 2]) for x in "abcd")
        rs_a, rs_b, rs_c, rs_d = (sb(f"rs_{x}", [P, TPB]) for x in "abcd")
        ARENA = 9920
        arena = sb("arena", [P, ARENA])
        used = [0]

        def take(shape, dt=F32):
            words = 1
            for n in shape:
                words *= n
            if dt == BF16:
                words //= 2
            piece = arena[:, used[0]:used[0] + words]
            used[0] += (words + 7) // 8 * 8

            if dt != F32:
                piece = piece.bitcast(dt)
            names = "abcd"[:len(shape)]
            return piece.rearrange(f"p ({' '.join(names)}) -> p {' '.join(names)}",
                                   **dict(zip(names[1:], shape[1:]))) if len(shape) > 1 else piece

        xn = take([TPB, D])
        hT = take([S])
        q_neg = take([TPB])
        q_sum = take([TPB])
        q_rec = take([TPB])
        q_exp = take([TPB, D])
        v_lin = take([TPB, D])
        k_neg = take([1])
        k_sum = take([1])
        k_rec = take([1])
        k_exp = take([S])
        qk_T = take([2, S])
        ctx_lin = take([D])
        m_lin = take([D])
        y_lin = take([TPB, D])
        h_norm = take([TPB, D])
        xc = take([TPB, D])
        xnT = take([S])
        qkf = take([2, S])
        v_tmp = take([TPB, D])
        parts = take([2, PARTS, S], BF16)
        va = take([NBUF, TPB, VA_COLS])
        neg_max = take([2, TPB, HALF])
        max_f = sb("max_f", [HALF, 2, S])
        max_parts = sb("max_parts", [HALF, 2, PARTS, S], BF16)
        probs = take([2, TPB * S])
        oT = take([HEADS // 4, S])
        o_rec = take([TPB, HEADS])
        o_rows = take([TPB, D])
        o_T = take([S])
        h2b = take([TPB, D])
        x3 = take([TPB, D])
        xm = take([TPB, D])
        xmT = take([S])
        mod3 = take([3, D])
        mod_gb = take([1, D])

        used[0] = 0
        upper = take([P])
        ones = take([P])
        onehot = take([TILES * E])
        hid = take([2, FC, GT * P])
        hid_flat = hid[:].rearrange("p n c s -> p (n c s)")

        def route_buf(n, cols):
            return hid_flat[:, n * TILES * E:n * TILES * E + cols]

        lmax = take([2, TILES])
        shifted = take([TILES, NL])
        w_moe = take([TILES])
        w_rm = take([TILES])
        slot_u = take([TILES], U32)
        expert_u = take([MAX_TILES], U32)
        small = take([6, E])
        y_shared = take([GT, D])
        gb2 = take([GB, D])
        out_rows = take([4, ROW])
        out_slots = take([4], U32)
        rows_buf = take([2, ROW])
        tile_T = take([2, P])
        y_moe = take([2, D])
        y_out = take([2, D])
        meta = take([2, 2])
        meta_slot = take([2], U32)
        fin_moe = hid_flat[:, 0:2 * GT * D].rearrange("p (n m d) -> p n m d", n=2, m=GT)
        fin_gb = hid_flat[:, 2 * GT * D:2 * GT * D + 2 * GB * D].rearrange("p (n m d) -> p n m d", n=2, m=GB)

        bank = [ctx.enter_context(nc.psum_tensor(f"bank{n}", [P, 512], F32)) for n in range(8)]
        work, max_bank, exp_bank, o_bank = bank[0:2], bank[2:4], bank[4:6], bank[6:8]

        (c_loaded, rows_loaded, weights_loaded, mods_ready, mods_stored, ident_ready, consts_ready, half_ready,
         silu_step, silu_exp, setup_full, setup_taken, mod_step, slots_cleared, slots_stored, ones_ready) = map(sem, (
             "c_loaded rows_loaded weights_loaded mods_ready mods_stored ident_ready consts_ready half_ready "
             "silu_step silu_exp setup_full setup_taken mod_step slots_cleared slots_stored ones_ready").split())
        (x_loaded, mod3_loaded, gb_loaded, max_full, max_done, exp_full, exp_done, pv_done, q_max_ready, q_exp_done,
         k_max_ready, recips, y_scaled, x1_ready, h_scaled, h2_ready, qk_split, split_stored, qk_spread, va_ready,
         oT_ready, o_rec_ready, h2b_ready, x3_scaled, res_ready, kept) = map(sem, (
             "x_loaded mod3_loaded gb_loaded max_full max_done exp_full exp_done pv_done q_max_ready q_exp_done "
             "k_max_ready recips y_scaled x1_ready h_scaled h2_ready qk_split split_stored qk_spread va_ready "
             "oT_ready o_rec_ready h2b_ready x3_scaled res_ready kept").split())
        stats_a, stats_b, stats_c, stats_d = (sem(f"stats_{x}") for x in "abcd")
        mean_a, mean_b, mean_c, mean_d = (sem(f"mean_{x}") for x in "abcd")
        rstd_a, rstd_b, rstd_c, rstd_d = (sem(f"rstd_{x}") for x in "abcd")
        norm_a, norm_b, norm_c, norm_d = (sem(f"norm_{x}") for x in "abcd")
        work_full = [sem(f"work_full{n}") for n in range(2)]
        work_free = [sem(f"work_free{n}") for n in range(2)]
        max_split = [sem(f"max_split{n}") for n in range(2)]
        max_spread = [sem(f"max_spread{n}") for n in range(2)]
        (route_step, route_exp, ones_again, counts_full, route_ready, experts_loaded, gb2_loaded, up_full, gelu_done,
         down_full, down_taken, shared_step, shared_added, scatter_staged, tile_T_full, tile_T_ready, weight_step,
         stage_ready, moe_up_full, moe_gelu_done, moe_y_full, moe_y_taken, pool_step, fin_step) = map(sem, (
             "route_step route_exp ones_again counts_full route_ready experts_loaded gb2_loaded up_full gelu_done "
             "down_full down_taken shared_step shared_added scatter_staged tile_T_full tile_T_ready weight_step "
             "stage_ready moe_up_full moe_gelu_done moe_y_full moe_y_taken pool_step fin_step").split())
        sorted_sem = [sem(f"sorted{n}") for n in range(4)]
        rows_in_loaded = [sem(f"rows_in_loaded{n}") for n in range(2)]
        meta_taken = [sem(f"meta_taken{n}") for n in range(2)]
        moe_scattered = [sem(f"moe_scattered{n}") for n in range(2)]
        fin_loaded = [sem(f"fin_loaded{n}") for n in range(2)]
        fin_ready = [sem(f"fin_ready{n}") for n in range(2)]
        fin_stored = [sem(f"fin_stored{n}") for n in range(2)]

        def mod_rows(b, first, n):
            return mod_dram[bass.ds(b, 1), first:first + n, :].to_broadcast([P, n, D])

        def batch(buf, b):
            return buf[:, bass.ds(b * TPB, TPB), :]

        def tile(buf, b, n):
            return buf[:, bass.ds(b * TPB + n, 1), :]

        def over(row, n):
            return row.unsqueeze(1).to_broadcast([P, n, D])

        def wait_apart(eng, sem, value):
            wait(eng, sem, value)
            if not isinstance(value, int):
                eng.nop(nofuse=True)

        def full(eng, t, name):
            job = JOB[name]
            wait(eng, work_full[job % 2], bank_uses(t, job) + 1)

        def taken(eng, t, name, wait=wait):
            job = JOB[name]
            wait(eng, work_free[job % 2], bank_uses(t, job) + 1)

        def drive(eng, run):
            for t in range(MAIN_FROM):
                run(t, t % NBUF)
            with eng.Fori(MAIN_FROM, MAIN_TO, NBUF) as t0:
                for r in range(NBUF):
                    run(t0 + r, (MAIN_FROM + r) % NBUF)
            for t in range(MAIN_TO, PIPE):
                run(t, t % NBUF)

        def drive_tiles(eng, run):
            for n in range(2):
                run(0, n)
            with eng.Fori(1, MAX_TILES // 2) as k:
                for n in range(2):
                    run(k, n)
            run(MAX_TILES // 2, 0)

        def drive_groups(eng, run):
            for n in range(2):
                run(0, n)
            with eng.Fori(1, GROUPS // 2) as k:
                for n in range(2):
                    run(k, n)

        def gb_rows(g):
            return mod_dram[bass.ds(g * GB, GB), 3, :].unsqueeze(0).to_broadcast([P, GB, D])

        def later(k):
            return not isinstance(k, int) or k > 0

        LN1G, LN1B, LN2G, LN2B, BQ, BK, B1 = range(7)

        def vec(n):
            return vecs_T[:, n:n + 1]

        c_in, c_exp, c_silu = xc[0:B, 0, :], xc[0:B, 1, :], h_norm[0:B, 0, :]
        c_T = h_norm[:, 1, 0:B]
        wmod = keep[:, 0:6, :].rearrange("p a b -> p (a b)")
        mods = keep[0:B, 6:12, :]
        gsign, gabs = keep[0:B, 12, :], keep[0:B, 13, :]

        WEIGHTS = [
            (w_qv[:, 0:D], wqkv_lin_d[0]), (w_qv[:, D:2 * D], wqkv_lin_d[2]), (w_k[:], wqkv_lin_d[1]),
            (w_lo[:], wo_lin_d), (w_qkv[:], wqkv_d), (w_ao[:], wo_d), (w_log[:], wlog_d),
            (b_lo[:], bo_lin_d.unsqueeze(0).to_broadcast([P, D])),
            (b_v[:], bv_d.unsqueeze(0).to_broadcast([P, D])),
            (b_ao[:], bo_d.unsqueeze(0).to_broadcast([P, D])),
            (b_log[:], blog_d.unsqueeze(0).to_broadcast([P, NL])),
            (w_shared[:, 0:FFN], w1_d[E]),
            (w_shared[:, FFN:WB1].rearrange("p (c n) -> p c n", c=FC), w2_d[E].rearrange("(c p) n -> p c n", p=P)),
            (w_shared[:, WB2:WCOLS], b2_d[E:E + 1, :].to_broadcast([P, D])),
        ]

        block = ctx.enter_context(nc.Block())

        @block.sync
        def _(sp):
            sp.dma_start(c_in, c_d).then_inc(c_loaded, 16)
            sp.dma_start(wmod, wmod_d).then_inc(rows_loaded, 16)
            sp.dma_start(rows_in[0:4, :], vec_d).then_inc(rows_loaded, 16)
            sp.dma_start(rows_in[4:6, :], bqk_d).then_inc(rows_loaded, 16)
            sp.dma_start(rows_in[6:NVEC, :], b1_d).then_inc(rows_loaded, 16)
            for dst, src in WEIGHTS:
                sp.dma_start(dst, src).then_inc(weights_loaded, 16)
            sp.wait_ge(mods_ready, 3)
            for n, row in enumerate((2, 4, 3, 5)):
                sp.dma_start(mod_dram[:, n, :], mods[:, row, :]).then_inc(mods_stored, 16)
            sp.wait_ge(mods_stored, 64)

            def spread_max(b, buf, half):
                wait_apart(sp, max_split[half], 4 * b + 4)
                for i in range(PARTS):
                    sp.dma_start(q_all[QK_ROWS + i:QK_ROWS + i + 1, buf, half * HALF:(half + 1) * HALF, :],
                                 max_parts[:, half, i, :]).then_inc(max_spread[half], 16)

            def iteration(t, r):
                if active(t, LOAD):
                    wait_apart(sp, x_loaded, 16 * (t - LOAD))
                    sp.dma_start(batch(res, t), x_d[bass.ds(t, 1), :, :].rearrange("a (n p) d -> p (a n) d", p=P)
                                 ).then_inc(x_loaded, 16)
                if active(t, FRONT):
                    b = t - FRONT
                    wait_apart(sp, h2_ready, b)
                    wait_apart(sp, mod3_loaded, 16 * b)
                    sp.dma_start(mod3[:], mod_rows(b, 0, 3)).then_inc(mod3_loaded, 16)
                if active(t, BACK):
                    b = t - BACK
                    wait_apart(sp, x3_scaled, b)
                    wait_apart(sp, gb_loaded, 16 * b)
                    sp.dma_start(mod_gb[:], mod_rows(b, 3, 1)).then_inc(gb_loaded, 16)
                if active(t, EXP):
                    spread_max(t - EXP, (r - EXP) % NBUF, 1)
                if active(t, SPREAD):
                    b, buf = t - SPREAD, (r - SPREAD) % NBUF
                    wait_apart(sp, qk_split, 4 * b + 4)
                    wait_apart(sp, qk_spread, 64 * b)
                    for n in range(2):
                        sp.dma_start(split_dram[n].rearrange("i p s -> p i s"), parts[:, n]).then_inc(split_stored, 16)
                    wait_apart(sp, split_stored, 32 * b + 32)
                    if isinstance(b, int) and b < NBUF:
                        sp.wait_ge(ones_ready, 1)
                    else:
                        wait_apart(sp, exp_full, HEADS * (b - NBUF + 1))
                    for i in range(PARTS):
                        sp.dma_start(q_all[i * PARTS * DH:(i + 1) * PARTS * DH, buf].rearrange("p h s -> p (h s)"),
                                     split_dram[0, i].rearrange("(d h) s -> d (h s)", d=DH).unsqueeze(0)
                                     .to_broadcast([PARTS, DH, HEADS * S])).then_inc(qk_spread, 16)
                    sp.dma_start(k_all[0:QK_ROWS, buf].rearrange("p h s -> p (h s)"),
                                 split_dram[1].rearrange("i (d h) s -> (i d) (h s)", d=DH).unsqueeze(0)
                                 .to_broadcast([PARTS, PARTS * DH, HEADS * S])).then_inc(qk_spread, 16)
                if active(t, MAX):
                    spread_max(t - MAX, (r - MAX) % NBUF, 0)

            drive(sp, iteration)

            sp.wait_ge(exp_full, B * HEADS)
            for e in range(E):
                sp.dma_start(w_exp[:, e, 0:FFN], w1_d[e]).then_inc(experts_loaded, 16)
                sp.dma_start(w_exp[:, e, FFN:WB1].rearrange("p (c n) -> p c n", c=FC),
                             w2_d[e].rearrange("(c p) n -> p c n", p=P)).then_inc(experts_loaded, 16)
                sp.dma_start(w_exp[:, e, WB2:WCOLS], b2_d[e:e + 1, :].to_broadcast([P, D])
                             ).then_inc(experts_loaded, 16)

            def load_gb(g):
                if later(g):
                    wait_apart(sp, shared_added, g)
                sp.dma_start(gb2[:], gb_rows(g)).then_inc(gb2_loaded, 16)
                wait_apart(sp, gb2_loaded, 16 * g + 16)

            sp.wait_ge(route_ready, 1)
            load_gb(0)
            with sp.Fori(1, GROUPS) as g:
                load_gb(g)

            for n in range(4):
                sp.wait_ge(sorted_sem[n], 16 * GROUPS)

            def moe_tile(k, n):
                if later(k):
                    wait_apart(sp, meta_taken[n], k)
                    wait_apart(sp, tile_T_full, 2 * k + n - 1)
                    wait_apart(sp, rows_in_loaded[n], 16 * k)
                sp.dma_start(rows_buf[:, n, :], sorted_dram[bass.ds((2 * k + n) * P, P), :]
                             ).then_inc(rows_in_loaded[n], 16)

            drive_tiles(sp, moe_tile)

            for n in range(2):
                wait_apart(sp, moe_scattered[n], 16 * ((MAX_TILES + 1 - n) // 2))

            def final(k, n):
                g = 2 * k + n
                if later(k):
                    wait_apart(sp, fin_loaded[n], 32 * k)
                    wait_apart(sp, fin_stored[n], 16 * k)
                sp.dma_start(fin_moe[:, n], moe_dram[bass.ds(g * GT * P, GT * P), :]
                             .rearrange("(n p) d -> p n d", p=P)).then_inc(fin_loaded[n], 16)
                sp.dma_start(fin_gb[:, n], gb_rows(g)).then_inc(fin_loaded[n], 16)

            drive_groups(sp, final)
            for n in range(2):
                wait_apart(sp, fin_stored[n], 16 * (GROUPS // 2))

        @block.tensor
        def _(pe):
            pe.wait_ge(silu_step, 3)
            pe.wait_ge(ident_ready, 2)
            pe.transpose(bank[0][:, 0:B], c_silu, ident[0:B, 0:B]).then_inc(setup_full, 1)
            pe.wait_ge(rows_loaded, 64)
            pe.transpose(bank[1][:, 0:NVEC], rows_in[0:NVEC, :], ident[0:NVEC, 0:NVEC]).then_inc(setup_full, 1)
            pe.wait_ge(setup_taken, 1)
            for n in range(2):
                pe.matmul(bank[2 + n][0:B, 0:3 * D], c_T, wmod[:, 3 * D * n:3 * D * (n + 1)], start=True, stop=True
                          ).then_inc(setup_full, 1)
            pe.wait_ge(mod_step, 3)
            for n in range(2):
                pe.transpose(bank[0][:, n * B:(n + 1) * B], mods[:, n, :], ident[0:B, 0:B]).then_inc(setup_full, 1)
            pe.wait_ge(setup_taken, 3)
            pe.wait_ge(weights_loaded, 16 * len(WEIGHTS))

            def open_bank(t, name):
                k = JOB[name]
                wait(pe, work_free[k % 2], bank_uses(t, k))
                return work[k % 2]

            def close_bank(name, last):
                last.then_inc(work_full[JOB[name] % 2], 1)

            def transpose_tiles(t, name, tiles):
                w = open_bank(t, name)
                for n, src in enumerate(tiles):
                    last = pe.transpose(w[0:src.shape[1], n * P:(n + 1) * P], src, ident[:])
                close_bank(name, last)

            def scores_t(b, buf, h):
                if h == 0:
                    pe.wait_ge(max_spread[0], 48 * b + 48)
                if h == HALF:
                    pe.wait_ge(max_spread[1], 48 * b + 48)
                wait(pe, exp_done, b * HEADS + h - 1)
                for k in range(TPB):
                    last = pe.matmul(exp_bank[h % 2][:, k * S:(k + 1) * S], k_all[0:ALL_ROWS, buf, h, k * P:(k + 1) * P],
                                     q_all[0:ALL_ROWS, buf, h, :], start=True, stop=True)
                last.then_inc(exp_full, 1)

            def scores(b, buf, h):
                if h == 0:
                    pe.wait_ge(qk_spread, 64 * b + 64)
                wait(pe, max_done, b * HEADS + h - 1)
                for q in range(TPB):
                    last = pe.matmul(max_bank[h % 2][:, q * S:(q + 1) * S], q_all[0:QK_ROWS, buf, h, q * P:(q + 1) * P],
                                     k_all[0:QK_ROWS, buf, h, :], start=True, stop=True)
                last.then_inc(max_full, 1)

            def probs_v(b, buf, h):
                if h == 0:
                    pe.wait_ge(va_ready, b + 1)
                if h % HALF == 0:
                    wait(pe, oT_ready, 2 * b - 1 + h // HALF)
                pe.wait_ge(exp_done, b * HEADS + h + 1)
                j, g = h % 4, h // 4 % 2
                for k in range(TPB):
                    last = pe.matmul(o_bank[h // HALF][32 * j:32 * j + 32, g * S:(g + 1) * S],
                                     va[:, buf, k, h * VW:h * VW + 32], probs[:, h % 2, k * S:(k + 1) * S],
                                     start=(k == 0), stop=(k == TPB - 1))
                last.then_inc(pv_done, 1)

            def front(t, slot):
                b = t - FRONT
                if slot == 0:
                    pe.wait_ge(norm_a, 2 * b + 2)
                    transpose_tiles(t, "x_T", [xn[:, n, :] for n in range(TPB)])
                if slot == 1:
                    w = open_bank(t, "qv")
                    taken(pe, t, "x_T")
                    for n in range(TPB):
                        last = pe.matmul(w[:, 2 * D * n:2 * D * (n + 1)], hT[:, n * P:(n + 1) * P], w_qv[:],
                                         start=True, stop=True)
                    close_bank("qv", last)
                if slot == 2:
                    w = open_bank(t, "k")
                    close_bank("k", pe.matmul(w[:, 0:S], w_k[:], hT[:], start=True, stop=True))
                if slot == 4:
                    w = open_bank(t, "qk_T")
                    taken(pe, t, "qv")
                    taken(pe, t, "k")
                    for n in range(TPB):
                        pe.transpose(w[:, n * P:(n + 1) * P], q_exp[:, n, :], ident[:])
                    for n in range(TPB):
                        last = pe.transpose(w[:, S + n * P:S + (n + 1) * P], k_exp[:, n * P:(n + 1) * P], ident[:])
                    close_bank("qk_T", last)
                if slot == 5:
                    w = open_bank(t, "lin_ctx")
                    taken(pe, t, "qk_T")
                    for n in range(TPB):
                        last = pe.matmul(w[:, 0:D], v_lin[:, n, :], qk_T[:, 1, n * P:(n + 1) * P],
                                         start=(n == 0), stop=(n == TPB - 1))
                    close_bank("lin_ctx", last)
                if slot == 6:
                    w = open_bank(t, "lin_m")
                    taken(pe, t, "lin_ctx")
                    close_bank("lin_m", pe.matmul(w[:, 0:D], ctx_lin[:], w_lo[:], start=True, stop=True))
                if slot == 7:
                    w = open_bank(t, "lin_out")
                    taken(pe, t, "lin_m")
                    for n in range(TPB):
                        last = pe.matmul(w[:, n * D:(n + 1) * D], qk_T[:, 0, n * P:(n + 1) * P], m_lin[:],
                                         start=True, stop=True)
                    close_bank("lin_out", last)
                if slot == 14:
                    pe.wait_ge(norm_c, 2 * b + 2)
                    transpose_tiles(t, "h_T", [xc[:, n, :] for n in range(TPB)])
                if slot == 15:
                    w = open_bank(t, "qk")
                    taken(pe, t, "h_T")
                    for n in range(2):
                        last = pe.matmul(w[:, n * S:(n + 1) * S], w_qkv[:, n * D:(n + 1) * D], xnT[:],
                                         start=True, stop=True)
                    close_bank("qk", last)
                    w = open_bank(t, "v")
                    for n in range(TPB):
                        last = pe.matmul(w[:, n * D:(n + 1) * D], xnT[:, n * P:(n + 1) * P], w_qkv[:, 2 * D:3 * D],
                                         start=True, stop=True)
                    close_bank("v", last)

            def back(t, slot):
                b = t - BACK
                if slot in (1, 2):
                    pe.wait_ge(oT_ready, 2 * b + 2)
                    n = slot - 1
                    transpose_tiles(t, f"ctx_rows{n}", [oT[:, g, n * P:(n + 1) * P] for g in range(HEADS // 4)])
                if slot == 3:
                    taken(pe, t, "ctx_rows0")
                    taken(pe, t, "ctx_rows1")
                    transpose_tiles(t, "ctx_T", [o_rows[:, n, :] for n in range(TPB)])
                if slot == 5:
                    w = open_bank(t, "att_out")
                    taken(pe, t, "ctx_T")
                    for n in range(TPB):
                        last = pe.matmul(w[:, n * D:(n + 1) * D], o_T[:, n * P:(n + 1) * P], w_ao[:],
                                         start=True, stop=True)
                    close_bank("att_out", last)
                if slot == 9:
                    pe.wait_ge(norm_d, 2 * b + 2)
                    transpose_tiles(t, "moe_in_T", [xm[:, n, :] for n in range(TPB)])
                if slot == 10:
                    w = open_bank(t, "logits")
                    taken(pe, t, "moe_in_T")
                    for n in range(TPB):
                        last = pe.matmul(w[:, n * NL:(n + 1) * NL], xmT[:, n * P:(n + 1) * P], w_log[:],
                                         start=True, stop=True)
                    close_bank("logits", last)

            def iteration(t, r):
                for slot in range(HEADS):
                    if slot == 0 and active(t, BACK):
                        probs_v(t - BACK, (r - BACK) % NBUF, HEADS - 1)
                    if active(t, EXP):
                        scores_t(t - EXP, (r - EXP) % NBUF, slot)
                    if active(t, MAX):
                        scores(t - MAX, (r - MAX) % NBUF, slot)
                    if active(t, FRONT):
                        front(t, slot)
                    if slot == 0 and active(t, EXP):
                        pe.wait_ge(max_done, (t - EXP) * HEADS + HEADS)
                        transpose_tiles(t, "max_T_hi", [neg_max[:, 1, q, :] for q in range(TPB)])
                    if slot == HALF and active(t, MAX):
                        pe.wait_ge(max_done, (t - MAX) * HEADS + HALF)
                        transpose_tiles(t, "max_T_lo", [neg_max[:, 0, q, :] for q in range(TPB)])
                    if active(t, BACK):
                        back(t, slot)
                    if slot > 0 and active(t, EXP):
                        probs_v(t - EXP, (r - EXP) % NBUF, slot - 1)

            drive(pe, iteration)

            pe.wait_ge(route_step, 8)
            pe.wait_ge(consts_ready, 5)
            pe.matmul(bank[2][:, 0:TILES * E], upper[:], onehot[:], start=True, stop=True
                      ).then_inc(counts_full, 1)
            pe.matmul(bank[3][:, 0:TILES * E], ones[:], onehot[:], start=True, stop=True
                      ).then_inc(counts_full, 1)

            pe.wait_ge(kept, 2 * B)

            def shared_up(k, n, cs):
                g = 2 * k + n
                for c in cs:
                    if later(g) or c >= 2:
                        pe.wait_ge(gelu_done, g * FC + c - 1)
                    pe.matmul(bank[4 + c % 2][:], w_shared[:, c * P:(c + 1) * P], moe_in_T[:, bass.ds(g * GT * P, GT * P)],
                              start=True, stop=True).then_inc(up_full, 1)

            def shared_down(k, n):
                g = 2 * k + n
                pe.wait_ge(gelu_done, g * FC + FC)
                if later(k):
                    pe.wait_ge(down_taken, g - 1)
                for m in range(GT):
                    for c in range(FC):
                        last = pe.matmul(bank[6 + n][:, m * D:(m + 1) * D], hid[:, n, c, m * P:(m + 1) * P],
                                         w_shared[:, FFN + c * P:FFN + (c + 1) * P], start=(c == 0), stop=(c == FC - 1))
                last.then_inc(down_full, 1)

            def shared_step_pair(k, n, k_before, n_before):
                shared_up(k, n, range(2))
                shared_down(k_before, n_before)
                shared_up(k, n, range(2, FC))

            pe.wait_ge(route_ready, 1)
            shared_up(0, 0, range(FC))
            shared_step_pair(0, 1, 0, 0)
            shared_step_pair(1, 0, 0, 1)
            with pe.Fori(1, GROUPS // 2 - 1) as k:
                shared_step_pair(k, 1, k, 0)
                shared_step_pair(k + 1, 0, k, 1)
            shared_step_pair(GROUPS // 2 - 1, 1, GROUPS // 2 - 1, 0)
            shared_down(GROUPS // 2 - 1, 1)
            pe.wait_ge(down_taken, GROUPS)
            for n in range(2):
                pe.wait_ge(work_free[n], bank_uses(PIPE, n))

            def moe_transpose(k, n):
                pe.wait_ge(rows_in_loaded[n], 16 * k + 16)
                if later(k):
                    pe.wait_ge(tile_T_ready, 2 * k + n - 1)
                pe.transpose(bank[n][:, 0:P], rows_buf[:, n, 0:D], ident[:]).then_inc(tile_T_full, 1)

            def moe_up(k, n):
                j = 2 * k + n
                pe.wait_ge(tile_T_ready, j + 1)
                pe.wait_ge(stage_ready, j + 1)
                if later(k):
                    pe.wait_ge(moe_gelu_done, (j - 1) * FC)
                for c in range(FC):
                    last = pe.matmul(bank[4 + n][:, c * P:(c + 1) * P], staged[:, n, c * P:(c + 1) * P], tile_T[:, n, :],
                                     start=True, stop=True)
                last.then_inc(moe_up_full, 1)

            def moe_down(k, n):
                j = 2 * k + n
                pe.wait_ge(moe_gelu_done, j * FC + FC)
                if later(k):
                    pe.wait_ge(moe_y_taken, j - 1)
                for c in range(FC):
                    last = pe.matmul(bank[6 + n][:, 0:D], hid[:, n, c, 0:P], staged[:, n, FFN + c * P:FFN + (c + 1) * P],
                                     start=(c == 0), stop=(c == FC - 1))
                last.then_inc(moe_y_full, 1)

            def moe_steps(k):
                moe_transpose(k + 1, 0)
                moe_up(k, 1)
                moe_down(k, 0)
                moe_transpose(k + 1, 1)
                moe_up(k + 1, 0)
                moe_down(k, 1)

            moe_transpose(0, 0)
            moe_transpose(0, 1)
            moe_up(0, 0)
            moe_steps(0)
            last_k = MAX_TILES // 2 - 1
            with pe.Fori(1, last_k) as k:
                moe_steps(k)
            moe_transpose(last_k + 1, 0)
            moe_up(last_k, 1)
            moe_down(last_k, 0)
            moe_up(last_k + 1, 0)
            moe_down(last_k, 1)
            moe_down(last_k + 1, 0)

        @block.scalar
        def _(act):
            act.wait_ge(c_loaded, 16)
            act.activation(c_exp, c_in, ACT.Exp, scale=-1.0).then_inc(silu_exp, 1)

            def iteration(t, r):
                for slot in range(HEADS):
                    if active(t, BACK) and slot == 0:
                        act.wait_ge(pv_done, (t - BACK) * HEADS + HEADS)
                        act.activation(oT[:, 2:4, :].rearrange("p g s -> p (g s)"), o_bank[1][:], ACT.Copy
                                       ).then_inc(oT_ready, 1)
                    if active(t, EXP):
                        b = t - EXP
                        act.wait_ge(exp_full, b * HEADS + slot + 1)
                        wait(act, pv_done, b * HEADS + slot - 1)
                        act.activation(probs[:, slot % 2, :], exp_bank[slot % 2][:], ACT.Exp, scale=ATT_SCALE
                                       ).then_inc(exp_done, 1)
                    if active(t, EXP) and slot == HALF + 1:
                        act.wait_ge(pv_done, (t - EXP) * HEADS + HALF)
                        if active(t, BACK):
                            full(act, t, "ctx_rows1")
                        act.activation(oT[:, 0:2, :].rearrange("p g s -> p (g s)"), o_bank[0][:], ACT.Copy
                                       ).then_inc(oT_ready, 1)
                    if active(t, FRONT):
                        front(t, slot)
                    if active(t, EXP) and slot == 0:
                        take_max(t, "max_T_hi", t - EXP, 1)
                    if active(t, MAX) and slot == HALF:
                        take_max(t, "max_T_lo", t - MAX, 0)
                    if active(t, BACK):
                        back(t, slot)

            def free(ins, name):
                ins.then_inc(work_free[JOB[name] % 2], 1)

            def bank_of(name):
                return work[JOB[name] % 2]

            def take_max(t, name, b, half):
                full(act, t, name)
                wait(act, max_split[half], 4 * b)
                free(act.activation(max_f[:, half, :], bank_of(name)[0:HALF, 0:S], ACT.Copy), name)

            def front(t, slot):
                b = t - FRONT
                if slot == 0:
                    if isinstance(t, int) and b == 0:
                        act.wait_ge(setup_taken, 3)
                    full(act, t, "x_T")
                    free(act.activation(hT[:], bank_of("x_T")[:, 0:S], ACT.Identity, bias=modT[:, 0, bass.ds(b, 1)],
                                        scale=modT[:, 1, bass.ds(b, 1)]), "x_T")
                if slot == 1:
                    act.wait_ge(q_max_ready, b + 1)
                    w = bank_of("qv")[:].rearrange("p (n two d) -> p n two d", n=TPB, two=2)
                    for n in range(TPB):
                        act.activation(q_exp[:, n, :], w[:, n, 0, :], ACT.Exp, bias=q_neg[:, n:n + 1],
                                       accum_out=q_sum[:, n:n + 1]).then_inc(q_exp_done, 1)
                    free(act.activation(v_lin[:], w[:, :, 1, :], ACT.Copy), "qv")
                if slot == 2:
                    act.wait_ge(k_max_ready, b + 1)
                    free(act.activation(k_exp[:], bank_of("k")[:, 0:S], ACT.Exp, bias=k_neg[:], accum_out=k_sum[:]), "k")
                if slot == 4:
                    full(act, t, "qk_T")
                    free(act.activation(qk_T[:].rearrange("p n s -> p (n s)"), bank_of("qk_T")[:], ACT.Copy), "qk_T")
                if slot == 5:
                    full(act, t, "lin_ctx")
                    free(act.activation(ctx_lin[:], bank_of("lin_ctx")[:, 0:D], ACT.Copy), "lin_ctx")
                if slot == 14:
                    full(act, t, "h_T")
                    free(act.activation(xnT[:], bank_of("h_T")[:, 0:S], ACT.Identity, bias=vec(LN1B), scale=vec(LN1G)),
                         "h_T")
                if slot == 15:
                    full(act, t, "qk")
                    wait(act, qk_split, 4 * b)
                    for n in range(2):
                        last = act.activation(qkf[:, n, :], bank_of("qk")[:, n * S:(n + 1) * S], ACT.Identity,
                                              bias=vec(BQ + n))
                    free(last, "qk")

            def back(t, slot):
                b = t - BACK
                if slot == 3:
                    full(act, t, "ctx_T")
                    free(act.activation(o_T[:], bank_of("ctx_T")[:, 0:S], ACT.Copy), "ctx_T")
                if slot == 9:
                    full(act, t, "moe_in_T")
                    wait(act, kept, 2 * b)
                    free(act.activation(xmT[:], bank_of("moe_in_T")[:, 0:S], ACT.Identity, bias=vec(LN2B),
                                        scale=vec(LN2G)), "moe_in_T")

            drive(act, iteration)

            act.wait_ge(route_step, 4)
            act.activation(shifted[:].rearrange("p t n -> p (t n)"), shifted[:].rearrange("p t n -> p (t n)"), ACT.Exp
                           ).then_inc(route_exp, 1)

            def shared_gelu(k, n):
                g = 2 * k + n
                if later(k):
                    act.wait_ge(down_full, g - 1)
                for c in range(FC):
                    act.wait_ge(up_full, g * FC + c + 1)
                    act.activation(hid[:, n, c, :], bank[4 + c % 2][:], ACT.Gelu, bias=vec(B1 + E * FC + c)
                                   ).then_inc(gelu_done, 1)

            drive_groups(act, shared_gelu)

            def moe_turn(k, n):
                act.wait_ge(tile_T_full, 2 * k + n + 1)
                act.activation(tile_T[:, n, :], bank[n][:, 0:P], ACT.Identity, bias=vec(LN2B), scale=vec(LN2G)
                               ).then_inc(tile_T_ready, 1)

            def moe_gelu(k, n):
                j = 2 * k + n
                act.wait_ge(moe_up_full, j + 1)
                if later(k):
                    act.wait_ge(moe_y_full, j - 1)
                for c in range(FC):
                    act.activation(hid[:, n, c, 0:P], bank[4 + n][:, c * P:(c + 1) * P], ACT.Gelu,
                                   bias=staged[:, n, WB1 + c:WB1 + c + 1]).then_inc(moe_gelu_done, 1)

            def moe_steps(k):
                moe_turn(k, 1)
                moe_gelu(k, 0)
                moe_turn(k + 1, 0)
                moe_gelu(k, 1)

            moe_turn(0, 0)
            moe_steps(0)
            with act.Fori(1, MAX_TILES // 2) as k:
                moe_steps(k)
            moe_gelu(MAX_TILES // 2, 0)

            def store(k, n):
                g = 2 * k + n
                act.wait_ge(fin_ready[n], k + 1)
                act.dma_start(out_d[bass.ds(g * GB, GB), :, :].rearrange("b (n p) d -> p (b n) d", p=P), fin_moe[:, n]
                              ).then_inc(fin_stored[n], 16)

            drive_groups(act, store)

        @block.vector
        def _(dve):
            dve.memset(half_neg[:], -0.5).then_inc(half_ready, 1)
            dve.memset(va[:], 1.0).then_inc(half_ready, 1)
            dve.wait_ge(silu_exp, 1)
            dve.tensor_scalar(c_exp, c_exp, 1.0, None, ALU.add).then_inc(silu_step, 1)
            dve.wait_ge(silu_step, 1)
            dve.reciprocal(c_exp, c_exp).then_inc(silu_step, 1)
            dve.wait_ge(silu_step, 2)
            dve.tensor_tensor(c_silu, c_in, c_exp, ALU.mult).then_inc(silu_step, 1)
            dve.wait_ge(setup_full, 1)
            dve.tensor_copy(c_T, bank[0][:, 0:B]).then_inc(setup_taken, 1)
            dve.wait_ge(setup_full, 2)
            dve.tensor_copy(vecs_T[:, 0:NVEC], bank[1][:, 0:NVEC]).then_inc(setup_taken, 1)
            dve.wait_ge(setup_full, 4)
            for n in range(2):
                dve.tensor_copy(mods[:, 3 * n:3 * n + 3, :], bank[2 + n][0:B, 0:3 * D].rearrange("b (n d) -> b n d", d=D)
                                ).then_inc(mod_step, 1)
            dve.wait_ge(mod_step, 2)
            dve.tensor_scalar(mods[:, 1, :], mods[:, 1, :], 1.0, None, ALU.add).then_inc(mod_step, 1)
            dve.tensor_scalar(mods[:, 4, :], mods[:, 4, :], 1.0, None, ALU.add).then_inc(mods_ready, 1)
            steps = 3
            for n, row in enumerate((2, 5)):
                g = mods[:, row, :]
                if n:
                    dve.wait_ge(mods_ready, 2)
                dve.tensor_scalar(gsign, g, 0.0, 2.0, ALU.is_ge, ALU.mult).then_inc(mod_step, 1)
                dve.tensor_scalar(gabs, g, -1.0, 0.25, ALU.mult, ALU.max).then_inc(mod_step, 1)
                dve.wait_ge(mod_step, steps + 2)
                dve.tensor_tensor(gabs, gabs, g, ALU.max).then_inc(mod_step, 1)
                dve.wait_ge(mod_step, steps + 3)
                dve.scalar_tensor_tensor(g, gsign, -1.0, gabs, ALU.add, ALU.mult).then_inc(mods_ready, 1)
                steps += 3
            dve.memset(slots0[:], 0.0).then_inc(slots_cleared, 1)
            dve.wait_ge(setup_full, 6)
            dve.tensor_copy(modT[:].rearrange("p n b -> p (n b)"), bank[0][:, 0:2 * B]).then_inc(setup_taken, 1)
            dve.wait_ge(weights_loaded, 16 * len(WEIGHTS))

            def free(ins, name):
                ins.then_inc(work_free[JOB[name] % 2], 1)

            def bank_of(name):
                return work[JOB[name] % 2]

            def moments(src, st, mv, b, stats, mean):
                for n in range(TPB):
                    dve.bn_stats(st[:, n, :], src(n)).then_inc(stats, 1)
                wait_apart(dve, stats, 2 * b + 2)
                for n in range(TPB):
                    dve.bn_aggr(mv[:, n, :], st[:, n, :]).then_inc(mean, 1)

            def normalise(dst, src, mv, rs, b, rstd, norm):
                dve.wait_ge(rstd, 2 * b + 2)
                for n in range(TPB):
                    dve.tensor_scalar(dst[:, n:n + 1, :], src(n), mv[:, n, 0:1], rs[:, n:n + 1], ALU.subtract, ALU.mult
                                      ).then_inc(norm, 1)

            def iteration(t, r):
                for slot in range(HEADS):
                    if active(t, MAX):
                        b = t - MAX
                        if slot == 0:
                            if active(t - 1, MAX):
                                full(dve, t - 1, "max_T_lo")
                        if slot == HALF and active(t, EXP):
                            full(dve, t, "max_T_hi")
                        dve.wait_ge(max_full, b * HEADS + slot + 1)
                        dve.tensor_reduce(neg_max[:, slot // HALF, :, slot % HALF],
                                          max_bank[slot % 2][:].rearrange("p (q k) -> p q k", q=TPB), AX.X, ALU.max,
                                          negate=True).then_inc(max_done, 1)
                    if active(t, FRONT):
                        front(t, slot)
                    if active(t, BACK):
                        back(t, slot)
                    if active(t, LOAD) and slot == 13:
                        wait_apart(dve, x_loaded, 16 * (t - LOAD) + 16)
                        moments(lambda n: tile(res, t, n), st_a, mv_a, t, stats_a, mean_a)
                    if active(t, LOAD) and slot == 15:
                        if active(t, FRONT):
                            full(dve, t, "x_T")
                        normalise(xn, lambda n: tile(res, t, n), mv_a, rs_a, t, rstd_a, norm_a)

            def front(t, slot):
                b = t - FRONT
                if slot == 1:
                    full(dve, t, "qv")
                    w = bank_of("qv")[:].rearrange("p (n two d) -> p n two d", n=TPB, two=2)
                    dve.tensor_reduce(q_neg[:], w[:, :, 0, :], AX.X, ALU.max, negate=True).then_inc(q_max_ready, 1)
                if slot == 2:
                    full(dve, t, "k")
                    dve.tensor_reduce(k_neg[:], bank_of("k")[:, 0:S], AX.X, ALU.max, negate=True
                                      ).then_inc(k_max_ready, 1)
                if slot == 6:
                    taken(dve, t, "k")
                    dve.reciprocal(k_rec[:], k_sum[:]).then_inc(recips, 1)
                    dve.reciprocal(q_rec[:], q_sum[:]).then_inc(recips, 1)
                    dve.wait_ge(recips, 2 * b + 2)
                    full(dve, t, "lin_m")
                    free(dve.tensor_scalar(m_lin[:], bank_of("lin_m")[:, 0:D], k_rec[:], LIN_SCALE, ALU.mult, ALU.mult),
                         "lin_m")
                if slot == 7:
                    full(dve, t, "lin_out")
                    for n in range(TPB):
                        last = dve.scalar_tensor_tensor(y_lin[:, n, :], bank_of("lin_out")[:, n * D:(n + 1) * D],
                                                        q_rec[:, n:n + 1], b_lo[:], ALU.mult, ALU.add)
                    free(last, "lin_out")
                if slot == 9:
                    wait_apart(dve, x1_ready, b + 1)
                    moments(lambda n: tile(res, b, n), st_b, mv_b, b, stats_b, mean_b)
                if slot == 10:
                    normalise(h_norm, lambda n: tile(res, b, n), mv_b, rs_b, b, rstd_b, norm_b)
                if slot == 12:
                    wait_apart(dve, h2_ready, b + 1)
                    moments(lambda n: tile(keep, b, n), st_c, mv_c, b, stats_c, mean_c)
                if slot == 13:
                    normalise(xc, lambda n: tile(keep, b, n), mv_c, rs_c, b, rstd_c, norm_c)
                if slot == 15:
                    full(dve, t, "v")
                    wait(dve, va_ready, b)
                    free(dve.tensor_tensor(v_tmp[:], bank_of("v")[:, 0:TPB * D].rearrange("p (n d) -> p n d", d=D),
                                           over(b_v[:], TPB), ALU.add), "v")

            def back(t, slot):
                b = t - BACK
                if slot in (1, 2):
                    n, name = slot - 1, f"ctx_rows{slot - 1}"
                    full(dve, t, name)
                    w = bank_of(name)[:].rearrange("p (h c) -> p h c", c=32)
                    dve.reciprocal(o_rec[:, n, :], w[:, :, DH]).then_inc(o_rec_ready, 1)
                    dve.wait_ge(o_rec_ready, 2 * b + n + 1)
                    free(dve.tensor_tensor(o_rows[:, n, :].rearrange("p (h d) -> p h d", d=DH), w[:, :, 0:DH],
                                           o_rec[:, n, :].unsqueeze(2).to_broadcast([P, HEADS, DH]), ALU.mult), name)
                if slot == 5:
                    full(dve, t, "att_out")
                    dve.wait_ge(h2b_ready, b + 1)
                    wait(dve, x3_scaled, b)
                    free(dve.tensor_tensor(x3[:], bank_of("att_out")[:, 0:TPB * D].rearrange("p (n d) -> p n d", d=D),
                                           h2b[:], ALU.add), "att_out")
                if slot == 6:
                    taken(dve, t, "att_out")
                    moments(lambda n: x3[:, n:n + 1, :], st_d, mv_d, b, stats_d, mean_d)
                if slot == 8:
                    wait(dve, kept, 2 * b)
                    normalise(xm, lambda n: x3[:, n:n + 1, :], mv_d, rs_d, b, rstd_d, norm_d)
                if slot == 10:
                    full(dve, t, "logits")
                    free(dve.tensor_tensor(batch(logit, b), bank_of("logits")[:, 0:TPB * NL]
                                           .rearrange("p (n d) -> p n d", d=NL),
                                           b_log[:].unsqueeze(1).to_broadcast([P, TPB, NL]), ALU.add), "logits")

            drive(dve, iteration)

            count = [0]

            def step(ins):
                ins.then_inc(route_step, 1)
                count[0] += 1
                dve.wait_ge(route_step, count[0])

            def per_tile(x, n):
                return x.unsqueeze(2).to_broadcast([P, TILES, n])

            def tiles_experts(x):
                return x.rearrange("p (t e) -> p t e", e=E)

            for n in range(2):
                dve.wait_ge(work_free[n], bank_uses(PIPE, n))
            dve.wait_ge(res_ready, B)
            dve.wait_ge(kept, 2 * B)
            dve.memset(ones[:], 1.0).then_inc(ones_again, 1)
            gates = logit[:, :, 0:E]
            step(dve.tensor_reduce(lmax[:, 0, :], gates, AX.X, ALU.max))
            step(dve.tensor_reduce(lmax[:, 1, :], logit[:, :, E:NL], AX.X, ALU.max))
            step(dve.tensor_tensor(shifted[:, :, 0:E], gates, per_tile(lmax[:, 0, :], E), ALU.subtract))
            step(dve.tensor_tensor(shifted[:, :, E:NL], logit[:, :, E:NL], per_tile(lmax[:, 1, :], 2), ALU.subtract))
            key, a, incl, tot = (tiles_experts(route_buf(n, TILES * E)) for n in range(4))
            onehot3 = tiles_experts(onehot[:])
            step(dve.tensor_tensor(key, gates, per_tile(lmax[:, 0, :], E), ALU.is_equal))
            step(dve.tensor_tensor(key, key, order[:].unsqueeze(1).to_broadcast([P, TILES, E]), ALU.mult))
            step(dve.tensor_reduce(w_moe[:], key, AX.X, ALU.max))
            step(dve.tensor_tensor(onehot3, key, per_tile(w_moe[:], E), ALU.is_equal))
            dve.wait_ge(counts_full, 2)
            step(dve.tensor_copy(tot, tiles_experts(bank[3][:])))
            incl = route_buf(2, TILES * E).rearrange("p (e t) -> p e t", t=TILES)
            zero = route_buf(4, TILES)
            step(dve.memset(zero, 0.0))
            for e in range(E):
                dve.tensor_tensor_scan(incl[:, e, :], tot[:, :, e], zero, 0.0, ALU.add, ALU.add).then_inc(route_step, 1)
            count[0] += E
            dve.wait_ge(route_step, count[0])
            tiles_e, ends, base = small[:, 0, :], small[:, 1, :], small[:, 2, :]
            cmp = route_buf(5, TILES * E).rearrange("p (e t) -> p e t", t=TILES)
            step(dve.tensor_tensor(cmp, tile_first[:].unsqueeze(1).to_broadcast([P, E, TILES]),
                                   incl[:, :, TILES - 1:TILES].to_broadcast([P, E, TILES]), ALU.is_lt))
            step(dve.tensor_reduce(tiles_e, cmp, AX.X, ALU.add))
            step(dve.tensor_tensor_scan(ends, tiles_e, zero[:, 0:E], 0.0, ALU.add, ALU.add))
            step(dve.tensor_tensor(base, ends, tiles_e, ALU.subtract))
            step(dve.tensor_scalar(base, base, float(P), None, ALU.mult))
            step(dve.tensor_tensor(a, incl.rearrange("p e t -> p t e"), tot, ALU.subtract))
            step(dve.tensor_tensor(a, a, tiles_experts(bank[2][:]), ALU.add))
            step(dve.tensor_tensor(a, a, base.unsqueeze(1).to_broadcast([P, TILES, E]), ALU.add))
            step(dve.tensor_tensor(a, a, onehot3, ALU.mult))
            step(dve.tensor_reduce(lmax[:, 0, :], a, AX.X, ALU.add))
            step(dve.tensor_copy(slot_u[:], lmax[:, 0, :]))
            cmp2 = hid_flat[:, 0:MAX_TILES * (E - 1)].rearrange("p (t e) -> p t e", e=E - 1)
            step(dve.tensor_tensor(cmp2, ends[:, 0:E - 1].unsqueeze(1).to_broadcast([P, MAX_TILES, E - 1]),
                                   tile_no[:].unsqueeze(2).to_broadcast([P, MAX_TILES, E - 1]), ALU.is_le))
            exp_f = route_buf(4, MAX_TILES)
            step(dve.tensor_reduce(exp_f, cmp2, AX.X, ALU.add))
            step(dve.tensor_copy(expert_u[:], exp_f))
            dve.wait_ge(route_exp, 1)
            step(dve.tensor_reduce(w_moe[:], shifted[:, :, 0:E], AX.X, ALU.add))
            step(dve.tensor_reduce(w_rm[:], shifted[:, :, E:NL], AX.X, ALU.add))
            step(dve.reciprocal(w_moe[:], w_moe[:]))
            step(dve.reciprocal(w_rm[:], w_rm[:]))
            step(dve.tensor_tensor(w_moe[:], w_moe[:], w_rm[:], ALU.mult))
            step(dve.tensor_tensor(token_meta[:, :, 1], w_moe[:], shifted[:, :, E], ALU.mult))
            dve.tensor_tensor(w_rm[:], w_rm[:], shifted[:, :, E + 1], ALU.mult).then_inc(route_ready, 1)
            dve.wait_ge(route_ready, 1)

            dve.wait_ge(experts_loaded, 16 * 3 * E)
            b1_all = vecs_T[:, B1:B1 + E * FC].rearrange("p (e c) -> p e c", c=FC)
            dve.tensor_copy(w_exp[:, :, WB1:WB2], b1_all).then_inc(weight_step, 1)

            def shared_out(k, n):
                g = 2 * k + n
                wn = w_rm[:, bass.ds(g * GT, GT)].unsqueeze(2).to_broadcast([P, GT, D])
                dve.wait_ge(down_full, g + 1)
                wait(dve, shared_added, g)
                dve.tensor_tensor(y_shared[:], bank[6 + n][:].rearrange("p (m d) -> p m d", d=D),
                                  over(w_shared[:, WB2:WCOLS], GT), ALU.add).then_inc(down_taken, 1)
                dve.wait_ge(down_taken, g + 1)
                dve.tensor_tensor(y_shared[:], y_shared[:], wn, ALU.mult).then_inc(shared_step, 1)
                dve.wait_ge(shared_step, 2 * g + 1)
                dve.wait_ge(gb2_loaded, 16 * g + 16)
                y4 = y_shared[:].rearrange("p (b n) d -> p b n d", n=TPB)
                dve.tensor_tensor(y4, y4, gb2[:].unsqueeze(2).to_broadcast([P, GB, TPB, D]), ALU.mult
                                  ).then_inc(shared_step, 1)
                dve.wait_ge(shared_step, 2 * g + 2)
                rows = res[:, bass.ds(g * GT, GT), :]
                dve.tensor_tensor(rows, rows, y_shared[:], ALU.add).then_inc(shared_added, 1)

            drive_groups(dve, shared_out)

            dve.wait_ge(weight_step, 1)

            def stage_weights(k, n):
                j = 2 * k + n
                if later(k):
                    dve.wait_ge(moe_y_taken, j - 1)
                expert = dve.value_load(expert_u[0:1, bass.ds(j, 1)], min_val=0, max_val=E - 1)
                dve.tensor_copy(staged[:, n, :], w_exp[:, bass.ds(expert, 1), :].rearrange("p e w -> p (e w)")
                                ).then_inc(stage_ready, 1)

            def moe_out(k, n):
                j = 2 * k + n
                dve.wait_ge(moe_y_full, j + 1)
                dve.wait_ge(stage_ready, j + 1)
                if later(k):
                    dve.wait_ge(pool_step, 2 * (j - 1))
                dve.tensor_tensor(y_moe[:, n, :], bank[6 + n][:, 0:D], staged[:, n, WB2:WCOLS], ALU.add
                                  ).then_inc(moe_y_taken, 1)

            def moe_steps(k):
                for n in range(2):
                    moe_out(k, n)
                    stage_weights(k + 1, n)

            stage_weights(0, 0)
            stage_weights(0, 1)
            moe_steps(0)
            with dve.Fori(1, MAX_TILES // 2 - 1) as k:
                moe_steps(k)
            moe_out(MAX_TILES // 2 - 1, 0)
            stage_weights(MAX_TILES // 2, 0)
            moe_out(MAX_TILES // 2 - 1, 1)
            moe_out(MAX_TILES // 2, 0)

            def final(k, n):
                g = 2 * k + n
                dve.wait_ge(fin_loaded[n], 32 * k + 32)
                f4 = fin_moe[:, n].rearrange("p (b m) d -> p b m d", m=TPB)
                dve.tensor_tensor(f4, f4, fin_gb[:, n].unsqueeze(2).to_broadcast([P, GB, TPB, D]), ALU.mult
                                  ).then_inc(fin_step, 1)
                dve.wait_ge(fin_step, g + 1)
                dve.tensor_tensor(fin_moe[:, n], fin_moe[:, n], res[:, bass.ds(g * GT, GT), :], ALU.add
                                  ).then_inc(fin_ready[n], 1)

            drive_groups(dve, final)

        @block.gpsimd
        def _(pool):
            pool.memset(ident[:], 0.0).then_inc(ident_ready, 1)
            pool.wait_ge(ident_ready, 1)
            pool.affine_select(out=ident[:], in_=ident[:], compare_op=ALU.not_equal, fill=1.0, base=0,
                               pattern=[[-1, P]], channel_multiplier=1).then_inc(ident_ready, 1)
            pool.iota(tile_first[:], [[P, TILES]], base=0, channel_multiplier=0, allow_small_or_imprecise_dtypes=True
                      ).then_inc(consts_ready, 1)
            pool.iota(tile_no[:], [[1, MAX_TILES]], base=0, channel_multiplier=0, allow_small_or_imprecise_dtypes=True
                      ).then_inc(consts_ready, 1)
            pool.iota(order[:], [[-1, E]], base=E, channel_multiplier=0, allow_small_or_imprecise_dtypes=True
                      ).then_inc(consts_ready, 1)
            pool.iota(token_meta[:, :, 0], [[P, TILES]], base=0, channel_multiplier=1,
                      allow_small_or_imprecise_dtypes=True).then_inc(consts_ready, 1)
            pool.wait_ge(slots_cleared, 1)
            pool.iota(slots0[:, :, D], [[P, MAX_TILES]], base=B * S, channel_multiplier=1,
                      allow_small_or_imprecise_dtypes=True).then_inc(slots_cleared, 1)
            pool.wait_ge(slots_cleared, 2)
            pool.dma_start(sorted_dram.rearrange("(t p) n -> p t n", p=P), slots0).then_inc(slots_stored, 16)
            pool.wait_ge(half_ready, 2)

            def rstd(mv, rs, b, mean, ready):
                wait_apart(pool, mean, 2 * b + 2)
                pool.tensor_scalar(rs[:], mv[:, :, 1], EPS, None, ALU.add).then_inc(ready, 1)
                wait_apart(pool, ready, 2 * b + 1)
                pool.tensor_tensor(rs[:], rs[:], half_neg[:], ALU.pow).then_inc(ready, 1)

            def split(src, out, done, sem_split):
                pool.tensor_copy(out(0), src).then_inc(sem_split, 1)
                wait_apart(pool, sem_split, done + 1)
                pool.tensor_tensor(src, src, out(0), ALU.subtract).then_inc(sem_split, 1)
                wait_apart(pool, sem_split, done + 2)
                pool.tensor_copy(out(1), src).then_inc(sem_split, 1)
                wait_apart(pool, sem_split, done + 3)
                pool.tensor_tensor(out(2), src, out(1), ALU.subtract).then_inc(sem_split, 1)

            def split_max(b, half):
                wait_apart(pool, max_spread[half], 48 * b)
                split(max_f[:, half, :], lambda i: max_parts[:, half, i, :], 4 * b,
                      max_split[half])

            def iteration(t, r):
                for slot in range(HEADS):
                    if active(t, EXP) and slot == 0:
                        taken(pool, t, "max_T_hi", wait_apart)
                        split_max(t - EXP, 1)
                    if active(t, BACK):
                        back(t, slot)
                    if active(t, SPREAD) and slot == 1:
                        b, buf = t - SPREAD, (r - SPREAD) % NBUF
                        taken(pool, t - 1, "qk", wait_apart)
                        wait_apart(pool, split_stored, 32 * b)
                        split(qkf[:], lambda i: parts[:, :, i, :], 4 * b, qk_split)
                        taken(pool, t - 1, "v", wait_apart)
                        wait_apart(pool, pv_done, (b - NBUF + 1) * HEADS)
                        pool.tensor_copy(va[:, buf, :, 0:HEADS * VW].rearrange("p n (h w) -> p n h w", w=VW)[:, :, :, 0:DH],
                                         v_tmp[:].rearrange("p n (h d) -> p n h d", d=DH)).then_inc(va_ready, 1)
                    if active(t, FRONT):
                        front(t, slot)
                    if active(t, MAX) and slot == HALF:
                        taken(pool, t, "max_T_lo", wait_apart)
                        split_max(t - MAX, 0)
                    if active(t, LOAD) and slot == 14:
                        rstd(mv_a, rs_a, t, mean_a, rstd_a)
                if isinstance(t, int) and t == 1:
                    pool.wait_ge(slots_stored, 16)
                    pool.memset(k_all[:], 1.0).then_inc(ones_ready, 1)

            def front(t, slot):
                b = t - FRONT
                if slot == 7:
                    taken(pool, t, "lin_out", wait_apart)
                    wait_apart(pool, mod3_loaded, 16 * b + 16)
                    pool.tensor_tensor(y_lin[:], y_lin[:], over(mod3[:, 0, :], TPB), ALU.mult).then_inc(y_scaled, 1)
                    wait_apart(pool, y_scaled, b + 1)
                    pool.tensor_tensor(batch(res, b), batch(res, b), y_lin[:], ALU.add).then_inc(x1_ready, 1)
                if slot == 9:
                    rstd(mv_b, rs_b, b, mean_b, rstd_b)
                if slot == 10:
                    wait_apart(pool, norm_b, 2 * b + 2)
                    pool.tensor_tensor(h_norm[:], h_norm[:], over(mod3[:, 1, :], TPB), ALU.mult).then_inc(h_scaled, 1)
                    wait_apart(pool, h_scaled, b + 1)
                    pool.tensor_tensor(batch(keep, b), h_norm[:], over(mod3[:, 2, :], TPB), ALU.add).then_inc(h2_ready, 1)
                if slot == 12:
                    rstd(mv_c, rs_c, b, mean_c, rstd_c)

            def back(t, slot):
                b = t - BACK
                if slot == 0:
                    wait_apart(pool, res_ready, b)
                    pool.tensor_tensor(h2b[:], batch(keep, b), over(b_ao[:], TPB), ALU.add).then_inc(h2b_ready, 1)
                if slot == 6:
                    rstd(mv_d, rs_d, b, mean_d, rstd_d)
                    wait_apart(pool, gb_loaded, 16 * b + 16)
                    pool.tensor_tensor(h2b[:], x3[:], mod_gb[:].to_broadcast([P, TPB, D]), ALU.mult
                                       ).then_inc(x3_scaled, 1)
                    wait_apart(pool, x3_scaled, b + 1)
                    pool.tensor_tensor(batch(res, b), batch(res, b), h2b[:], ALU.add).then_inc(res_ready, 1)
                if slot == 9:
                    wait_apart(pool, norm_d, 2 * b + 2)
                    pool.tensor_copy(batch(keep, b), xm[:]).then_inc(kept, 1)
                if slot == 10:
                    taken(pool, t, "moe_in_T", wait_apart)
                    pool.tensor_copy(moe_in_T[:, bass.ds(b * S, S)], xmT[:]).then_inc(kept, 1)

            drive(pool, iteration)

            pool.wait_ge(ones_again, 1)
            pool.affine_select(out=upper[:], in_=ones[:], compare_op=ALU.is_gt, fill=0.0, base=0,
                               pattern=[[1, P]], channel_multiplier=-1).then_inc(consts_ready, 1)

            pool.wait_ge(route_ready, 1)

            def scatter(k, n):
                i = 4 * k + n
                if later(k):
                    wait_apart(pool, sorted_sem[n], 16 * k)
                pool.tensor_copy(out_rows[:, n:n + 1, 0:D], keep[:, bass.ds(i, 1), :]).then_inc(scatter_staged, 1)
                pool.tensor_copy(out_rows[:, n:n + 1, D:ROW], token_meta[:, bass.ds(i, 1), :]).then_inc(scatter_staged, 1)
                pool.tensor_copy(out_slots[:, n:n + 1], slot_u[:, bass.ds(i, 1)]).then_inc(scatter_staged, 1)
                wait_apart(pool, scatter_staged, 3 * i + 3)
                pool.indirect_dma_start(sorted_dram, bass.IndirectOffsetOnAxis(ap=out_slots[:, n:n + 1], axis=0),
                                        out_rows[:, n, :], None).then_inc(sorted_sem[n], 16)

            for n in range(4):
                scatter(0, n)
            with pool.Fori(1, TILES // 4) as k:
                for n in range(4):
                    scatter(k, n)

            def take_meta(k, n):
                wait_apart(pool, rows_in_loaded[n], 16 * k + 16)
                pool.tensor_copy(meta[:, n, :], rows_buf[:, n, D:ROW]).then_inc(meta_taken[n], 1)

            def scatter_moe(k, n):
                j = 2 * k + n
                if later(k):
                    wait_apart(pool, moe_scattered[n], 16 * k)
                wait_apart(pool, meta_taken[n], k + 1)
                pool.tensor_copy(meta_slot[:, n:n + 1], meta[:, n, 0:1]).then_inc(pool_step, 1)
                wait_apart(pool, moe_y_taken, j + 1)
                pool.tensor_scalar(y_out[:, n, :], y_moe[:, n, :], meta[:, n, 1:2], None, ALU.mult).then_inc(pool_step, 1)
                wait_apart(pool, pool_step, 2 * j + 2)
                pool.indirect_dma_start(moe_dram, bass.IndirectOffsetOnAxis(ap=meta_slot[:, n:n + 1], axis=0),
                                        y_out[:, n, :], None).then_inc(moe_scattered[n], 16)

            def moe_steps(k):
                take_meta(k, 1)
                scatter_moe(k, 0)
                take_meta(k + 1, 0)
                scatter_moe(k, 1)

            take_meta(0, 0)
            moe_steps(0)
            with pool.Fori(1, MAX_TILES // 2) as k:
                moe_steps(k)
            scatter_moe(MAX_TILES // 2, 0)


INPUTS = ("x c wmod wqkv_lin wo_lin bo_lin vec wqkv bqk bv wo bo wlog blog w1 b1 w2 b2").split()


def kernel(L0_attn_x, L0_attn_Wq, L0_attn_Wk, L0_attn_Wv, L0_attn_Wo, L0_attn_bo, L0_ffn_ln1_g, L0_ffn_ln1_b,
           L0_ffn_Wqkv, L0_ffn_bqkv, L0_ffn_Wo, L0_ffn_bo, L0_ffn_ln2_g, L0_ffn_ln2_b, L0_ffn_gate_w, L0_ffn_W1,
           L0_ffn_b1, L0_ffn_W2, L0_ffn_b2, L0_ffn_rW1, L0_ffn_rb1, L0_ffn_rW2, L0_ffn_rb2, L0_ffn_coef_w,
           L0_ffn_coef_b, L0_c, L0_wmod):
    import numpy as np
    import concourse.bacc as bacc
    from concourse.bass_utils import run_bass_kernel_spmd

    def heads_last(w):
        w = np.asarray(w)
        return w.reshape(*w.shape[:-1], HEADS, DH).swapaxes(-1, -2).reshape(w.shape)

    wqkv, bqkv = np.asarray(L0_ffn_Wqkv), np.asarray(L0_ffn_bqkv)
    data = {
        "x": L0_attn_x, "c": L0_c, "wmod": L0_wmod,
        "wqkv_lin": np.stack([L0_attn_Wq, L0_attn_Wk, L0_attn_Wv]), "wo_lin": L0_attn_Wo, "bo_lin": L0_attn_bo,
        "vec": np.stack([L0_ffn_ln1_g, L0_ffn_ln1_b, L0_ffn_ln2_g, L0_ffn_ln2_b]),
        "wqkv": np.concatenate([heads_last(wqkv[:, 0:D]), heads_last(wqkv[:, D:2 * D]), wqkv[:, 2 * D:]], 1),
        "bqk": np.stack([heads_last(bqkv[0:D]), heads_last(bqkv[D:2 * D])]), "bv": bqkv[2 * D:],
        "wo": L0_ffn_Wo, "bo": L0_ffn_bo,
        "wlog": np.concatenate([L0_ffn_gate_w, L0_ffn_coef_w], 1),
        "blog": np.concatenate([np.zeros(E, np.float32), L0_ffn_coef_b]),
        "w1": np.concatenate([L0_ffn_W1, np.asarray(L0_ffn_rW1)[None]]),
        "b1": np.concatenate([L0_ffn_b1, np.asarray(L0_ffn_rb1)[None]]).reshape((E + 1) * FC, P),
        "w2": np.concatenate([L0_ffn_W2, np.asarray(L0_ffn_rW2)[None]]),
        "b2": np.concatenate([L0_ffn_b2, np.asarray(L0_ffn_rb2)[None]]),
    }
    nc = bacc.Bacc("TRN2", target_bir_lowering=False, num_devices=1)
    arrays, args = {}, []
    for name in INPUTS:
        a = np.ascontiguousarray(data[name])
        arrays[f"in_{name}"] = a
        args.append(nc.dram_tensor(f"in_{name}", a.shape, mybir.dt.from_np(a.dtype), kind="ExternalInput").ap())
    out = nc.dram_tensor("out", [B, S, D], F32, kind="ExternalOutput").ap()
    adaln_block(nc, *args, out)
    got = run_bass_kernel_spmd(nc, [arrays], core_ids=[0])
    return got.results[0]["out"]
```

```python
from contextlib import ExitStack

import concourse.bass as bass
from concourse import mybir

ALU = mybir.AluOpType
ACT = mybir.ActivationFunctionType
AX = mybir.AxisListType
F32 = mybir.dt.float32
BF16 = mybir.dt.bfloat16
U32 = mybir.dt.uint32

P = 128
B, S, D = 32, 256, 128
TPB = S // P
TILES = B * TPB
HEADS, DH = 16, 8
FFN, E = 512, 8
FC = FFN // P
EPS = 1e-5
ATT_SCALE = float(DH) ** -0.5
LIN_SCALE = float(DH) ** -0.5 / D
PARTS = 3
QK_ROWS = PARTS * PARTS * DH
ALL_ROWS = QK_ROWS + PARTS
NBUF = 3
HALF = HEADS // 2
VW = DH + 1
VA_COLS = HEADS * VW + 32 - VW
MAX_TILES = TILES + E - 1
NB = 4
FG = 8
SLOTS = MAX_TILES * P
ROW = D + 2
NVEC = 6 + (E + 1) * FC
GT = 4
GB = GT // TPB
GROUPS = TILES // GT
WB1 = FFN + FC * P
WB2 = WB1 + FC
WCOLS = WB2 + D
NL = E + 2

LOAD, FRONT, NORM, SPREAD, MAX, EXP, BACK = range(7)
JOBS = [
    ("x_T", FRONT, 0), ("v", SPREAD, 1), ("max_T_hi", EXP, 1), ("qv", FRONT, 2), ("k", FRONT, 3), ("ctx_rows0", BACK, 4),
    ("ctx_rows1", BACK, 5), ("qk_T", FRONT, 6), ("ctx_T", BACK, 7), ("lin_ctx", FRONT, 8), ("max_T_lo", MAX, 9),
    ("att_out", BACK, 9), ("lin_m", FRONT, 10), ("h_T", NORM, 11), ("lin_out", FRONT, 12), ("qk", NORM, 13),
    ("moe_in_T", BACK, 14), ("logits", BACK, 15),
]
JOB = {name: n for n, (name, _, _) in enumerate(JOBS)}
SLOT = {name: slot for name, _, slot in JOBS}
PIPE = B + BACK
MAIN_FROM = BACK + 1
MAIN_TO = MAIN_FROM + (B - MAIN_FROM) // NBUF * NBUF


def done_iterations(t, stage):
    return min(max(t - stage, 0), B) if isinstance(t, int) else t - stage


def active(t, stage):
    return 0 <= t - stage < B if isinstance(t, int) else True


def bank_uses(t, job):
    n = 0
    for k in range(job % 2, len(JOBS), 2):
        n = n + done_iterations(t, JOBS[k][1])
        if k < job and active(t, JOBS[k][1]):
            n = n + 1
    return n


def wait(eng, sem, value):
    if not isinstance(value, int) or value > 0:
        eng.wait_ge(sem, value)


def adaln_block(nc, x_d, c_d, wmod_d, wqkv_lin_d, wo_lin_d, bo_lin_d, vec_d, wqkv_d, bqk_d, bv_d, wo_d, bo_d,
                wlog_d, blog_d, w1_d, b1_d, w2_d, b2_d, out_d):
    with ExitStack() as ctx:
        def sb(name, shape, dt=F32):
            return ctx.enter_context(nc.sbuf_tensor(name, shape, dt))

        def sem(name):
            return ctx.enter_context(nc.semaphore(name))

        mod_dram = nc.dram_tensor("mod_rows", [B, 4, D], F32, kind="Internal").ap()
        split_dram = nc.dram_tensor("split_qk", [2, PARTS, P, S], BF16, kind="Internal").ap()
        sorted_dram = nc.dram_tensor("sorted_tokens", [SLOTS, ROW], F32, kind="Internal").ap()
        moe_dram = nc.dram_tensor("moe_out", [B * S + SLOTS, D], F32, kind="Internal").ap()

        res = sb("res", [P, TILES, D])
        keep = sb("keep", [P, TILES, D])
        moe_in_T = sb("moe_in_T", [P, B * S])
        big = sb("big", [P, NBUF * HEADS * S])
        w_shared = sb("w_shared", [P, WCOLS])
        logit = sb("logit", [P, TILES, NL])
        ident = sb("ident", [P, P])
        ident_half = sb("ident_half", [P, P], BF16)
        vecs_T = sb("vecs_T", [P, 48])
        BIGH = NBUF * HEADS * S // 2
        q_all = big[:, 0:BIGH].bitcast(BF16).rearrange("p (n h s) -> p n h s", n=NBUF, h=HEADS)
        k_all = big[:, BIGH:2 * BIGH].bitcast(BF16).rearrange("p (n h s) -> p n h s", n=NBUF, h=HEADS)
        w_exp = big[:, 0:E * WCOLS].rearrange("p (e n) -> p e n", e=E)
        slots0 = big[:, 0:MAX_TILES * ROW].rearrange("p (t n) -> p t n", n=ROW)
        staged = moe_in_T[:, 0:NB * WCOLS].rearrange("p (n w) -> p n w", n=NB)
        fin = moe_in_T[:].rearrange("p (t d) -> p t d", d=D)
        gb_all = keep[:, 0:B, :]

        w_qv = sb("w_qv", [P, 2 * D])
        w_k = sb("w_k", [P, D])
        w_lo = sb("w_lo", [P, D])
        w_qkv = sb("w_qkv", [P, 3 * D])
        w_ao = sb("w_ao", [P, D])
        w_log = sb("w_log", [P, NL])
        b_lo = sb("b_lo", [P, D])
        b_v = sb("b_v", [P, D])
        b_ao = sb("b_ao", [P, D])
        b_log = sb("b_log", [P, NL])
        half_neg = sb("half_neg", [P, TPB])
        modT = sb("modT", [P, 2, B])
        rows_in = sb("rows_in", [NVEC, P])
        tile_first = sb("tile_first", [P, TILES])
        tile_no = sb("tile_no", [P, MAX_TILES])
        order = sb("order", [P, E])
        token_meta = sb("token_meta", [P, TILES, 2])

        st_a, st_b, st_c, st_d = (sb(f"st_{x}", [P, TPB, 6]) for x in "abcd")
        mv_a, mv_b, mv_c, mv_d = (sb(f"mv_{x}", [P, TPB, 2]) for x in "abcd")
        rs_a, rs_b, rs_c, rs_d = (sb(f"rs_{x}", [P, TPB]) for x in "abcd")
        ARENA = 9920
        arena = sb("arena", [P, ARENA])
        used = [0]

        def take(shape, dt=F32):
            words = 1
            for n in shape:
                words *= n
            if dt == BF16:
                words //= 2
            piece = arena[:, used[0]:used[0] + words]
            used[0] += (words + 7) // 8 * 8

            if dt != F32:
                piece = piece.bitcast(dt)
            names = "abcd"[:len(shape)]
            return piece.rearrange(f"p ({' '.join(names)}) -> p {' '.join(names)}",
                                   **dict(zip(names[1:], shape[1:]))) if len(shape) > 1 else piece

        xn = take([TPB, D])
        hT = take([S])
        q_neg = take([TPB])
        q_sum = take([TPB])
        q_rec = take([TPB])
        q_exp = take([TPB, D])
        v_lin = take([TPB, D])
        k_neg = take([1])
        k_sum = take([1])
        k_rec = take([1])
        k_exp = take([S])
        qk_T = take([2, S])
        ctx_lin = take([D])
        m_lin = take([D])
        y_lin = take([TPB, D])
        h_norm = take([TPB, D])
        xc = take([TPB, D])
        xnT = take([S])
        qkf = take([2, S])
        parts = take([2, PARTS, S], BF16)
        va = take([NBUF, TPB, VA_COLS])
        neg_max = take([2, TPB, HALF])
        max_cols = take([2, TPB, PARTS, HALF], BF16)
        max_parts = sb("max_parts", [PARTS * HALF, 2, S], BF16)
        probs = take([2, TPB * S])
        oT = take([HEADS // 4, S])
        o_rec = take([TPB, HEADS])
        o_rows = take([TPB, D])
        o_T = take([S])
        h2b = take([TPB, D])
        x3 = take([TPB, D])
        xm = take([TPB, D])
        xmT = take([S])
        mod_ga = take([1, D])
        mod_b = take([2, D])
        mod_gb = take([1, D])

        used[0] = 0
        upper = take([P])
        ones = take([P])
        onehot = take([TILES * E])
        hid = take([2, FC, GT * P])
        hid_flat = hid[:].rearrange("p n c s -> p (n c s)")

        def route_buf(n, cols):
            return hid_flat[:, n * TILES * E:n * TILES * E + cols]

        lmax = take([2, TILES])
        shifted = take([TILES, NL])
        w_moe = take([TILES])
        w_rm = take([TILES])
        slot_u = take([TILES], U32)
        expert_u = take([MAX_TILES], U32)
        small = take([6, E])
        y_shared = take([GT, D])
        gb2 = take([GB, D])
        out_rows = take([4, ROW])
        out_slots = take([4], U32)
        rows_buf = take([NB, ROW])
        tile_T = take([NB, P])
        y_moe = take([NB, D])
        y_out = take([NB, D])
        meta = take([NB, 2])
        meta_slot = take([NB], U32)
        hid_moe = hid_flat[:, 0:NB * FFN].rearrange("p (n c s) -> p n c s", n=NB, c=FC)

        bank = [ctx.enter_context(nc.psum_tensor(f"bank{n}", [P, 512], F32)) for n in range(8)]
        work, max_bank, exp_bank, o_bank = bank[0:2], bank[2:4], bank[4:6], bank[6:8]

        (c_loaded, rows_loaded, weights_loaded, mods_ready, mods_stored, ident_ready, consts_ready, half_ready,
         silu_step, silu_exp, setup_full, setup_taken, mod_step, slots_cleared, slots_stored, ones_ready) = map(sem, (
             "c_loaded rows_loaded weights_loaded mods_ready mods_stored ident_ready consts_ready half_ready "
             "silu_step silu_exp setup_full setup_taken mod_step slots_cleared slots_stored ones_ready").split())
        (x_loaded, ga_loaded, modb_loaded, gb_loaded, max_full, max_done, exp_full, exp_done, pv_done, q_max_ready, q_exp_done,
         k_max_ready, recips, y_scaled, x1_ready, h_scaled, h2_ready, qk_split, split_stored, qk_spread, norm_used,
         oT_ready, o_rec_ready, h2b_ready, x3_scaled, res_ready, kept) = map(sem, (
             "x_loaded ga_loaded modb_loaded gb_loaded max_full max_done exp_full exp_done pv_done q_max_ready q_exp_done "
             "k_max_ready recips y_scaled x1_ready h_scaled h2_ready qk_split split_stored qk_spread norm_used "
             "oT_ready o_rec_ready h2b_ready x3_scaled res_ready kept").split())
        stats_a, stats_b, stats_c, stats_d = (sem(f"stats_{x}") for x in "abcd")
        mean_a, mean_b, mean_c, mean_d = (sem(f"mean_{x}") for x in "abcd")
        rstd_a, rstd_b, rstd_c, rstd_d = (sem(f"rstd_{x}") for x in "abcd")
        norm_a, norm_b, norm_c, norm_d = (sem(f"norm_{x}") for x in "abcd")
        work_full = [sem(f"work_full{n}") for n in range(2)]
        work_free = [sem(f"work_free{n}") for n in range(2)]
        max_split = [sem(f"max_split{n}") for n in range(2)]
        max_spread = [sem(f"max_spread{n}") for n in range(2)]
        (route_step, route_exp, ones_again, counts_full, route_ready, experts_loaded, gb2_loaded, up_full, gelu_done,
         down_full, down_taken, shared_step, shared_added, scatter_staged, tile_T_full, tile_T_ready, weight_step,
         stage_ready, moe_up_full, moe_gelu_done, moe_y_full, moe_y_taken, pool_step, meta_taken,
         gb_all_loaded, fin_step, fin_stored) = map(sem, (
             "route_step route_exp ones_again counts_full route_ready experts_loaded gb2_loaded up_full gelu_done "
             "down_full down_taken shared_step shared_added scatter_staged tile_T_full tile_T_ready weight_step "
             "stage_ready moe_up_full moe_gelu_done moe_y_full moe_y_taken pool_step meta_taken "
             "gb_all_loaded fin_step fin_stored").split())
        sorted_sem = [sem(f"sorted{n}") for n in range(4)]
        rows_in_loaded = [sem(f"rows_in_loaded{n}") for n in range(NB)]
        moe_scattered = [sem(f"moe_scattered{n}") for n in range(NB)]
        fin_loaded = [sem(f"fin_loaded{n}") for n in range(FG)]
        def mod_rows(b, first, n):
            return mod_dram[bass.ds(b, 1), first:first + n, :].to_broadcast([P, n, D])

        def batch(buf, b):
            return buf[:, bass.ds(b * TPB, TPB), :]

        def tile(buf, b, n):
            return buf[:, bass.ds(b * TPB + n, 1), :]

        def over(row, n):
            return row.unsqueeze(1).to_broadcast([P, n, D])

        def wait_apart(eng, sem, value):
            wait(eng, sem, value)
            if not isinstance(value, int):
                eng.nop(nofuse=True)

        def full(eng, t, name):
            job = JOB[name]
            wait(eng, work_full[job % 2], bank_uses(t, job) + 1)

        def taken(eng, t, name, wait=wait):
            job = JOB[name]
            wait(eng, work_free[job % 2], bank_uses(t, job) + 1)

        def drive(eng, run):
            for t in range(MAIN_FROM):
                run(t, t % NBUF)
            with eng.Fori(0, (MAIN_TO - MAIN_FROM) // NBUF) as k:
                for r in range(NBUF):
                    run(k * NBUF + MAIN_FROM + r, (MAIN_FROM + r) % NBUF)
            for t in range(MAIN_TO, PIPE):
                run(t, t % NBUF)

        def drive_tiles(eng, run):
            rounds = (MAX_TILES - NB) // NB
            for j in range(2 * NB):
                run(j // NB, j % NB)
            with eng.Fori(2, rounds) as k:
                for n in range(NB):
                    run(k, n)
            for j in range(rounds * NB, MAX_TILES + 2):
                run(j // NB, j % NB)

        def moe_tile(k, n):
            k, n = k + n // NB, n % NB
            j = NB * k + n
            if isinstance(k, int) and not 0 <= j < MAX_TILES:
                return k, n, None
            return k, n, j

        def drive_groups(eng, run):
            for n in range(2):
                run(0, n)
            with eng.Fori(1, GROUPS // 2) as k:
                for n in range(2):
                    run(k, n)

        def gb_rows(g):
            return mod_dram[bass.ds(g * GB, GB), 3, :].unsqueeze(0).to_broadcast([P, GB, D])

        def later(k):
            return not isinstance(k, int) or k > 0

        LN1G, LN1B, LN2G, LN2B, BQ, BK, B1 = range(7)

        def vec(n):
            return vecs_T[:, n:n + 1]

        c_in, c_exp, c_silu = xc[0:B, 0, :], xc[0:B, 1, :], h_norm[0:B, 0, :]
        c_T = h_norm[:, 1, 0:B]
        wmod = keep[:, 0:6, :].rearrange("p a b -> p (a b)")
        mods = keep[0:B, 6:12, :]
        gsign, gabs = keep[0:B, 12, :], keep[0:B, 13, :]

        WEIGHTS = [
            (w_qv[:, 0:D], wqkv_lin_d[0]), (w_qv[:, D:2 * D], wqkv_lin_d[2]), (w_k[:], wqkv_lin_d[1]),
            (w_lo[:], wo_lin_d), (w_qkv[:], wqkv_d), (w_ao[:], wo_d), (w_log[:], wlog_d),
            (b_lo[:], bo_lin_d.unsqueeze(0).to_broadcast([P, D])),
            (b_v[:], bv_d.unsqueeze(0).to_broadcast([P, D])),
            (b_ao[:], bo_d.unsqueeze(0).to_broadcast([P, D])),
            (b_log[:], blog_d.unsqueeze(0).to_broadcast([P, NL])),
            (w_shared[:, 0:FFN], w1_d[E]),
            (w_shared[:, FFN:WB1].rearrange("p (c n) -> p c n", c=FC), w2_d[E].rearrange("(c p) n -> p c n", p=P)),
            (w_shared[:, WB2:WCOLS], b2_d[E:E + 1, :].to_broadcast([P, D])),
        ]

        block = ctx.enter_context(nc.Block())

        @block.sync
        def _(sp):
            sp.dma_start(c_in, c_d).then_inc(c_loaded, 16)
            sp.dma_start(wmod, wmod_d).then_inc(rows_loaded, 16)
            sp.dma_start(rows_in[0:4, :], vec_d).then_inc(rows_loaded, 16)
            sp.dma_start(rows_in[4:6, :], bqk_d).then_inc(rows_loaded, 16)
            sp.dma_start(rows_in[6:NVEC, :], b1_d).then_inc(rows_loaded, 16)
            for dst, src in WEIGHTS:
                sp.dma_start(dst, src).then_inc(weights_loaded, 16)
            sp.wait_ge(mods_ready, 3)
            for n, row in enumerate((2, 4, 3, 5)):
                sp.dma_start(mod_dram[:, n, :], mods[:, row, :]).then_inc(mods_stored, 16)
            sp.wait_ge(mods_stored, 64)

            def spread_max(t, name, buf, half):
                taken(sp, t, name, wait_apart)
                for i in range(PARTS):
                    sp.dma_start(q_all[QK_ROWS + i:QK_ROWS + i + 1, buf, half * HALF:(half + 1) * HALF, :],
                                 max_parts[i * HALF:(i + 1) * HALF, half, :]).then_inc(max_spread[half], 16)

            def iteration(t, r):
                if active(t, LOAD):
                    wait_apart(sp, x_loaded, 16 * (t - LOAD))
                    sp.dma_start(batch(res, t), x_d[bass.ds(t, 1), :, :].rearrange("a (n p) d -> p (a n) d", p=P)
                                 ).then_inc(x_loaded, 16)
                if active(t, FRONT):
                    b = t - FRONT
                    wait_apart(sp, y_scaled, b)
                    wait_apart(sp, ga_loaded, 16 * b)
                    sp.dma_start(mod_ga[:], mod_rows(b, 0, 1)).then_inc(ga_loaded, 16)
                if active(t, NORM):
                    b = t - NORM
                    wait_apart(sp, h2_ready, b)
                    wait_apart(sp, modb_loaded, 16 * b)
                    sp.dma_start(mod_b[:], mod_rows(b, 1, 2)).then_inc(modb_loaded, 16)
                if active(t, BACK):
                    b = t - BACK
                    wait_apart(sp, x3_scaled, b)
                    wait_apart(sp, gb_loaded, 16 * b)
                    sp.dma_start(mod_gb[:], mod_rows(b, 3, 1)).then_inc(gb_loaded, 16)
                if active(t, SPREAD):
                    b, buf = t - SPREAD, (r - SPREAD) % NBUF
                    wait_apart(sp, qk_split, 3 * b + 3)
                    wait_apart(sp, qk_spread, 64 * b)
                    for n in range(2):
                        sp.dma_start(split_dram[n].rearrange("i p s -> p i s"), parts[:, n]).then_inc(split_stored, 16)
                    wait_apart(sp, split_stored, 32 * b + 32)
                    if isinstance(b, int) and b < NBUF:
                        sp.wait_ge(ones_ready, 1)
                    else:
                        wait_apart(sp, exp_full, HEADS * (b - NBUF + 1))
                    for i in range(PARTS):
                        sp.dma_start(q_all[i * PARTS * DH:(i + 1) * PARTS * DH, buf].rearrange("p h s -> p (h s)"),
                                     split_dram[0, i].rearrange("(d h) s -> d (h s)", d=DH).unsqueeze(0)
                                     .to_broadcast([PARTS, DH, HEADS * S])).then_inc(qk_spread, 16)
                    sp.dma_start(k_all[0:QK_ROWS, buf].rearrange("p h s -> p (h s)"),
                                 split_dram[1].rearrange("i (d h) s -> (i d) (h s)", d=DH).unsqueeze(0)
                                 .to_broadcast([PARTS, PARTS * DH, HEADS * S])).then_inc(qk_spread, 16)
                if active(t, EXP):
                    spread_max(t, "max_T_hi", (r - EXP) % NBUF, 1)
                if active(t, MAX):
                    spread_max(t, "max_T_lo", (r - MAX) % NBUF, 0)

            drive(sp, iteration)

            sp.wait_ge(exp_full, B * HEADS)
            for e in range(E):
                sp.dma_start(w_exp[:, e, 0:FFN], w1_d[e]).then_inc(experts_loaded, 16)
                sp.dma_start(w_exp[:, e, FFN:WB1].rearrange("p (c n) -> p c n", c=FC),
                             w2_d[e].rearrange("(c p) n -> p c n", p=P)).then_inc(experts_loaded, 16)
                sp.dma_start(w_exp[:, e, WB2:WCOLS], b2_d[e:e + 1, :].to_broadcast([P, D])
                             ).then_inc(experts_loaded, 16)

            def load_gb(g):
                if later(g):
                    wait_apart(sp, shared_added, g)
                sp.dma_start(gb2[:], gb_rows(g)).then_inc(gb2_loaded, 16)
                wait_apart(sp, gb2_loaded, 16 * g + 16)

            sp.wait_ge(route_ready, 1)
            load_gb(0)
            with sp.Fori(1, GROUPS) as g:
                load_gb(g)

            for n in range(4):
                sp.wait_ge(sorted_sem[n], 16 * GROUPS)

            sp.dma_start(gb_all[:].rearrange("p b d -> p (b d)"),
                         mod_dram[:, 3, :].unsqueeze(0).to_broadcast([P, B, D])).then_inc(gb_all_loaded, 16)

            def load_rows(k, n):
                k, n, j = moe_tile(k, n)
                if j is not None:
                    wait_apart(sp, meta_taken, j - NB + 1)
                    wait_apart(sp, tile_T_full, j - NB + 1)
                    wait_apart(sp, rows_in_loaded[n], 16 * k)
                    sp.dma_start(rows_buf[:, n, :], sorted_dram[bass.ds(j * P, P), :]).then_inc(rows_in_loaded[n], 16)

            drive_tiles(sp, load_rows)

            for n in range(NB):
                sp.wait_ge(moe_scattered[n], 16 * ((MAX_TILES + NB - 1 - n) // NB))
            tiles = TILES // FG
            for g in range(FG):
                sp.dma_start(fin[:, g * tiles:(g + 1) * tiles, :],
                             moe_dram[g * tiles * P:(g + 1) * tiles * P, :].rearrange("(n p) d -> p n d", p=P)
                             ).then_inc(fin_loaded[g], 16)
            sp.wait_ge(fin_stored, 16 * FG)

        @block.tensor
        def _(pe):
            pe.wait_ge(silu_step, 3)
            pe.wait_ge(ident_ready, 2)
            pe.transpose(bank[0][:, 0:B], c_silu, ident[0:B, 0:B]).then_inc(setup_full, 1)
            pe.wait_ge(rows_loaded, 64)
            pe.transpose(bank[1][:, 0:NVEC], rows_in[0:NVEC, :], ident[0:NVEC, 0:NVEC]).then_inc(setup_full, 1)
            pe.wait_ge(setup_taken, 1)
            for n in range(2):
                pe.matmul(bank[2 + n][0:B, 0:3 * D], c_T, wmod[:, 3 * D * n:3 * D * (n + 1)], start=True, stop=True
                          ).then_inc(setup_full, 1)
            pe.wait_ge(mod_step, 3)
            for n in range(2):
                pe.transpose(bank[0][:, n * B:(n + 1) * B], mods[:, n, :], ident[0:B, 0:B]).then_inc(setup_full, 1)
            pe.wait_ge(setup_taken, 3)
            pe.wait_ge(weights_loaded, 16 * len(WEIGHTS))

            def open_bank(t, name):
                k = JOB[name]
                wait(pe, work_free[k % 2], bank_uses(t, k))
                return work[k % 2]

            def close_bank(name, last):
                last.then_inc(work_full[JOB[name] % 2], 1)

            def transpose_tiles(t, name, tiles):
                w = open_bank(t, name)
                for n, src in enumerate(tiles):
                    last = pe.transpose(w[0:src.shape[1], n * P:(n + 1) * P], src, ident[:])
                close_bank(name, last)

            def scores_t(b, buf, h):
                if h == 0:
                    pe.wait_ge(max_spread[0], 48 * b + 48)
                if h == HALF:
                    pe.wait_ge(max_spread[1], 48 * b + 48)
                wait(pe, exp_done, b * HEADS + h - 1)
                for k in range(TPB):
                    last = pe.matmul(exp_bank[h % 2][:, k * S:(k + 1) * S], k_all[0:ALL_ROWS, buf, h, k * P:(k + 1) * P],
                                     q_all[0:ALL_ROWS, buf, h, :], start=True, stop=True)
                last.then_inc(exp_full, 1)

            def scores(b, buf, h):
                if h == 0:
                    pe.wait_ge(qk_spread, 64 * b + 64)
                wait(pe, max_done, b * HEADS + h - 1)
                for q in range(TPB):
                    last = pe.matmul(max_bank[h % 2][:, q * S:(q + 1) * S], q_all[0:QK_ROWS, buf, h, q * P:(q + 1) * P],
                                     k_all[0:QK_ROWS, buf, h, :], start=True, stop=True)
                last.then_inc(max_full, 1)

            def transpose_max(t, name, b, half):
                pe.wait_ge(max_split[half], 4 * b + 4)
                w = open_bank(t, name)[:].bitcast(BF16)
                for n in range(TPB):
                    last = pe.transpose(w[0:PARTS * HALF, n * P:(n + 1) * P],
                                        max_cols[:, half, n].rearrange("p i h -> p (i h)"), ident_half[:])
                close_bank(name, last)

            def probs_v(t, b, buf, h):
                if h == 0:
                    taken(pe, t - EXP + SPREAD, "v")
                if h % HALF == 0:
                    wait(pe, oT_ready, 2 * b - 1 + h // HALF)
                pe.wait_ge(exp_done, b * HEADS + h + 1)
                j, g = h % 4, h // 4 % 2
                for k in range(TPB):
                    last = pe.matmul(o_bank[h // HALF][32 * j:32 * j + 32, g * S:(g + 1) * S],
                                     va[:, buf, k, h * VW:h * VW + 32], probs[:, h % 2, k * S:(k + 1) * S],
                                     start=(k == 0), stop=(k == TPB - 1))
                last.then_inc(pv_done, 1)

            def front(t, slot):
                b = t - FRONT
                if slot == SLOT["x_T"]:
                    pe.wait_ge(norm_a, 2 * b + 2)
                    transpose_tiles(t, "x_T", [xn[:, n, :] for n in range(TPB)])
                if slot == SLOT["qv"]:
                    w = open_bank(t, "qv")
                    taken(pe, t, "x_T")
                    for n in range(TPB):
                        last = pe.matmul(w[:, 2 * D * n:2 * D * (n + 1)], hT[:, n * P:(n + 1) * P], w_qv[:],
                                         start=True, stop=True)
                    close_bank("qv", last)
                if slot == SLOT["k"]:
                    w = open_bank(t, "k")
                    close_bank("k", pe.matmul(w[:, 0:S], w_k[:], hT[:], start=True, stop=True))
                if slot == SLOT["qk_T"]:
                    w = open_bank(t, "qk_T")
                    taken(pe, t, "qv")
                    taken(pe, t, "k")
                    for n in range(TPB):
                        pe.transpose(w[:, n * P:(n + 1) * P], q_exp[:, n, :], ident[:])
                    for n in range(TPB):
                        last = pe.transpose(w[:, S + n * P:S + (n + 1) * P], k_exp[:, n * P:(n + 1) * P], ident[:])
                    close_bank("qk_T", last)
                if slot == SLOT["lin_ctx"]:
                    w = open_bank(t, "lin_ctx")
                    taken(pe, t, "qk_T")
                    for n in range(TPB):
                        last = pe.matmul(w[:, 0:D], v_lin[:, n, :], qk_T[:, 1, n * P:(n + 1) * P],
                                         start=(n == 0), stop=(n == TPB - 1))
                    close_bank("lin_ctx", last)
                if slot == SLOT["lin_m"]:
                    w = open_bank(t, "lin_m")
                    taken(pe, t, "lin_ctx")
                    close_bank("lin_m", pe.matmul(w[:, 0:D], ctx_lin[:], w_lo[:], start=True, stop=True))
                if slot == SLOT["lin_out"]:
                    w = open_bank(t, "lin_out")
                    taken(pe, t, "lin_m")
                    for n in range(TPB):
                        last = pe.matmul(w[:, n * D:(n + 1) * D], qk_T[:, 0, n * P:(n + 1) * P], m_lin[:],
                                         start=True, stop=True)
                    close_bank("lin_out", last)

            def norm(t, slot):
                b = t - NORM
                if slot == SLOT["h_T"]:
                    pe.wait_ge(norm_c, 2 * b + 2)
                    transpose_tiles(t, "h_T", [xc[:, n, :] for n in range(TPB)])
                if slot == SLOT["qk"]:
                    w = open_bank(t, "qk")
                    taken(pe, t, "h_T")
                    for n in range(2):
                        last = pe.matmul(w[:, n * S:(n + 1) * S], w_qkv[:, n * D:(n + 1) * D], xnT[:],
                                         start=True, stop=True)
                    close_bank("qk", last)

            def spread(t, slot):
                if slot == SLOT["v"]:
                    w = open_bank(t, "v")
                    for n in range(TPB):
                        last = pe.matmul(w[:, n * D:(n + 1) * D], xnT[:, n * P:(n + 1) * P], w_qkv[:, 2 * D:3 * D],
                                         start=True, stop=True)
                    close_bank("v", last)

            def back(t, slot):
                b = t - BACK
                if slot in (SLOT["ctx_rows0"], SLOT["ctx_rows1"]):
                    pe.wait_ge(oT_ready, 2 * b + 2)
                    n = slot - SLOT["ctx_rows0"]
                    transpose_tiles(t, f"ctx_rows{n}", [oT[:, g, n * P:(n + 1) * P] for g in range(HEADS // 4)])
                if slot == SLOT["ctx_T"]:
                    taken(pe, t, "ctx_rows0")
                    taken(pe, t, "ctx_rows1")
                    transpose_tiles(t, "ctx_T", [o_rows[:, n, :] for n in range(TPB)])
                if slot == SLOT["att_out"]:
                    w = open_bank(t, "att_out")
                    taken(pe, t, "ctx_T")
                    for n in range(TPB):
                        last = pe.matmul(w[:, n * D:(n + 1) * D], o_T[:, n * P:(n + 1) * P], w_ao[:],
                                         start=True, stop=True)
                    close_bank("att_out", last)
                if slot == SLOT["moe_in_T"]:
                    pe.wait_ge(norm_d, 2 * b + 2)
                    transpose_tiles(t, "moe_in_T", [xm[:, n, :] for n in range(TPB)])
                if slot == SLOT["logits"]:
                    w = open_bank(t, "logits")
                    taken(pe, t, "moe_in_T")
                    for n in range(TPB):
                        last = pe.matmul(w[:, n * NL:(n + 1) * NL], xmT[:, n * P:(n + 1) * P], w_log[:],
                                         start=True, stop=True)
                    close_bank("logits", last)

            def iteration(t, r):
                for slot in range(HEADS):
                    if slot == 0 and active(t, BACK):
                        probs_v(t, t - BACK, (r - BACK) % NBUF, HEADS - 1)
                    if active(t, EXP):
                        scores_t(t - EXP, (r - EXP) % NBUF, slot)
                    if active(t, MAX):
                        scores(t - MAX, (r - MAX) % NBUF, slot)
                    if active(t, FRONT):
                        front(t, slot)
                    if active(t, NORM):
                        norm(t, slot)
                    if active(t, SPREAD):
                        spread(t, slot)
                    if slot == SLOT["max_T_hi"] and active(t, EXP):
                        transpose_max(t, "max_T_hi", t - EXP, 1)
                    if slot == SLOT["max_T_lo"] and active(t, MAX):
                        transpose_max(t, "max_T_lo", t - MAX, 0)
                    if active(t, BACK):
                        back(t, slot)
                    if slot > 0 and active(t, EXP):
                        probs_v(t, t - EXP, (r - EXP) % NBUF, slot - 1)

            drive(pe, iteration)

            pe.wait_ge(route_step, 8)
            pe.wait_ge(consts_ready, 5)
            pe.matmul(bank[2][:, 0:TILES * E], upper[:], onehot[:], start=True, stop=True
                      ).then_inc(counts_full, 1)
            pe.matmul(bank[3][:, 0:TILES * E], ones[:], onehot[:], start=True, stop=True
                      ).then_inc(counts_full, 1)

            for n in range(2):
                pe.wait_ge(work_free[n], bank_uses(PIPE, n))

            def shared_up(k, n, cs):
                g = 2 * k + n
                for c in cs:
                    if later(g) or c >= 2:
                        pe.wait_ge(gelu_done, g * FC + c - 1)
                    pe.matmul(bank[4 + c % 2][:], w_shared[:, c * P:(c + 1) * P], moe_in_T[:, bass.ds(g * GT * P, GT * P)],
                              start=True, stop=True).then_inc(up_full, 1)

            def shared_down(k, n):
                g = 2 * k + n
                pe.wait_ge(gelu_done, g * FC + FC)
                if later(k):
                    pe.wait_ge(down_taken, g - 1)
                for m in range(GT):
                    for c in range(FC):
                        last = pe.matmul(bank[6 + n][:, m * D:(m + 1) * D], hid[:, n, c, m * P:(m + 1) * P],
                                         w_shared[:, FFN + c * P:FFN + (c + 1) * P], start=(c == 0), stop=(c == FC - 1))
                last.then_inc(down_full, 1)

            def shared_step_pair(k, n, k_before, n_before):
                shared_up(k, n, range(2))
                shared_down(k_before, n_before)
                shared_up(k, n, range(2, FC))

            pe.wait_ge(route_ready, 1)
            shared_up(0, 0, range(FC))
            shared_step_pair(0, 1, 0, 0)
            shared_step_pair(1, 0, 0, 1)
            with pe.Fori(1, GROUPS // 2 - 1) as k:
                shared_step_pair(k, 1, k, 0)
                shared_step_pair(k + 1, 0, k, 1)
            shared_step_pair(GROUPS // 2 - 1, 1, GROUPS // 2 - 1, 0)
            shared_down(GROUPS // 2 - 1, 1)
            pe.wait_ge(down_taken, GROUPS)

            def moe_transpose(k, n):
                k, n, j = moe_tile(k, n)
                if j is not None:
                    pe.wait_ge(rows_in_loaded[n], 16 * k + 16)
                    wait(pe, tile_T_ready, j - 1)
                    pe.transpose(bank[n % 2][:, 0:P], rows_buf[:, n, 0:D], ident[:]).then_inc(tile_T_full, 1)

            def moe_up(k, n):
                k, n, j = moe_tile(k, n)
                if j is not None:
                    pe.wait_ge(tile_T_ready, j + 1)
                    pe.wait_ge(stage_ready, j + 1)
                    wait(pe, moe_gelu_done, (j - NB + 1) * FC)
                    for c in range(FC):
                        last = pe.matmul(bank[2 + n][:, c * P:(c + 1) * P], staged[:, n, c * P:(c + 1) * P],
                                         tile_T[:, n, :], start=True, stop=True)
                    last.then_inc(moe_up_full, 1)

            def moe_down(k, n):
                k, n, j = moe_tile(k, n)
                if j is not None:
                    pe.wait_ge(moe_gelu_done, j * FC + FC)
                    wait(pe, moe_y_taken, j - 1)
                    for c in range(FC):
                        last = pe.matmul(bank[6 + n % 2][:, 0:D], hid_moe[:, n, c, :],
                                         staged[:, n, FFN + c * P:FFN + (c + 1) * P], start=(c == 0), stop=(c == FC - 1))
                    last.then_inc(moe_y_full, 1)

            def moe_step(k, n):
                moe_up(k, n)
                moe_transpose(k, n + 2)
                moe_down(k, n - 2)

            moe_transpose(0, 0)
            moe_transpose(0, 1)
            drive_tiles(pe, moe_step)

        @block.scalar
        def _(act):
            act.wait_ge(c_loaded, 16)
            act.activation(c_exp, c_in, ACT.Exp, scale=-1.0).then_inc(silu_exp, 1)

            def iteration(t, r):
                for slot in range(HEADS):
                    if active(t, BACK) and slot == 0:
                        act.wait_ge(pv_done, (t - BACK) * HEADS + HEADS)
                        act.activation(oT[:, 2:4, :].rearrange("p g s -> p (g s)"), o_bank[1][:], ACT.Copy
                                       ).then_inc(oT_ready, 1)
                    if active(t, EXP):
                        b = t - EXP
                        act.wait_ge(exp_full, b * HEADS + slot + 1)
                        wait(act, pv_done, b * HEADS + slot - 1)
                        act.activation(probs[:, slot % 2, :], exp_bank[slot % 2][:], ACT.Exp, scale=ATT_SCALE
                                       ).then_inc(exp_done, 1)
                    if active(t, EXP) and slot == HALF + 1:
                        act.wait_ge(pv_done, (t - EXP) * HEADS + HALF)
                        if active(t, BACK):
                            full(act, t, "ctx_rows1")
                        act.activation(oT[:, 0:2, :].rearrange("p g s -> p (g s)"), o_bank[0][:], ACT.Copy
                                       ).then_inc(oT_ready, 1)
                    if active(t, FRONT):
                        front(t, slot)
                    if active(t, NORM):
                        norm(t, slot)
                    if active(t, EXP) and slot == SLOT["max_T_hi"]:
                        take_max(t, "max_T_hi", t - EXP, 1)
                    if active(t, MAX) and slot == SLOT["max_T_lo"]:
                        take_max(t, "max_T_lo", t - MAX, 0)
                    if active(t, BACK):
                        back(t, slot)

            def free(ins, name):
                ins.then_inc(work_free[JOB[name] % 2], 1)

            def bank_of(name):
                return work[JOB[name] % 2]

            def take_max(t, name, b, half):
                full(act, t, name)
                wait(act, max_spread[half], 48 * b)
                free(act.activation(max_parts[:, half, :], bank_of(name)[:].bitcast(BF16)[0:PARTS * HALF, 0:S], ACT.Copy),
                     name)

            def front(t, slot):
                b = t - FRONT
                if slot == SLOT["x_T"]:
                    if isinstance(t, int) and b == 0:
                        act.wait_ge(setup_taken, 3)
                    full(act, t, "x_T")
                    free(act.activation(hT[:], bank_of("x_T")[:, 0:S], ACT.Identity, bias=modT[:, 0, bass.ds(b, 1)],
                                        scale=modT[:, 1, bass.ds(b, 1)]), "x_T")
                if slot == SLOT["qv"] + 1:
                    act.wait_ge(q_max_ready, b + 1)
                    w = bank_of("qv")[:].rearrange("p (n two d) -> p n two d", n=TPB, two=2)
                    for n in range(TPB):
                        act.activation(q_exp[:, n, :], w[:, n, 0, :], ACT.Exp, bias=q_neg[:, n:n + 1],
                                       accum_out=q_sum[:, n:n + 1]).then_inc(q_exp_done, 1)
                    free(act.activation(v_lin[:], w[:, :, 1, :], ACT.Copy), "qv")
                if slot == SLOT["k"] + 1:
                    act.wait_ge(k_max_ready, b + 1)
                    free(act.activation(k_exp[:], bank_of("k")[:, 0:S], ACT.Exp, bias=k_neg[:], accum_out=k_sum[:]), "k")
                if slot == SLOT["qk_T"]:
                    full(act, t, "qk_T")
                    free(act.activation(qk_T[:].rearrange("p n s -> p (n s)"), bank_of("qk_T")[:], ACT.Copy), "qk_T")
                if slot == SLOT["lin_ctx"]:
                    full(act, t, "lin_ctx")
                    free(act.activation(ctx_lin[:], bank_of("lin_ctx")[:, 0:D], ACT.Copy), "lin_ctx")

            def norm(t, slot):
                b = t - NORM
                if slot == SLOT["h_T"]:
                    full(act, t, "h_T")
                    free(act.activation(xnT[:], bank_of("h_T")[:, 0:S], ACT.Identity, bias=vec(LN1B), scale=vec(LN1G)),
                         "h_T")
                if slot == SLOT["qk"]:
                    full(act, t, "qk")
                    wait(act, split_stored, 32 * b)
                    wait(act, qk_split, 3 * b)
                    for out in (parts[:, :, 0, :], qkf[:]):
                        for n in range(2):
                            last = act.activation(out[:, n, :], bank_of("qk")[:, n * S:(n + 1) * S], ACT.Identity,
                                                  bias=vec(BQ + n))
                    free(last, "qk")
                if slot == SLOT["qk"] + 2:
                    act.wait_ge(qk_split, 3 * b + 1)
                    act.activation(parts[:, :, 1, :], qkf[:], ACT.Copy).then_inc(qk_split, 1)

            def back(t, slot):
                b = t - BACK
                if slot == SLOT["ctx_T"]:
                    full(act, t, "ctx_T")
                    free(act.activation(o_T[:], bank_of("ctx_T")[:, 0:S], ACT.Copy), "ctx_T")
                if slot == SLOT["moe_in_T"]:
                    full(act, t, "moe_in_T")
                    for out in (xmT[:], moe_in_T[:, bass.ds(b * S, S)]):
                        last = act.activation(out, bank_of("moe_in_T")[:, 0:S], ACT.Identity, bias=vec(LN2B),
                                              scale=vec(LN2G))
                    free(last, "moe_in_T")

            drive(act, iteration)

            act.wait_ge(route_step, 4)
            act.activation(shifted[:].rearrange("p t n -> p (t n)"), shifted[:].rearrange("p t n -> p (t n)"), ACT.Exp
                           ).then_inc(route_exp, 1)

            def shared_gelu(k, n):
                g = 2 * k + n
                if later(k):
                    act.wait_ge(down_full, g - 1)
                for c in range(FC):
                    act.wait_ge(up_full, g * FC + c + 1)
                    act.activation(hid[:, n, c, :], bank[4 + c % 2][:], ACT.Gelu, bias=vec(B1 + E * FC + c)
                                   ).then_inc(gelu_done, 1)

            drive_groups(act, shared_gelu)

            def moe_turn(k, n):
                k, n, j = moe_tile(k, n)
                if j is not None:
                    act.wait_ge(tile_T_full, j + 1)
                    wait(act, moe_up_full, j - NB + 1)
                    act.activation(tile_T[:, n, :], bank[n % 2][:, 0:P], ACT.Identity, bias=vec(LN2B), scale=vec(LN2G)
                                   ).then_inc(tile_T_ready, 1)

            def moe_gelu(k, n):
                k, n, j = moe_tile(k, n)
                if j is not None:
                    act.wait_ge(moe_up_full, j + 1)
                    wait(act, moe_y_full, j - NB + 1)
                    for c in range(FC):
                        act.activation(hid_moe[:, n, c, :], bank[2 + n][:, c * P:(c + 1) * P], ACT.Gelu,
                                       bias=staged[:, n, WB1 + c:WB1 + c + 1]).then_inc(moe_gelu_done, 1)

            def moe_step(k, n):
                moe_gelu(k, n)
                moe_turn(k, n + 2)

            moe_turn(0, 0)
            moe_turn(0, 1)
            drive_tiles(act, moe_step)

            tiles = TILES // FG
            for g in range(FG):
                act.wait_ge(fin_step, 2 * g + 2)
                act.dma_start(out_d[g * B // FG:(g + 1) * B // FG].rearrange("b (n p) d -> p (b n) d", p=P),
                              fin[:, g * tiles:(g + 1) * tiles, :]).then_inc(fin_stored, 16)


        @block.vector
        def _(dve):
            dve.memset(half_neg[:], -0.5).then_inc(half_ready, 1)
            dve.wait_ge(ident_ready, 2)
            dve.tensor_copy(ident_half[:], ident[:]).then_inc(half_ready, 1)
            dve.memset(va[:], 1.0).then_inc(half_ready, 1)
            dve.wait_ge(silu_exp, 1)
            dve.tensor_scalar(c_exp, c_exp, 1.0, None, ALU.add).then_inc(silu_step, 1)
            dve.wait_ge(silu_step, 1)
            dve.reciprocal(c_exp, c_exp).then_inc(silu_step, 1)
            dve.wait_ge(silu_step, 2)
            dve.tensor_tensor(c_silu, c_in, c_exp, ALU.mult).then_inc(silu_step, 1)
            dve.wait_ge(setup_full, 1)
            dve.tensor_copy(c_T, bank[0][:, 0:B]).then_inc(setup_taken, 1)
            dve.wait_ge(setup_full, 2)
            dve.tensor_copy(vecs_T[:, 0:NVEC], bank[1][:, 0:NVEC]).then_inc(setup_taken, 1)
            dve.wait_ge(setup_full, 4)
            for n in range(2):
                dve.tensor_copy(mods[:, 3 * n:3 * n + 3, :], bank[2 + n][0:B, 0:3 * D].rearrange("b (n d) -> b n d", d=D)
                                ).then_inc(mod_step, 1)
            dve.wait_ge(mod_step, 2)
            dve.tensor_scalar(mods[:, 1, :], mods[:, 1, :], 1.0, None, ALU.add).then_inc(mod_step, 1)
            dve.tensor_scalar(mods[:, 4, :], mods[:, 4, :], 1.0, None, ALU.add).then_inc(mods_ready, 1)
            steps = 3
            for n, row in enumerate((2, 5)):
                g = mods[:, row, :]
                if n:
                    dve.wait_ge(mods_ready, 2)
                dve.tensor_scalar(gsign, g, 0.0, 2.0, ALU.is_ge, ALU.mult).then_inc(mod_step, 1)
                dve.tensor_scalar(gabs, g, -1.0, 0.25, ALU.mult, ALU.max).then_inc(mod_step, 1)
                dve.wait_ge(mod_step, steps + 2)
                dve.tensor_tensor(gabs, gabs, g, ALU.max).then_inc(mod_step, 1)
                dve.wait_ge(mod_step, steps + 3)
                dve.scalar_tensor_tensor(g, gsign, -1.0, gabs, ALU.add, ALU.mult).then_inc(mods_ready, 1)
                steps += 3
            dve.memset(slots0[:], 0.0).then_inc(slots_cleared, 1)
            dve.wait_ge(setup_full, 6)
            dve.tensor_copy(modT[:].rearrange("p n b -> p (n b)"), bank[0][:, 0:2 * B]).then_inc(setup_taken, 1)
            dve.wait_ge(weights_loaded, 16 * len(WEIGHTS))

            def free(ins, name):
                ins.then_inc(work_free[JOB[name] % 2], 1)

            def bank_of(name):
                return work[JOB[name] % 2]

            def moments(src, st, mv, b, stats, mean):
                for n in range(TPB):
                    dve.bn_stats(st[:, n, :], src(n)).then_inc(stats, 1)
                wait_apart(dve, stats, 2 * b + 2)
                for n in range(TPB):
                    dve.bn_aggr(mv[:, n, :], st[:, n, :]).then_inc(mean, 1)

            def normalise(dst, src, mv, rs, b, rstd, norm):
                dve.wait_ge(rstd, 2 * b + 2)
                for n in range(TPB):
                    dve.tensor_scalar(dst[:, n:n + 1, :], src(n), mv[:, n, 0:1], rs[:, n:n + 1], ALU.subtract, ALU.mult
                                      ).then_inc(norm, 1)

            def split_max(b, half):
                left, done = neg_max[:, half], max_split[half]
                for i in range(2):
                    dve.tensor_copy(max_cols[:, half, :, i, :], left).then_inc(done, 1)
                    dve.wait_ge(done, 4 * b + 2 * i + 1)
                    out = left if i == 0 else max_cols[:, half, :, 2, :]
                    dve.tensor_tensor(out, left, max_cols[:, half, :, i, :], ALU.subtract).then_inc(done, 1)
                    if i == 0:
                        dve.wait_ge(done, 4 * b + 2)

            def iteration(t, r):
                for slot in range(HEADS):
                    if active(t, MAX):
                        b = t - MAX
                        half = slot // HALF
                        if slot % HALF == 0:
                            wait(dve, max_split[half], 4 * b)
                        dve.wait_ge(max_full, b * HEADS + slot + 1)
                        dve.tensor_reduce(neg_max[:, slot // HALF, :, slot % HALF],
                                          max_bank[slot % 2][:].rearrange("p (q k) -> p q k", q=TPB), AX.X, ALU.max,
                                          negate=True).then_inc(max_done, 1)
                        if slot == HALF - 1 and active(t - 1, MAX):
                            full(dve, t - 1, "max_T_lo")
                        if slot == HEADS - 1 and active(t, EXP):
                            full(dve, t, "max_T_hi")
                        if slot % HALF == HALF - 1:
                            dve.wait_ge(max_done, b * HEADS + slot + 1)
                            split_max(b, half)
                    if active(t, FRONT):
                        front(t, slot)
                    if active(t, NORM):
                        norm(t, slot)
                    if active(t, SPREAD):
                        spread(t, slot, (r - SPREAD) % NBUF)
                    if active(t, BACK):
                        back(t, slot)
                    if active(t, LOAD) and slot == 11:
                        wait_apart(dve, x_loaded, 16 * (t - LOAD) + 16)
                        moments(lambda n: tile(res, t, n), st_a, mv_a, t, stats_a, mean_a)
                    if active(t, LOAD) and slot == 14:
                        if active(t, FRONT):
                            full(dve, t, "x_T")
                        normalise(xn, lambda n: tile(res, t, n), mv_a, rs_a, t, rstd_a, norm_a)

            def front(t, slot):
                b = t - FRONT
                if slot == SLOT["qv"]:
                    full(dve, t, "qv")
                    w = bank_of("qv")[:].rearrange("p (n two d) -> p n two d", n=TPB, two=2)
                    dve.tensor_reduce(q_neg[:], w[:, :, 0, :], AX.X, ALU.max, negate=True).then_inc(q_max_ready, 1)
                if slot == SLOT["k"]:
                    full(dve, t, "k")
                    dve.tensor_reduce(k_neg[:], bank_of("k")[:, 0:S], AX.X, ALU.max, negate=True
                                      ).then_inc(k_max_ready, 1)
                if slot == SLOT["lin_m"]:
                    taken(dve, t, "k")
                    dve.reciprocal(k_rec[:], k_sum[:]).then_inc(recips, 1)
                    dve.reciprocal(q_rec[:], q_sum[:]).then_inc(recips, 1)
                    dve.wait_ge(recips, 2 * b + 2)
                    full(dve, t, "lin_m")
                    free(dve.tensor_scalar(m_lin[:], bank_of("lin_m")[:, 0:D], k_rec[:], LIN_SCALE, ALU.mult, ALU.mult),
                         "lin_m")
                if slot == SLOT["lin_out"]:
                    full(dve, t, "lin_out")
                    for n in range(TPB):
                        last = dve.scalar_tensor_tensor(y_lin[:, n, :], bank_of("lin_out")[:, n * D:(n + 1) * D],
                                                        q_rec[:, n:n + 1], b_lo[:], ALU.mult, ALU.add)
                    free(last, "lin_out")

            def norm(t, slot):
                b = t - NORM
                if slot == 1:
                    wait_apart(dve, x1_ready, b + 1)
                    moments(lambda n: tile(res, b, n), st_b, mv_b, b, stats_b, mean_b)
                if slot == 3:
                    normalise(h_norm, lambda n: tile(res, b, n), mv_b, rs_b, b, rstd_b, norm_b)
                if slot == 7:
                    wait_apart(dve, h2_ready, b + 1)
                    moments(lambda n: tile(keep, b, n), st_c, mv_c, b, stats_c, mean_c)
                if slot == 9:
                    normalise(xc, lambda n: tile(keep, b, n), mv_c, rs_c, b, rstd_c, norm_c)

            def spread(t, slot, buf):
                b = t - SPREAD
                if slot == SLOT["v"]:
                    full(dve, t, "v")
                    wait(dve, pv_done, (b - NBUF + 1) * HEADS)
                    free(dve.tensor_tensor(
                        va[:, buf, :, 0:HEADS * VW].rearrange("p n (h w) -> p n h w", w=VW)[:, :, :, 0:DH],
                        bank_of("v")[:, 0:TPB * D].rearrange("p (n h d) -> p n h d", n=TPB, d=DH),
                        b_v[:].rearrange("p (h d) -> p h d", d=DH).unsqueeze(1).to_broadcast([P, TPB, HEADS, DH]),
                        ALU.add), "v")

            def back(t, slot):
                b = t - BACK
                if slot in (SLOT["ctx_rows0"], SLOT["ctx_rows1"]):
                    n = slot - SLOT["ctx_rows0"]
                    name = f"ctx_rows{n}"
                    full(dve, t, name)
                    w = bank_of(name)[:].rearrange("p (h c) -> p h c", c=32)
                    dve.reciprocal(o_rec[:, n, :], w[:, :, DH]).then_inc(o_rec_ready, 1)
                    dve.wait_ge(o_rec_ready, 2 * b + n + 1)
                    free(dve.tensor_tensor(o_rows[:, n, :].rearrange("p (h d) -> p h d", d=DH), w[:, :, 0:DH],
                                           o_rec[:, n, :].unsqueeze(2).to_broadcast([P, HEADS, DH]), ALU.mult), name)
                if slot == SLOT["att_out"]:
                    full(dve, t, "att_out")
                    dve.wait_ge(h2b_ready, b + 1)
                    wait(dve, x3_scaled, b)
                    free(dve.tensor_tensor(x3[:], bank_of("att_out")[:, 0:TPB * D].rearrange("p (n d) -> p n d", d=D),
                                           h2b[:], ALU.add), "att_out")
                if slot == SLOT["att_out"] + 1:
                    taken(dve, t, "att_out")
                    moments(lambda n: x3[:, n:n + 1, :], st_d, mv_d, b, stats_d, mean_d)
                if slot == SLOT["att_out"] + 3:
                    wait(dve, kept, b)
                    normalise(xm, lambda n: x3[:, n:n + 1, :], mv_d, rs_d, b, rstd_d, norm_d)
                if slot == SLOT["logits"]:
                    full(dve, t, "logits")
                    free(dve.tensor_tensor(batch(logit, b), bank_of("logits")[:, 0:TPB * NL]
                                           .rearrange("p (n d) -> p n d", d=NL),
                                           b_log[:].unsqueeze(1).to_broadcast([P, TPB, NL]), ALU.add), "logits")

            drive(dve, iteration)

            count = [0]

            def step(ins):
                ins.then_inc(route_step, 1)
                count[0] += 1
                dve.wait_ge(route_step, count[0])

            def per_tile(x, n):
                return x.unsqueeze(2).to_broadcast([P, TILES, n])

            def tiles_experts(x):
                return x.rearrange("p (t e) -> p t e", e=E)

            for n in range(2):
                dve.wait_ge(work_free[n], bank_uses(PIPE, n))
            dve.wait_ge(res_ready, B)
            dve.wait_ge(kept, B)
            dve.memset(ones[:], 1.0).then_inc(ones_again, 1)
            gates = logit[:, :, 0:E]
            step(dve.tensor_reduce(lmax[:, 0, :], gates, AX.X, ALU.max))
            step(dve.tensor_reduce(lmax[:, 1, :], logit[:, :, E:NL], AX.X, ALU.max))
            step(dve.tensor_tensor(shifted[:, :, 0:E], gates, per_tile(lmax[:, 0, :], E), ALU.subtract))
            step(dve.tensor_tensor(shifted[:, :, E:NL], logit[:, :, E:NL], per_tile(lmax[:, 1, :], 2), ALU.subtract))
            key, a, incl, tot = (tiles_experts(route_buf(n, TILES * E)) for n in range(4))
            onehot3 = tiles_experts(onehot[:])
            step(dve.tensor_tensor(key, gates, per_tile(lmax[:, 0, :], E), ALU.is_equal))
            step(dve.tensor_tensor(key, key, order[:].unsqueeze(1).to_broadcast([P, TILES, E]), ALU.mult))
            step(dve.tensor_reduce(w_moe[:], key, AX.X, ALU.max))
            step(dve.tensor_tensor(onehot3, key, per_tile(w_moe[:], E), ALU.is_equal))
            dve.wait_ge(counts_full, 2)
            step(dve.tensor_copy(tot, tiles_experts(bank[3][:])))
            incl = route_buf(2, TILES * E).rearrange("p (e t) -> p e t", t=TILES)
            zero = route_buf(4, TILES)
            step(dve.memset(zero, 0.0))
            for e in range(E):
                dve.tensor_tensor_scan(incl[:, e, :], tot[:, :, e], zero, 0.0, ALU.add, ALU.add).then_inc(route_step, 1)
            count[0] += E
            dve.wait_ge(route_step, count[0])
            tiles_e, ends, base = small[:, 0, :], small[:, 1, :], small[:, 2, :]
            cmp = route_buf(5, TILES * E).rearrange("p (e t) -> p e t", t=TILES)
            step(dve.tensor_tensor(cmp, tile_first[:].unsqueeze(1).to_broadcast([P, E, TILES]),
                                   incl[:, :, TILES - 1:TILES].to_broadcast([P, E, TILES]), ALU.is_lt))
            step(dve.tensor_reduce(tiles_e, cmp, AX.X, ALU.add))
            step(dve.tensor_tensor_scan(ends, tiles_e, zero[:, 0:E], 0.0, ALU.add, ALU.add))
            step(dve.tensor_tensor(base, ends, tiles_e, ALU.subtract))
            step(dve.tensor_scalar(base, base, float(P), None, ALU.mult))
            step(dve.tensor_tensor(a, incl.rearrange("p e t -> p t e"), tot, ALU.subtract))
            step(dve.tensor_tensor(a, a, tiles_experts(bank[2][:]), ALU.add))
            step(dve.tensor_tensor(a, a, base.unsqueeze(1).to_broadcast([P, TILES, E]), ALU.add))
            step(dve.tensor_tensor(a, a, onehot3, ALU.mult))
            step(dve.tensor_reduce(lmax[:, 0, :], a, AX.X, ALU.add))
            step(dve.tensor_copy(slot_u[:], lmax[:, 0, :]))
            cmp2 = hid_flat[:, 0:MAX_TILES * (E - 1)].rearrange("p (t e) -> p t e", e=E - 1)
            step(dve.tensor_tensor(cmp2, ends[:, 0:E - 1].unsqueeze(1).to_broadcast([P, MAX_TILES, E - 1]),
                                   tile_no[:].unsqueeze(2).to_broadcast([P, MAX_TILES, E - 1]), ALU.is_le))
            exp_f = route_buf(4, MAX_TILES)
            step(dve.tensor_reduce(exp_f, cmp2, AX.X, ALU.add))
            step(dve.tensor_copy(expert_u[:], exp_f))
            dve.wait_ge(route_exp, 1)
            step(dve.tensor_reduce(w_moe[:], shifted[:, :, 0:E], AX.X, ALU.add))
            step(dve.tensor_reduce(w_rm[:], shifted[:, :, E:NL], AX.X, ALU.add))
            step(dve.reciprocal(w_moe[:], w_moe[:]))
            step(dve.reciprocal(w_rm[:], w_rm[:]))
            step(dve.tensor_tensor(w_moe[:], w_moe[:], w_rm[:], ALU.mult))
            step(dve.tensor_tensor(token_meta[:, :, 1], w_moe[:], shifted[:, :, E], ALU.mult))
            dve.tensor_tensor(w_rm[:], w_rm[:], shifted[:, :, E + 1], ALU.mult).then_inc(route_ready, 1)
            dve.wait_ge(route_ready, 1)

            dve.wait_ge(experts_loaded, 16 * 3 * E)
            b1_all = vecs_T[:, B1:B1 + E * FC].rearrange("p (e c) -> p e c", c=FC)
            dve.tensor_copy(w_exp[:, :, WB1:WB2], b1_all).then_inc(weight_step, 1)

            def shared_out(k, n):
                g = 2 * k + n
                wn = w_rm[:, bass.ds(g * GT, GT)].unsqueeze(2).to_broadcast([P, GT, D])
                dve.wait_ge(down_full, g + 1)
                wait(dve, shared_added, g)
                dve.tensor_tensor(y_shared[:], bank[6 + n][:].rearrange("p (m d) -> p m d", d=D),
                                  over(w_shared[:, WB2:WCOLS], GT), ALU.add).then_inc(down_taken, 1)
                dve.wait_ge(down_taken, g + 1)
                dve.tensor_tensor(y_shared[:], y_shared[:], wn, ALU.mult).then_inc(shared_step, 1)
                dve.wait_ge(shared_step, 2 * g + 1)
                dve.wait_ge(gb2_loaded, 16 * g + 16)
                y4 = y_shared[:].rearrange("p (b n) d -> p b n d", n=TPB)
                dve.tensor_tensor(y4, y4, gb2[:].unsqueeze(2).to_broadcast([P, GB, TPB, D]), ALU.mult
                                  ).then_inc(shared_step, 1)
                dve.wait_ge(shared_step, 2 * g + 2)
                rows = res[:, bass.ds(g * GT, GT), :]
                dve.tensor_tensor(rows, rows, y_shared[:], ALU.add).then_inc(shared_added, 1)

            drive_groups(dve, shared_out)

            dve.wait_ge(weight_step, 1)

            def stage_weights(k, n):
                k, n, j = moe_tile(k, n)
                if j is not None:
                    wait(dve, moe_y_taken, j - NB + 1)
                    expert = dve.value_load(expert_u[0:1, bass.ds(j, 1)], min_val=0, max_val=E - 1)
                    dve.tensor_copy(staged[:, n, :], w_exp[:, bass.ds(expert, 1), :].rearrange("p e w -> p (e w)")
                                    ).then_inc(stage_ready, 1)

            def moe_out(k, n):
                k, n, j = moe_tile(k, n)
                if j is not None:
                    dve.wait_ge(moe_y_full, j + 1)
                    dve.wait_ge(stage_ready, j + 1)
                    wait(dve, pool_step, 2 * (j - NB + 1))
                    dve.tensor_tensor(y_moe[:, n, :], bank[6 + n % 2][:, 0:D], staged[:, n, WB2:WCOLS], ALU.add
                                      ).then_inc(moe_y_taken, 1)

            def moe_step(k, n):
                moe_out(k, n - 2)
                stage_weights(k, n + 2)

            dve.wait_ge(down_full, GROUPS)
            for n in range(2):
                stage_weights(0, n)
            drive_tiles(dve, moe_step)

            tiles = TILES // FG
            dve.wait_ge(gb_all_loaded, 16)
            for g in range(FG):
                dve.wait_ge(fin_loaded[g], 16)
                rows = fin[:, g * tiles:(g + 1) * tiles, :]
                f4 = rows.rearrange("p (b n) d -> p b n d", n=TPB)
                dve.tensor_tensor(f4, f4, gb_all[:, g * B // FG:(g + 1) * B // FG, :].unsqueeze(2)
                                  .to_broadcast([P, B // FG, TPB, D]), ALU.mult).then_inc(fin_step, 1)
                dve.wait_ge(fin_step, 2 * g + 1)
                dve.tensor_tensor(rows, rows, res[:, g * tiles:(g + 1) * tiles, :], ALU.add).then_inc(fin_step, 1)

        @block.gpsimd
        def _(pool):
            pool.memset(ident[:], 0.0).then_inc(ident_ready, 1)
            pool.wait_ge(ident_ready, 1)
            pool.affine_select(out=ident[:], in_=ident[:], compare_op=ALU.not_equal, fill=1.0, base=0,
                               pattern=[[-1, P]], channel_multiplier=1).then_inc(ident_ready, 1)
            pool.iota(tile_first[:], [[P, TILES]], base=0, channel_multiplier=0, allow_small_or_imprecise_dtypes=True
                      ).then_inc(consts_ready, 1)
            pool.iota(tile_no[:], [[1, MAX_TILES]], base=0, channel_multiplier=0, allow_small_or_imprecise_dtypes=True
                      ).then_inc(consts_ready, 1)
            pool.iota(order[:], [[-1, E]], base=E, channel_multiplier=0, allow_small_or_imprecise_dtypes=True
                      ).then_inc(consts_ready, 1)
            pool.iota(token_meta[:, :, 0], [[P, TILES]], base=0, channel_multiplier=1,
                      allow_small_or_imprecise_dtypes=True).then_inc(consts_ready, 1)
            pool.wait_ge(slots_cleared, 1)
            pool.iota(slots0[:, :, D], [[P, MAX_TILES]], base=B * S, channel_multiplier=1,
                      allow_small_or_imprecise_dtypes=True).then_inc(slots_cleared, 1)
            pool.wait_ge(slots_cleared, 2)
            pool.dma_start(sorted_dram.rearrange("(t p) n -> p t n", p=P), slots0).then_inc(slots_stored, 16)
            pool.wait_ge(half_ready, 3)

            def rstd(mv, rs, b, mean, ready):
                wait_apart(pool, mean, 2 * b + 2)
                pool.tensor_scalar(rs[:], mv[:, :, 1], EPS, None, ALU.add).then_inc(ready, 1)
                wait_apart(pool, ready, 2 * b + 1)
                pool.tensor_tensor(rs[:], rs[:], half_neg[:], ALU.pow).then_inc(ready, 1)

            def iteration(t, r):
                for slot in range(HEADS):
                    if active(t, FRONT):
                        front(t, slot)
                    if active(t, NORM):
                        norm(t, slot)
                    if active(t, BACK):
                        back(t, slot)
                    if active(t, NORM) and slot == SLOT["qk"]:
                        taken(pool, t, "qk", wait_apart)
                        pool.tensor_tensor(qkf[:], qkf[:], parts[:, :, 0, :], ALU.subtract).then_inc(qk_split, 1)
                    if active(t, NORM) and slot == SLOT["qk"] + 2:
                        wait_apart(pool, qk_split, 3 * (t - NORM) + 2)
                        pool.tensor_tensor(parts[:, :, 2, :], qkf[:], parts[:, :, 1, :], ALU.subtract).then_inc(qk_split, 1)
                    if active(t, LOAD) and slot == 11:
                        rstd(mv_a, rs_a, t, mean_a, rstd_a)
                if isinstance(t, int) and t == 1:
                    pool.wait_ge(slots_stored, 16)
                    pool.memset(k_all[:], 1.0).then_inc(ones_ready, 1)

            def front(t, slot):
                b = t - FRONT
                if slot == SLOT["lin_out"]:
                    taken(pool, t, "lin_out", wait_apart)
                    wait_apart(pool, ga_loaded, 16 * b + 16)
                    pool.tensor_tensor(y_lin[:], y_lin[:], over(mod_ga[:, 0, :], TPB), ALU.mult).then_inc(y_scaled, 1)
                    wait_apart(pool, y_scaled, b + 1)
                    pool.tensor_tensor(batch(res, b), batch(res, b), y_lin[:], ALU.add).then_inc(x1_ready, 1)

            def norm(t, slot):
                b = t - NORM
                if slot == 1:
                    rstd(mv_b, rs_b, b, mean_b, rstd_b)
                if slot == 3:
                    wait_apart(pool, norm_b, 2 * b + 2)
                    wait_apart(pool, modb_loaded, 16 * b + 16)
                    pool.tensor_tensor(h_norm[:], h_norm[:], over(mod_b[:, 0, :], TPB), ALU.mult).then_inc(h_scaled, 1)
                    wait_apart(pool, h_scaled, b + 1)
                    pool.tensor_tensor(batch(keep, b), h_norm[:], over(mod_b[:, 1, :], TPB), ALU.add).then_inc(h2_ready, 1)
                if slot == 7:
                    rstd(mv_c, rs_c, b, mean_c, rstd_c)

            def back(t, slot):
                b = t - BACK
                if slot == 0:
                    wait_apart(pool, res_ready, b)
                    pool.tensor_tensor(h2b[:], batch(keep, b), over(b_ao[:], TPB), ALU.add).then_inc(h2b_ready, 1)
                if slot == SLOT["att_out"] + 1:
                    rstd(mv_d, rs_d, b, mean_d, rstd_d)
                    wait_apart(pool, gb_loaded, 16 * b + 16)
                    pool.tensor_tensor(h2b[:], x3[:], mod_gb[:].to_broadcast([P, TPB, D]), ALU.mult
                                       ).then_inc(x3_scaled, 1)
                    wait_apart(pool, x3_scaled, b + 1)
                    pool.tensor_tensor(batch(res, b), batch(res, b), h2b[:], ALU.add).then_inc(res_ready, 1)
                if slot == SLOT["att_out"] + 3:
                    wait_apart(pool, norm_d, 2 * b + 2)
                    pool.tensor_copy(batch(keep, b), xm[:]).then_inc(kept, 1)

            drive(pool, iteration)

            pool.wait_ge(ones_again, 1)
            pool.affine_select(out=upper[:], in_=ones[:], compare_op=ALU.is_gt, fill=0.0, base=0,
                               pattern=[[1, P]], channel_multiplier=-1).then_inc(consts_ready, 1)

            pool.wait_ge(route_ready, 1)

            def scatter(k, n):
                i = 4 * k + n
                if later(k):
                    wait_apart(pool, sorted_sem[n], 16 * k)
                pool.tensor_copy(out_rows[:, n:n + 1, 0:D], keep[:, bass.ds(i, 1), :]).then_inc(scatter_staged, 1)
                pool.tensor_copy(out_rows[:, n:n + 1, D:ROW], token_meta[:, bass.ds(i, 1), :]).then_inc(scatter_staged, 1)
                pool.tensor_copy(out_slots[:, n:n + 1], slot_u[:, bass.ds(i, 1)]).then_inc(scatter_staged, 1)
                wait_apart(pool, scatter_staged, 3 * i + 3)
                pool.indirect_dma_start(sorted_dram, bass.IndirectOffsetOnAxis(ap=out_slots[:, n:n + 1], axis=0),
                                        out_rows[:, n, :], None).then_inc(sorted_sem[n], 16)

            for n in range(4):
                scatter(0, n)
            with pool.Fori(1, TILES // 4) as k:
                for n in range(4):
                    scatter(k, n)

            def take_meta(k, n):
                k, n, j = moe_tile(k, n)
                if j is not None:
                    wait_apart(pool, rows_in_loaded[n], 16 * k + 16)
                    pool.tensor_copy(meta[:, n, :], rows_buf[:, n, D:ROW]).then_inc(meta_taken, 1)

            def scatter_moe(k, n):
                k, n, j = moe_tile(k, n)
                if j is not None:
                    wait_apart(pool, moe_scattered[n], 16 * k)
                    wait_apart(pool, meta_taken, j + 1)
                    pool.tensor_copy(meta_slot[:, n:n + 1], meta[:, n, 0:1]).then_inc(pool_step, 1)
                    wait_apart(pool, moe_y_taken, j + 1)
                    pool.tensor_scalar(y_out[:, n, :], y_moe[:, n, :], meta[:, n, 1:2], None, ALU.mult
                                       ).then_inc(pool_step, 1)
                    wait_apart(pool, pool_step, 2 * j + 2)
                    pool.indirect_dma_start(moe_dram, bass.IndirectOffsetOnAxis(ap=meta_slot[:, n:n + 1], axis=0),
                                            y_out[:, n, :], None).then_inc(moe_scattered[n], 16)

            def moe_step(k, n):
                scatter_moe(k, n - 2)
                take_meta(k, n + 1)

            take_meta(0, 0)
            drive_tiles(pool, moe_step)


INPUTS = ("x c wmod wqkv_lin wo_lin bo_lin vec wqkv bqk bv wo bo wlog blog w1 b1 w2 b2").split()


def kernel(L0_attn_x, L0_attn_Wq, L0_attn_Wk, L0_attn_Wv, L0_attn_Wo, L0_attn_bo, L0_ffn_ln1_g, L0_ffn_ln1_b,
           L0_ffn_Wqkv, L0_ffn_bqkv, L0_ffn_Wo, L0_ffn_bo, L0_ffn_ln2_g, L0_ffn_ln2_b, L0_ffn_gate_w, L0_ffn_W1,
           L0_ffn_b1, L0_ffn_W2, L0_ffn_b2, L0_ffn_rW1, L0_ffn_rb1, L0_ffn_rW2, L0_ffn_rb2, L0_ffn_coef_w,
           L0_ffn_coef_b, L0_c, L0_wmod):
    import numpy as np
    import concourse.bacc as bacc
    from concourse.bass_utils import run_bass_kernel_spmd

    def heads_last(w):
        w = np.asarray(w)
        return w.reshape(*w.shape[:-1], HEADS, DH).swapaxes(-1, -2).reshape(w.shape)

    wqkv, bqkv = np.asarray(L0_ffn_Wqkv), np.asarray(L0_ffn_bqkv)
    data = {
        "x": L0_attn_x, "c": L0_c, "wmod": L0_wmod,
        "wqkv_lin": np.stack([L0_attn_Wq, L0_attn_Wk, L0_attn_Wv]), "wo_lin": L0_attn_Wo, "bo_lin": L0_attn_bo,
        "vec": np.stack([L0_ffn_ln1_g, L0_ffn_ln1_b, L0_ffn_ln2_g, L0_ffn_ln2_b]),
        "wqkv": np.concatenate([heads_last(wqkv[:, 0:D]), heads_last(wqkv[:, D:2 * D]), wqkv[:, 2 * D:]], 1),
        "bqk": np.stack([heads_last(bqkv[0:D]), heads_last(bqkv[D:2 * D])]), "bv": bqkv[2 * D:],
        "wo": L0_ffn_Wo, "bo": L0_ffn_bo,
        "wlog": np.concatenate([L0_ffn_gate_w, L0_ffn_coef_w], 1),
        "blog": np.concatenate([np.zeros(E, np.float32), L0_ffn_coef_b]),
        "w1": np.concatenate([L0_ffn_W1, np.asarray(L0_ffn_rW1)[None]]),
        "b1": np.concatenate([L0_ffn_b1, np.asarray(L0_ffn_rb1)[None]]).reshape((E + 1) * FC, P),
        "w2": np.concatenate([L0_ffn_W2, np.asarray(L0_ffn_rW2)[None]]),
        "b2": np.concatenate([L0_ffn_b2, np.asarray(L0_ffn_rb2)[None]]),
    }
    nc = bacc.Bacc("TRN2", target_bir_lowering=False, num_devices=1)
    arrays, args = {}, []
    for name in INPUTS:
        a = np.ascontiguousarray(data[name])
        arrays[f"in_{name}"] = a
        args.append(nc.dram_tensor(f"in_{name}", a.shape, mybir.dt.from_np(a.dtype), kind="ExternalInput").ap())
    out = nc.dram_tensor("out", [B, S, D], F32, kind="ExternalOutput").ap()
    adaln_block(nc, *args, out)
    got = run_bass_kernel_spmd(nc, [arrays], core_ids=[0])
    return got.results[0]["out"]
```

```python
from contextlib import ExitStack

import concourse.bass as bass
from concourse import mybir

ALU = mybir.AluOpType
ACT = mybir.ActivationFunctionType
AX = mybir.AxisListType
F32 = mybir.dt.float32
BF16 = mybir.dt.bfloat16
U32 = mybir.dt.uint32

P = 128
B, S, D = 32, 256, 128
TPB = S // P
TILES = B * TPB
HEADS, DH = 16, 8
FFN, E = 512, 8
FC = FFN // P
EPS = 1e-5
ATT_SCALE = float(DH) ** -0.5
LIN_SCALE = float(DH) ** -0.5 / D
PARTS = 3
QK_ROWS = PARTS * PARTS * DH
ALL_ROWS = QK_ROWS + PARTS
NBUF = 3
HALF = HEADS // 2
PROBS = 2
LAG = 1
VW = DH + 1
VA_COLS = HEADS * VW + 32 - VW
MAX_TILES = TILES + E - 1
NB = 4
FG = 8
POOL_GROUPS = [2, 5]
SLOTS = MAX_TILES * P
ROW = D + 2
CLEAR = B * S // ROW
NVEC = 6 + (E + 1) * FC
GT = 4
GB = GT // TPB
GROUPS = TILES // GT
WB1 = FFN + FC * P
WB2 = WB1 + FC
WCOLS = WB2 + D
NL = E + 2

LOAD, FRONT, NORM, SPREAD, MAX, EXP, BACK = range(7)
JOBS = [
    ("x_T", FRONT, 0), ("v", SPREAD, 1), ("ctx_rows0", BACK, 2), ("max_T_hi", EXP, 3), ("ctx_rows1", BACK, 3),
    ("qv", FRONT, 4), ("k", FRONT, 5), ("qk_T", FRONT, 7), ("ctx_T", BACK, 7), ("lin_ctx", FRONT, 8),
    ("att_out", BACK, 8), ("max_T_lo", MAX, 10), ("lin_m", FRONT, 11), ("h_T", NORM, 12), ("moe_in_T", BACK, 13),
    ("lin_out", FRONT, 14), ("qk", NORM, 14), ("logits", BACK, 15),
]
JOB = {name: n for n, (name, _, _) in enumerate(JOBS)}
STEPS = {
    "stats_a": 12, "norm_a": 14, "q_exp": 5, "k_exp": 6, "recips": 8, "stats_b": 0, "norm_b": 3, "stats_c": 6,
    "norm_c": 8, "part0": 15, "part1": 1, "oT_lo": 9, "oT_hi": 0, "h2b": 0, "stats_d": 9, "norm_d": 11, "keep_T": 14,
}
SLOT = {**{name: slot for name, _, slot in JOBS}, **STEPS}
PIPE = B + BACK
MAIN_FROM = BACK + 1
MAIN_TO = MAIN_FROM + (B - MAIN_FROM) // NBUF * NBUF


def done_iterations(t, stage):
    return min(max(t - stage, 0), B) if isinstance(t, int) else t - stage


def active(t, stage):
    return 0 <= t - stage < B if isinstance(t, int) else True


def bank_uses(t, job):
    n = 0
    for k in range(job % 2, len(JOBS), 2):
        n = n + done_iterations(t, JOBS[k][1])
        if k < job and active(t, JOBS[k][1]):
            n = n + 1
    return n


def wait(eng, sem, value):
    if not isinstance(value, int) or value > 0:
        eng.wait_ge(sem, value)


def adaln_block(nc, x_d, c_d, wmod_d, wqkv_lin_d, wo_lin_d, bo_lin_d, vec_d, wqkv_d, bqk_d, bv_d, wo_d, bo_d,
                wlog_d, blog_d, w1_d, b1_d, w2_d, b2_d, out_d):
    with ExitStack() as ctx:
        def sb(name, shape, dt=F32):
            return ctx.enter_context(nc.sbuf_tensor(name, shape, dt))

        def sem(name):
            return ctx.enter_context(nc.semaphore(name))

        mod_dram = nc.dram_tensor("mod_rows", [B, 4, D], F32, kind="Internal").ap()
        split_dram = nc.dram_tensor("split_qk", [2, PARTS, P, S], BF16, kind="Internal").ap()
        sorted_dram = nc.dram_tensor("sorted_tokens", [SLOTS, ROW], F32, kind="Internal").ap()
        moe_dram = nc.dram_tensor("moe_out", [B * S + SLOTS, D], F32, kind="Internal").ap()

        res = sb("res", [P, TILES, D])
        keep = sb("keep", [P, TILES, D])
        moe_in_T = sb("moe_in_T", [P, B * S])
        big = sb("big", [P, NBUF * HEADS * S])
        w_shared = sb("w_shared", [P, WCOLS])
        logit = sb("logit", [P, TILES, NL])
        ident = sb("ident", [P, P])
        ident_half = sb("ident_half", [P, P], BF16)
        vecs_T = sb("vecs_T", [P, 48])
        BIGH = NBUF * HEADS * S // 2
        q_all = big[:, 0:BIGH].bitcast(BF16).rearrange("p (n h s) -> p n h s", n=NBUF, h=HEADS)
        k_all = big[:, BIGH:2 * BIGH].bitcast(BF16).rearrange("p (n h s) -> p n h s", n=NBUF, h=HEADS)
        w_exp = big[:, 0:E * WCOLS].rearrange("p (e n) -> p e n", e=E)
        slots0 = moe_in_T[:, 0:CLEAR * ROW].rearrange("p (t n) -> p t n", n=ROW)
        staged = moe_in_T[:, 0:NB * WCOLS].rearrange("p (n w) -> p n w", n=NB)
        fin = moe_in_T[:].rearrange("p (t d) -> p t d", d=D)
        gb_all = keep[:, 0:B, :]

        w_qv = sb("w_qv", [P, 2 * D])
        w_k = sb("w_k", [P, D])
        w_lo = sb("w_lo", [P, D])
        w_qkv = sb("w_qkv", [P, 3 * D])
        w_ao = sb("w_ao", [P, D])
        w_log = sb("w_log", [P, NL])
        b_lo = sb("b_lo", [P, D])
        b_v = sb("b_v", [P, D])
        b_ao = sb("b_ao", [P, D])
        b_log = sb("b_log", [P, NL])
        half_neg = sb("half_neg", [P, TPB])
        modT = sb("modT", [P, 2, B])
        rows_in = sb("rows_in", [NVEC, P])
        tile_first = sb("tile_first", [P, TILES])
        tile_no = sb("tile_no", [P, MAX_TILES])
        order = sb("order", [P, E])
        token_meta = sb("token_meta", [P, TILES, 2])

        st_a, st_b, st_c, st_d = (sb(f"st_{x}", [P, TPB, 6]) for x in "abcd")
        mv_a, mv_b, mv_c, mv_d = (sb(f"mv_{x}", [P, TPB, 2]) for x in "abcd")
        rs_a, rs_b, rs_c, rs_d = (sb(f"rs_{x}", [P, TPB]) for x in "abcd")
        ARENA = 9920
        arena = sb("arena", [P, ARENA])
        used = [0]

        def take(shape, dt=F32):
            words = 1
            for n in shape:
                words *= n
            if dt == BF16:
                words //= 2
            piece = arena[:, used[0]:used[0] + words]
            used[0] += (words + 7) // 8 * 8
            assert used[0] <= ARENA
            if dt != F32:
                piece = piece.bitcast(dt)
            names = "abcd"[:len(shape)]
            return piece.rearrange(f"p ({' '.join(names)}) -> p {' '.join(names)}",
                                   **dict(zip(names[1:], shape[1:]))) if len(shape) > 1 else piece

        xn = take([TPB, D])
        hT = take([S])
        q_neg = take([TPB])
        q_sum = take([TPB])
        q_rec = take([TPB])
        q_exp = take([TPB, D])
        v_lin = take([TPB, D])
        k_neg = take([1])
        k_sum = take([1])
        k_rec = take([1])
        k_exp = take([S])
        qk_T = take([2, S])
        ctx_lin = take([D])
        m_lin = take([D])
        y_lin = take([TPB, D])
        h_norm = take([TPB, D])
        xc = take([TPB, D])
        xnT = take([S])
        qkf = take([2, S])
        parts = take([2, PARTS, S], BF16)
        va = take([NBUF, TPB, VA_COLS])
        neg_max = take([2, TPB, HALF])
        max_cols = take([2, TPB, PARTS, HALF], BF16)
        max_parts = sb("max_parts", [PARTS * HALF, 2, S], BF16)
        probs = take([PROBS, TPB * S])
        oT = take([HEADS // 4, S])
        o_rec = take([TPB, HEADS])
        o_rows = take([TPB, D])
        o_T = take([S])
        h2b = take([TPB, D])
        x3 = take([TPB, D])
        xm = take([TPB, D])
        xmT = take([S])
        mod_ga = take([1, D])
        mod_b = take([2, D])
        mod_gb = take([1, D])

        used[0] = 0
        upper = take([P])
        ones = take([P])
        onehot = take([TILES * E])
        hid = take([2, FC, GT * P])
        hid_flat = hid[:].rearrange("p n c s -> p (n c s)")

        def route_buf(n, cols):
            return big[:, E * WCOLS + n * TILES * E:E * WCOLS + n * TILES * E + cols]

        lmax = take([2, TILES])
        shifted = take([TILES, NL])
        w_moe = take([TILES])
        w_rm = take([TILES])
        slot_u = take([TILES], U32)
        expert_u = take([MAX_TILES], U32)
        small = take([3, E])
        y_shared = take([GT, D])
        gb2 = take([GB, D])
        out_rows = take([2, GT, ROW])
        out_slots = take([2, GT], U32)
        rows_buf = take([NB, ROW])
        tile_T = take([NB, P])
        y_moe = take([NB, D])
        y_out = take([NB, D])
        meta = take([NB, 2])
        meta_slot = take([NB], U32)
        hid_moe = hid_flat[:, 0:NB * FFN].rearrange("p (n c s) -> p n c s", n=NB, c=FC)

        bank = [ctx.enter_context(nc.psum_tensor(f"bank{n}", [P, 512], F32)) for n in range(8)]
        work, max_bank, exp_bank, o_bank = bank[0:2], bank[2:4], bank[4:6], bank[6:8]

        def sems(names):
            return [sem(name) for name in names.split()]

        (c_loaded, rows_loaded, weights_loaded, shared_loaded, mods_ready, mods_stored, ident_ready, consts_ready,
         half_ready, silu_step, silu_exp, setup_full, setup_taken, mod_step, slots_cleared, slots_stored,
         ones_ready) = sems(
             "c_loaded rows_loaded weights_loaded shared_loaded mods_ready mods_stored ident_ready consts_ready "
             "half_ready silu_step silu_exp setup_full setup_taken mod_step slots_cleared slots_stored ones_ready")
        (x_loaded, ga_loaded, modb_loaded, gb_loaded, max_full, max_done, exp_full, exp_done, pv_done, q_max_ready,
         k_max_ready, recips, y_scaled, x1_ready, h_scaled, h2_ready, qk_split, split_stored, qk_spread, oT_ready,
         o_rec_ready, h2b_ready, x3_scaled, res_ready, kept) = sems(
             "x_loaded ga_loaded modb_loaded gb_loaded max_full max_done exp_full exp_done pv_done q_max_ready "
             "k_max_ready recips y_scaled x1_ready h_scaled h2_ready qk_split split_stored qk_spread oT_ready "
             "o_rec_ready h2b_ready x3_scaled res_ready kept")
        stats_a, stats_b, stats_c, stats_d = (sem(f"stats_{x}") for x in "abcd")
        mean_a, mean_b, mean_c, mean_d = (sem(f"mean_{x}") for x in "abcd")
        rstd_a, rstd_b, rstd_c, rstd_d = (sem(f"rstd_{x}") for x in "abcd")
        norm_a, norm_b, norm_c, norm_d = (sem(f"norm_{x}") for x in "abcd")
        work_full = [sem(f"work_full{n}") for n in range(2)]
        work_free = [sem(f"work_free{n}") for n in range(2)]
        max_split = [sem(f"max_split{n}") for n in range(2)]
        max_spread = [sem(f"max_spread{n}") for n in range(2)]
        (route_step, route_exp, ones_set, counts_full, route_ready, experts_loaded, gb2_loaded, up_full, gelu_done,
         down_full, down_taken, shared_step, shared_added, scatter_staged, tile_T_full, tile_T_ready, weight_step,
         stage_ready, moe_up_full, moe_gelu_done, moe_y_full, moe_y_taken, y_weighted, meta_taken, gb_all_loaded,
         fin_stored) = sems(
             "route_step route_exp ones_set counts_full route_ready experts_loaded gb2_loaded up_full gelu_done "
             "down_full down_taken shared_step shared_added scatter_staged tile_T_full tile_T_ready weight_step "
             "stage_ready moe_up_full moe_gelu_done moe_y_full moe_y_taken y_weighted meta_taken gb_all_loaded "
             "fin_stored")
        sorted_sem = [sem(f"sorted{n}") for n in range(2)]
        rows_in_loaded = [sem(f"rows_in_loaded{n}") for n in range(NB)]
        moe_scattered = [sem(f"moe_scattered{n}") for n in range(NB)]
        fin_loaded = [sem(f"fin_loaded{n}") for n in range(FG)]
        fin_step = [sem(f"fin_step{n}") for n in range(FG)]
        def mod_rows(b, first, n):
            return mod_dram[bass.ds(b, 1), first:first + n, :].to_broadcast([P, n, D])

        def batch(buf, b):
            return buf[:, bass.ds(b * TPB, TPB), :]

        def tile(buf, b, n):
            return buf[:, bass.ds(b * TPB + n, 1), :]

        def over(row, n):
            return row.unsqueeze(1).to_broadcast([P, n, D])

        def wait_apart(eng, sem, value):
            wait(eng, sem, value)
            if not isinstance(value, int):
                eng.nop(nofuse=True)

        def full(eng, t, name, wait=wait):
            job = JOB[name]
            wait(eng, work_full[job % 2], bank_uses(t, job) + 1)

        def taken(eng, t, name, wait=wait):
            job = JOB[name]
            wait(eng, work_free[job % 2], bank_uses(t, job) + 1)

        def drive(eng, run):
            for t in range(MAIN_FROM):
                run(t, t % NBUF)
            with eng.Fori(0, (MAIN_TO - MAIN_FROM) // NBUF) as k:
                for r in range(NBUF):
                    run(k * NBUF + MAIN_FROM + r, (MAIN_FROM + r) % NBUF)
            for t in range(MAIN_TO, PIPE):
                run(t, t % NBUF)

        def drive_tiles(eng, run):
            rounds = (MAX_TILES - NB) // NB
            for j in range(2 * NB):
                run(j // NB, j % NB)
            with eng.Fori(2, rounds) as k:
                for n in range(NB):
                    run(k, n)
            for j in range(rounds * NB, MAX_TILES + 2):
                run(j // NB, j % NB)

        def moe_tile(k, n):
            k, n = k + n // NB, n % NB
            j = NB * k + n
            if isinstance(k, int) and not 0 <= j < MAX_TILES:
                return k, n, None
            return k, n, j

        def drive_groups(eng, run):
            for n in range(2):
                run(0, n)
            with eng.Fori(1, GROUPS // 2) as k:
                for n in range(2):
                    run(k, n)

        def gb_rows(g):
            return mod_dram[bass.ds(g * GB, GB), 3, :].unsqueeze(0).to_broadcast([P, GB, D])

        def add_experts(eng, groups):
            eng.wait_ge(gb_all_loaded, 16)
            tiles, batches = TILES // FG, B // FG
            for g in groups:
                eng.wait_ge(fin_loaded[g], 16)
                rows = fin[:, g * tiles:(g + 1) * tiles, :]
                by_batch = rows.rearrange("p (b n) d -> p b n d", n=TPB)
                gb = gb_all[:, g * batches:(g + 1) * batches, :].unsqueeze(2).to_broadcast([P, batches, TPB, D])
                eng.tensor_tensor(by_batch, by_batch, gb, ALU.mult).then_inc(fin_step[g], 1)
                eng.wait_ge(fin_step[g], 1)
                eng.tensor_tensor(rows, rows, res[:, g * tiles:(g + 1) * tiles, :], ALU.add).then_inc(fin_step[g], 1)

        def later(k):
            return not isinstance(k, int) or k > 0

        LN1G, LN1B, LN2G, LN2B, BQ, BK, B1 = range(7)

        def vec(n):
            return vecs_T[:, n:n + 1]

        c_in, c_exp, c_silu = xc[0:B, 0, :], xc[0:B, 1, :], h_norm[0:B, 0, :]
        c_T = h_norm[:, 1, 0:B]
        wmod = keep[:, 0:6, :].rearrange("p a b -> p (a b)")
        mods = keep[0:B, 6:12, :]
        gsign, gabs = keep[0:B, 12, :], keep[0:B, 13, :]

        WEIGHTS = [
            (w_qv[:, 0:D], wqkv_lin_d[0]), (w_qv[:, D:2 * D], wqkv_lin_d[2]), (w_k[:], wqkv_lin_d[1]),
            (w_lo[:], wo_lin_d), (w_qkv[:], wqkv_d), (w_ao[:], wo_d), (w_log[:], wlog_d),
            (b_lo[:], bo_lin_d.unsqueeze(0).to_broadcast([P, D])),
            (b_v[:], bv_d.unsqueeze(0).to_broadcast([P, D])),
            (b_ao[:], bo_d.unsqueeze(0).to_broadcast([P, D])),
            (b_log[:], blog_d.unsqueeze(0).to_broadcast([P, NL])),
        ]
        SHARED_WEIGHTS = [
            (w_shared[:, 0:FFN], w1_d[E]),
            (w_shared[:, FFN:WB1].rearrange("p (c n) -> p c n", c=FC), w2_d[E].rearrange("(c p) n -> p c n", p=P)),
            (w_shared[:, WB2:WCOLS], b2_d[E:E + 1, :].to_broadcast([P, D])),
        ]

        block = ctx.enter_context(nc.Block())

        @block.sync
        def _(sp):
            sp.dma_start(c_in, c_d).then_inc(c_loaded, 16)
            sp.dma_start(wmod, wmod_d).then_inc(rows_loaded, 16)
            sp.dma_start(rows_in[0:4, :], vec_d).then_inc(rows_loaded, 16)
            sp.dma_start(rows_in[4:6, :], bqk_d).then_inc(rows_loaded, 16)
            sp.dma_start(rows_in[6:NVEC, :], b1_d).then_inc(rows_loaded, 16)
            for dst, src in WEIGHTS:
                sp.dma_start(dst, src).then_inc(weights_loaded, 16)
            def spread_max(t, name, buf, half):
                taken(sp, t, name, wait_apart)
                for i in range(PARTS):
                    sp.dma_start(q_all[QK_ROWS + i:QK_ROWS + i + 1, buf, half * HALF:(half + 1) * HALF, :],
                                 max_parts[i * HALF:(i + 1) * HALF, half, :]).then_inc(max_spread[half], 16)

            def clear_slots(first, n):
                sp.dma_start(sorted_dram[first * P:(first + n) * P, :].rearrange("(t p) n -> p t n", p=P),
                             slots0[:, 0:n, :]).then_inc(slots_stored, 16)

            def iteration(t, r):
                if isinstance(t, int) and t == 2:
                    sp.wait_ge(slots_cleared, 2)
                    clear_slots(0, CLEAR)
                if isinstance(t, int) and t == 5:
                    sp.wait_ge(slots_cleared, 3)
                    clear_slots(CLEAR, MAX_TILES - CLEAR)
                if active(t, LOAD):
                    wait_apart(sp, x_loaded, 16 * (t - LOAD))
                    sp.dma_start(batch(res, t), x_d[bass.ds(t, 1), :, :].rearrange("a (n p) d -> p (a n) d", p=P)
                                 ).then_inc(x_loaded, 16)
                if active(t, FRONT):
                    b = t - FRONT
                    if isinstance(b, int) and b == 0:
                        sp.wait_ge(mods_stored, 64)
                    wait_apart(sp, y_scaled, b)
                    wait_apart(sp, ga_loaded, 16 * b)
                    sp.dma_start(mod_ga[:], mod_rows(b, 0, 1)).then_inc(ga_loaded, 16)
                if active(t, NORM):
                    b = t - NORM
                    wait_apart(sp, h2_ready, b)
                    wait_apart(sp, modb_loaded, 16 * b)
                    sp.dma_start(mod_b[:], mod_rows(b, 1, 2)).then_inc(modb_loaded, 16)
                if active(t, BACK):
                    b = t - BACK
                    wait_apart(sp, x3_scaled, b)
                    wait_apart(sp, gb_loaded, 16 * b)
                    sp.dma_start(mod_gb[:], mod_rows(b, 3, 1)).then_inc(gb_loaded, 16)
                if active(t, EXP):
                    spread_max(t, "max_T_hi", (r - EXP) % NBUF, 1)
                if active(t, SPREAD):
                    b, buf = t - SPREAD, (r - SPREAD) % NBUF
                    wait_apart(sp, qk_split, 4 * b + 4)
                    wait_apart(sp, qk_spread, 64 * b)
                    for n in range(2):
                        sp.dma_start(split_dram[n].rearrange("i p s -> p i s"), parts[:, n]).then_inc(split_stored, 16)
                    wait_apart(sp, split_stored, 32 * b + 32)
                    if isinstance(b, int) and b < NBUF:
                        sp.wait_ge(ones_ready, 1)
                    else:
                        wait_apart(sp, exp_full, HEADS * (b - NBUF + 1))
                    for i in range(PARTS):
                        sp.dma_start(q_all[i * PARTS * DH:(i + 1) * PARTS * DH, buf].rearrange("p h s -> p (h s)"),
                                     split_dram[0, i].rearrange("(d h) s -> d (h s)", d=DH).unsqueeze(0)
                                     .to_broadcast([PARTS, DH, HEADS * S])).then_inc(qk_spread, 16)
                    sp.dma_start(k_all[0:QK_ROWS, buf].rearrange("p h s -> p (h s)"),
                                 split_dram[1].rearrange("i (d h) s -> (i d) (h s)", d=DH).unsqueeze(0)
                                 .to_broadcast([PARTS, PARTS * DH, HEADS * S])).then_inc(qk_spread, 16)
                if active(t, MAX):
                    spread_max(t, "max_T_lo", (r - MAX) % NBUF, 0)

            drive(sp, iteration)

            sp.wait_ge(exp_full, B * HEADS)
            for e in range(E):
                sp.dma_start(w_exp[:, e, 0:FFN], w1_d[e]).then_inc(experts_loaded, 16)
                sp.dma_start(w_exp[:, e, FFN:WB1].rearrange("p (c n) -> p c n", c=FC),
                             w2_d[e].rearrange("(c p) n -> p c n", p=P)).then_inc(experts_loaded, 16)
                sp.dma_start(w_exp[:, e, WB2:WCOLS], b2_d[e:e + 1, :].to_broadcast([P, D])
                             ).then_inc(experts_loaded, 16)

            def load_gb(g):
                if later(g):
                    wait_apart(sp, shared_added, g)
                sp.dma_start(gb2[:], gb_rows(g)).then_inc(gb2_loaded, 16)
                wait_apart(sp, gb2_loaded, 16 * g + 16)

            sp.wait_ge(route_ready, 1)
            load_gb(0)
            with sp.Fori(1, GROUPS) as g:
                load_gb(g)

            for n in range(2):
                sp.wait_ge(sorted_sem[n], 16 * TILES // 2)

            def load_rows(k, n):
                k, n, j = moe_tile(k, n)
                if j is not None:
                    wait_apart(sp, meta_taken, j - NB + 1)
                    wait_apart(sp, tile_T_full, j - NB + 1)
                    wait_apart(sp, rows_in_loaded[n], 16 * k)
                    sp.dma_start(rows_buf[:, n, :], sorted_dram[bass.ds(j * P, P), :]).then_inc(rows_in_loaded[n], 16)

            drive_tiles(sp, load_rows)
            sp.dma_start(gb_all[:].rearrange("p b d -> p (b d)"),
                         mod_dram[:, 3, :].unsqueeze(0).to_broadcast([P, B, D])).then_inc(gb_all_loaded, 16)

            for n in range(NB):
                sp.wait_ge(moe_scattered[n], 16 * ((MAX_TILES + NB - 1 - n) // NB))
            tiles = TILES // FG
            for g in range(FG):
                sp.dma_start(fin[:, g * tiles:(g + 1) * tiles, :],
                             moe_dram[g * tiles * P:(g + 1) * tiles * P, :].rearrange("(n p) d -> p n d", p=P)
                             ).then_inc(fin_loaded[g], 16)
            sp.wait_ge(fin_stored, 16 * FG)

        @block.tensor
        def _(pe):
            pe.wait_ge(silu_step, 3)
            pe.wait_ge(ident_ready, 2)
            pe.transpose(bank[0][:, 0:B], c_silu, ident[0:B, 0:B]).then_inc(setup_full, 1)
            pe.wait_ge(rows_loaded, 64)
            pe.transpose(bank[1][:, 0:NVEC], rows_in[0:NVEC, :], ident[0:NVEC, 0:NVEC]).then_inc(setup_full, 1)
            pe.wait_ge(setup_taken, 1)
            for n in range(2):
                pe.matmul(bank[2 + n][0:B, 0:3 * D], c_T, wmod[:, 3 * D * n:3 * D * (n + 1)], start=True, stop=True
                          ).then_inc(setup_full, 1)
            pe.wait_ge(mod_step, 3)
            for n in range(2):
                pe.transpose(bank[0][:, n * B:(n + 1) * B], mods[:, n, :], ident[0:B, 0:B]).then_inc(setup_full, 1)
            pe.wait_ge(setup_taken, 3)
            pe.wait_ge(weights_loaded, 16 * len(WEIGHTS))

            def open_bank(t, name):
                k = JOB[name]
                wait(pe, work_free[k % 2], bank_uses(t, k))
                return work[k % 2]

            def close_bank(name, last):
                last.then_inc(work_full[JOB[name] % 2], 1)

            def transpose_tiles(t, name, tiles):
                w = open_bank(t, name)
                for n, src in enumerate(tiles):
                    last = pe.transpose(w[0:src.shape[1], n * P:(n + 1) * P], src, ident[:])
                close_bank(name, last)

            def scores_t(b, buf, h):
                if h == 0:
                    pe.wait_ge(max_spread[0], 48 * b + 48)
                if h == HALF:
                    pe.wait_ge(max_spread[1], 48 * b + 48)
                wait(pe, exp_done, b * HEADS + h - 1)
                for k in range(TPB):
                    last = pe.matmul(exp_bank[h % 2][:, k * S:(k + 1) * S],
                                     k_all[0:ALL_ROWS, buf, h, k * P:(k + 1) * P],
                                     q_all[0:ALL_ROWS, buf, h, :], start=True, stop=True)
                last.then_inc(exp_full, 1)

            def scores(b, buf, h):
                if h == 0:
                    pe.wait_ge(qk_spread, 64 * b + 64)
                wait(pe, max_done, b * HEADS + h - 1)
                for q in range(TPB):
                    last = pe.matmul(max_bank[h % 2][:, q * S:(q + 1) * S], q_all[0:QK_ROWS, buf, h, q * P:(q + 1) * P],
                                     k_all[0:QK_ROWS, buf, h, :], start=True, stop=True)
                last.then_inc(max_full, 1)

            def transpose_max(t, name, b, half):
                pe.wait_ge(max_split[half], 4 * b + 4)
                w = open_bank(t, name)[:].bitcast(BF16)
                for n in range(TPB):
                    last = pe.transpose(w[0:PARTS * HALF, n * P:(n + 1) * P],
                                        max_cols[:, half, n].rearrange("p i h -> p (i h)"), ident_half[:])
                close_bank(name, last)

            def probs_v(t, b, buf, h):
                if h == 0:
                    taken(pe, t - EXP + SPREAD, "v")
                if h % HALF == 0:
                    wait(pe, oT_ready, 2 * b - 1 + h // HALF)
                pe.wait_ge(exp_done, b * HEADS + h + 1)
                j, g = h % 4, h // 4 % 2
                for k in range(TPB):
                    last = pe.matmul(o_bank[h // HALF][32 * j:32 * j + 32, g * S:(g + 1) * S],
                                     va[:, buf, k, h * VW:h * VW + 32], probs[:, h % PROBS, k * S:(k + 1) * S],
                                     start=(k == 0), stop=(k == TPB - 1))
                last.then_inc(pv_done, 1)

            def front(t, slot):
                b = t - FRONT
                if slot == SLOT["x_T"]:
                    pe.wait_ge(norm_a, 2 * b + 2)
                    transpose_tiles(t, "x_T", [xn[:, n, :] for n in range(TPB)])
                if slot == SLOT["qv"]:
                    w = open_bank(t, "qv")
                    taken(pe, t, "x_T")
                    for n in range(TPB):
                        last = pe.matmul(w[:, 2 * D * n:2 * D * (n + 1)], hT[:, n * P:(n + 1) * P], w_qv[:],
                                         start=True, stop=True)
                    close_bank("qv", last)
                if slot == SLOT["k"]:
                    w = open_bank(t, "k")
                    close_bank("k", pe.matmul(w[:, 0:S], w_k[:], hT[:], start=True, stop=True))
                if slot == SLOT["qk_T"]:
                    w = open_bank(t, "qk_T")
                    taken(pe, t, "qv")
                    taken(pe, t, "k")
                    for n in range(TPB):
                        pe.transpose(w[:, n * P:(n + 1) * P], q_exp[:, n, :], ident[:])
                    for n in range(TPB):
                        last = pe.transpose(w[:, S + n * P:S + (n + 1) * P], k_exp[:, n * P:(n + 1) * P], ident[:])
                    close_bank("qk_T", last)
                if slot == SLOT["lin_ctx"]:
                    w = open_bank(t, "lin_ctx")
                    taken(pe, t, "qk_T")
                    for n in range(TPB):
                        last = pe.matmul(w[:, 0:D], v_lin[:, n, :], qk_T[:, 1, n * P:(n + 1) * P],
                                         start=(n == 0), stop=(n == TPB - 1))
                    close_bank("lin_ctx", last)
                if slot == SLOT["lin_m"]:
                    w = open_bank(t, "lin_m")
                    taken(pe, t, "lin_ctx")
                    close_bank("lin_m", pe.matmul(w[:, 0:D], ctx_lin[:], w_lo[:], start=True, stop=True))
                if slot == SLOT["lin_out"]:
                    w = open_bank(t, "lin_out")
                    taken(pe, t, "lin_m")
                    for n in range(TPB):
                        last = pe.matmul(w[:, n * D:(n + 1) * D], qk_T[:, 0, n * P:(n + 1) * P], m_lin[:],
                                         start=True, stop=True)
                    close_bank("lin_out", last)

            def norm(t, slot):
                b = t - NORM
                if slot == SLOT["h_T"]:
                    pe.wait_ge(norm_c, 2 * b + 2)
                    transpose_tiles(t, "h_T", [xc[:, n, :] for n in range(TPB)])
                if slot == SLOT["qk"]:
                    w = open_bank(t, "qk")
                    taken(pe, t, "h_T")
                    for n in range(2):
                        last = pe.matmul(w[:, n * S:(n + 1) * S], w_qkv[:, n * D:(n + 1) * D], xnT[:],
                                         start=True, stop=True)
                    close_bank("qk", last)

            def spread(t, slot):
                if slot == SLOT["v"]:
                    w = open_bank(t, "v")
                    for n in range(TPB):
                        last = pe.matmul(w[:, n * D:(n + 1) * D], xnT[:, n * P:(n + 1) * P], w_qkv[:, 2 * D:3 * D],
                                         start=True, stop=True)
                    close_bank("v", last)

            def back(t, slot):
                b = t - BACK
                if slot in (SLOT["ctx_rows0"], SLOT["ctx_rows1"]):
                    pe.wait_ge(oT_ready, 2 * b + 2)
                    n = slot - SLOT["ctx_rows0"]
                    transpose_tiles(t, f"ctx_rows{n}", [oT[:, g, n * P:(n + 1) * P] for g in range(HEADS // 4)])
                if slot == SLOT["ctx_T"]:
                    taken(pe, t, "ctx_rows0")
                    taken(pe, t, "ctx_rows1")
                    transpose_tiles(t, "ctx_T", [o_rows[:, n, :] for n in range(TPB)])
                if slot == SLOT["att_out"]:
                    w = open_bank(t, "att_out")
                    taken(pe, t, "ctx_T")
                    for n in range(TPB):
                        last = pe.matmul(w[:, n * D:(n + 1) * D], o_T[:, n * P:(n + 1) * P], w_ao[:],
                                         start=True, stop=True)
                    close_bank("att_out", last)
                if slot == SLOT["moe_in_T"]:
                    pe.wait_ge(norm_d, 2 * b + 2)
                    transpose_tiles(t, "moe_in_T", [xm[:, n, :] for n in range(TPB)])
                if slot == SLOT["logits"]:
                    w = open_bank(t, "logits")
                    taken(pe, t, "moe_in_T")
                    for n in range(TPB):
                        last = pe.matmul(w[:, n * NL:(n + 1) * NL], xmT[:, n * P:(n + 1) * P], w_log[:],
                                         start=True, stop=True)
                    close_bank("logits", last)

            def iteration(t, r):
                for slot in range(HEADS):
                    if active(t, MAX):
                        scores(t - MAX, (r - MAX) % NBUF, slot)
                    if active(t, EXP):
                        scores_t(t - EXP, (r - EXP) % NBUF, slot)
                    if active(t, FRONT):
                        front(t, slot)
                    if active(t, NORM):
                        norm(t, slot)
                    if active(t, SPREAD):
                        spread(t, slot)
                    if slot == SLOT["max_T_hi"] and active(t, EXP):
                        transpose_max(t, "max_T_hi", t - EXP, 1)
                    if slot == SLOT["max_T_lo"] and active(t, MAX):
                        transpose_max(t, "max_T_lo", t - MAX, 0)
                    if active(t, BACK):
                        back(t, slot)
                    if slot < LAG and active(t, BACK):
                        probs_v(t, t - BACK, (r - BACK) % NBUF, HEADS - LAG + slot)
                    if slot >= LAG and active(t, EXP):
                        probs_v(t, t - EXP, (r - EXP) % NBUF, slot - LAG)

            drive(pe, iteration)

            for n in range(2):
                pe.wait_ge(work_free[n], bank_uses(PIPE, n))
            pe.wait_ge(kept, 2 * B)

            def shared_up(k, n, cs):
                g = 2 * k + n
                for c in cs:
                    if later(g) or c >= 2:
                        pe.wait_ge(gelu_done, g * FC + c - 1)
                    pe.matmul(bank[4 + c % 2][:], w_shared[:, c * P:(c + 1) * P],
                              moe_in_T[:, bass.ds(g * GT * P, GT * P)], start=True, stop=True).then_inc(up_full, 1)

            def shared_down(k, n):
                g = 2 * k + n
                pe.wait_ge(gelu_done, g * FC + FC)
                if later(k):
                    pe.wait_ge(down_taken, g - 1)
                for m in range(GT):
                    for c in range(FC):
                        last = pe.matmul(bank[6 + n][:, m * D:(m + 1) * D], hid[:, n, c, m * P:(m + 1) * P],
                                         w_shared[:, FFN + c * P:FFN + (c + 1) * P], start=(c == 0), stop=(c == FC - 1))
                last.then_inc(down_full, 1)

            def shared_step_pair(k, n, k_before, n_before):
                shared_up(k, n, range(2))
                shared_down(k_before, n_before)
                shared_up(k, n, range(2, FC))

            pe.wait_ge(res_ready, B)
            pe.wait_ge(shared_loaded, 16 * len(SHARED_WEIGHTS))
            shared_up(0, 0, range(FC))
            pe.wait_ge(route_step, 8)
            pe.wait_ge(consts_ready, 5)
            pe.matmul(bank[2][:, 0:TILES * E], upper[:], onehot[:], start=True, stop=True
                      ).then_inc(counts_full, 1)
            pe.matmul(bank[3][:, 0:TILES * E], ones[:], onehot[:], start=True, stop=True
                      ).then_inc(counts_full, 1)
            shared_step_pair(0, 1, 0, 0)
            shared_step_pair(1, 0, 0, 1)
            with pe.Fori(1, GROUPS // 2 - 1) as k:
                shared_step_pair(k, 1, k, 0)
                shared_step_pair(k + 1, 0, k, 1)
            shared_step_pair(GROUPS // 2 - 1, 1, GROUPS // 2 - 1, 0)
            shared_down(GROUPS // 2 - 1, 1)

            def moe_transpose(k, n):
                k, n, j = moe_tile(k, n)
                if j is not None:
                    pe.wait_ge(rows_in_loaded[n], 16 * k + 16)
                    wait(pe, tile_T_ready, j - 1)
                    pe.transpose(bank[n % 2][:, 0:P], rows_buf[:, n, 0:D], ident[:]).then_inc(tile_T_full, 1)

            def moe_up(k, n):
                k, n, j = moe_tile(k, n)
                if j is not None:
                    pe.wait_ge(tile_T_ready, j + 1)
                    pe.wait_ge(stage_ready, j + 1)
                    wait(pe, moe_gelu_done, (j - NB + 1) * FC)
                    for c in range(FC):
                        last = pe.matmul(bank[2 + n][:, c * P:(c + 1) * P], staged[:, n, c * P:(c + 1) * P],
                                         tile_T[:, n, :], start=True, stop=True)
                    last.then_inc(moe_up_full, 1)

            def moe_down(k, n):
                k, n, j = moe_tile(k, n)
                if j is not None:
                    pe.wait_ge(moe_gelu_done, j * FC + FC)
                    if isinstance(j, int) and j < 2:
                        pe.wait_ge(down_taken, GROUPS - 1 + j)
                    wait(pe, moe_y_taken, j - 1)
                    for c in range(FC):
                        last = pe.matmul(bank[6 + n % 2][:, 0:D], hid_moe[:, n, c, :],
                                         staged[:, n, FFN + c * P:FFN + (c + 1) * P],
                                         start=(c == 0), stop=(c == FC - 1))
                    last.then_inc(moe_y_full, 1)

            def moe_step(k, n):
                moe_up(k, n)
                moe_transpose(k, n + 2)
                moe_down(k, n - 2)

            moe_transpose(0, 0)
            moe_transpose(0, 1)
            drive_tiles(pe, moe_step)

        @block.scalar
        def _(act):
            act.wait_ge(c_loaded, 16)
            act.activation(c_exp, c_in, ACT.Exp, scale=-1.0).then_inc(silu_exp, 1)
            act.wait_ge(mods_ready, 3)
            for n, row in enumerate((2, 4, 3, 5)):
                act.dma_start(mod_dram[:, n, :], mods[:, row, :]).then_inc(mods_stored, 16)
            for dst, src in SHARED_WEIGHTS:
                act.dma_start(dst, src).then_inc(shared_loaded, 16)

            def iteration(t, r):
                for slot in range(HEADS):
                    if active(t, EXP):
                        b = t - EXP
                        act.wait_ge(exp_full, b * HEADS + slot + 1)
                        wait(act, pv_done, b * HEADS + slot - PROBS + 1)
                        act.activation(probs[:, slot % PROBS, :], exp_bank[slot % 2][:], ACT.Exp, scale=ATT_SCALE
                                       ).then_inc(exp_done, 1)
                    if active(t, BACK) and slot == SLOT["oT_hi"]:
                        act.wait_ge(pv_done, (t - BACK) * HEADS + HEADS)
                        act.activation(oT[:, 2:4, :].rearrange("p g s -> p (g s)"), o_bank[1][:], ACT.Copy
                                       ).then_inc(oT_ready, 1)
                    if active(t, EXP) and slot == SLOT["oT_lo"]:
                        act.wait_ge(pv_done, (t - EXP) * HEADS + HALF)
                        if active(t, BACK):
                            full(act, t, "ctx_rows1")
                        act.activation(oT[:, 0:2, :].rearrange("p g s -> p (g s)"), o_bank[0][:], ACT.Copy
                                       ).then_inc(oT_ready, 1)
                    if active(t, FRONT):
                        front(t, slot)
                    if active(t, NORM):
                        norm(t, slot)
                    if active(t, SPREAD):
                        spread(t, slot)
                    if active(t, EXP) and slot == SLOT["max_T_hi"]:
                        take_max(t, "max_T_hi", t - EXP, 1)
                    if active(t, MAX) and slot == SLOT["max_T_lo"]:
                        take_max(t, "max_T_lo", t - MAX, 0)
                    if active(t, BACK):
                        back(t, slot)

            def free(ins, name):
                ins.then_inc(work_free[JOB[name] % 2], 1)

            def bank_of(name):
                return work[JOB[name] % 2]

            def take_max(t, name, b, half):
                full(act, t, name)
                wait(act, max_spread[half], 48 * b)
                free(act.activation(max_parts[:, half, :], bank_of(name)[:].bitcast(BF16)[0:PARTS * HALF, 0:S],
                                    ACT.Copy), name)

            def front(t, slot):
                b = t - FRONT
                if slot == SLOT["x_T"]:
                    if isinstance(t, int) and b == 0:
                        act.wait_ge(setup_taken, 3)
                    full(act, t, "x_T")
                    free(act.activation(hT[:], bank_of("x_T")[:, 0:S], ACT.Identity, bias=modT[:, 0, bass.ds(b, 1)],
                                        scale=modT[:, 1, bass.ds(b, 1)]), "x_T")
                if slot == SLOT["q_exp"]:
                    act.wait_ge(q_max_ready, b + 1)
                    w = bank_of("qv")[:].rearrange("p (n two d) -> p n two d", n=TPB, two=2)
                    for n in range(TPB):
                        act.activation(q_exp[:, n, :], w[:, n, 0, :], ACT.Exp, bias=q_neg[:, n:n + 1],
                                       accum_out=q_sum[:, n:n + 1])
                    free(act.activation(v_lin[:], w[:, :, 1, :], ACT.Copy), "qv")
                if slot == SLOT["k_exp"]:
                    act.wait_ge(k_max_ready, b + 1)
                    free(act.activation(k_exp[:], bank_of("k")[:, 0:S], ACT.Exp, bias=k_neg[:], accum_out=k_sum[:]),
                         "k")
                if slot == SLOT["qk_T"]:
                    full(act, t, "qk_T")
                    free(act.activation(qk_T[:].rearrange("p n s -> p (n s)"), bank_of("qk_T")[:], ACT.Copy), "qk_T")
                if slot == SLOT["lin_ctx"]:
                    full(act, t, "lin_ctx")
                    free(act.activation(ctx_lin[:], bank_of("lin_ctx")[:, 0:D], ACT.Copy), "lin_ctx")

            def norm(t, slot):
                b = t - NORM
                if slot == SLOT["h_T"]:
                    full(act, t, "h_T")
                    free(act.activation(xnT[:], bank_of("h_T")[:, 0:S], ACT.Identity, bias=vec(LN1B), scale=vec(LN1G)),
                         "h_T")
                if slot == SLOT["qk"]:
                    full(act, t, "qk")
                    wait(act, qk_split, 4 * b)
                    for n in range(2):
                        last = act.activation(qkf[:, n, :], bank_of("qk")[:, n * S:(n + 1) * S], ACT.Identity,
                                              bias=vec(BQ + n))
                    free(last, "qk")
                if slot == SLOT["part0"]:
                    taken(act, t, "qk")
                    wait(act, split_stored, 32 * b)
                    act.activation(parts[:, :, 0, :], qkf[:], ACT.Copy).then_inc(qk_split, 1)

            def spread(t, slot):
                if slot == SLOT["part1"]:
                    act.wait_ge(qk_split, 4 * (t - SPREAD) + 2)
                    act.activation(parts[:, :, 1, :], qkf[:], ACT.Copy).then_inc(qk_split, 1)

            def back(t, slot):
                b = t - BACK
                if slot == SLOT["ctx_T"]:
                    full(act, t, "ctx_T")
                    free(act.activation(o_T[:], bank_of("ctx_T")[:, 0:S], ACT.Copy), "ctx_T")
                if slot == SLOT["moe_in_T"]:
                    full(act, t, "moe_in_T")
                    wait(act, kept, 2 * b)
                    free(act.activation(xmT[:], bank_of("moe_in_T")[:, 0:S], ACT.Identity, bias=vec(LN2B),
                                        scale=vec(LN2G)), "moe_in_T")

            drive(act, iteration)

            act.wait_ge(route_step, 4)
            act.activation(shifted[:].rearrange("p t n -> p (t n)"), shifted[:].rearrange("p t n -> p (t n)"), ACT.Exp
                           ).then_inc(route_exp, 1)

            def shared_gelu(k, n):
                g = 2 * k + n
                if later(k):
                    act.wait_ge(down_full, g - 1)
                for c in range(FC):
                    act.wait_ge(up_full, g * FC + c + 1)
                    act.activation(hid[:, n, c, :], bank[4 + c % 2][:], ACT.Gelu, bias=vec(B1 + E * FC + c)
                                   ).then_inc(gelu_done, 1)

            drive_groups(act, shared_gelu)

            def moe_turn(k, n):
                k, n, j = moe_tile(k, n)
                if j is not None:
                    act.wait_ge(tile_T_full, j + 1)
                    wait(act, moe_up_full, j - NB + 1)
                    act.activation(tile_T[:, n, :], bank[n % 2][:, 0:P], ACT.Identity, bias=vec(LN2B), scale=vec(LN2G)
                                   ).then_inc(tile_T_ready, 1)

            def moe_gelu(k, n):
                k, n, j = moe_tile(k, n)
                if j is not None:
                    act.wait_ge(moe_up_full, j + 1)
                    wait(act, moe_y_full, j - NB + 1)
                    for c in range(FC):
                        act.activation(hid_moe[:, n, c, :], bank[2 + n][:, c * P:(c + 1) * P], ACT.Gelu,
                                       bias=staged[:, n, WB1 + c:WB1 + c + 1]).then_inc(moe_gelu_done, 1)

            def moe_step(k, n):
                moe_gelu(k, n)
                moe_turn(k, n + 2)

            moe_turn(0, 0)
            moe_turn(0, 1)
            drive_tiles(act, moe_step)

            tiles = TILES // FG
            for g in range(FG):
                act.wait_ge(fin_step[g], 2)
                act.dma_start(out_d[g * B // FG:(g + 1) * B // FG].rearrange("b (n p) d -> p (b n) d", p=P),
                              fin[:, g * tiles:(g + 1) * tiles, :]).then_inc(fin_stored, 16)


        @block.vector
        def _(dve):
            dve.memset(half_neg[:], -0.5).then_inc(half_ready, 1)
            dve.wait_ge(ident_ready, 2)
            dve.tensor_copy(ident_half[:], ident[:]).then_inc(half_ready, 1)
            dve.memset(va[:], 1.0).then_inc(half_ready, 1)
            dve.wait_ge(silu_exp, 1)
            dve.tensor_scalar(c_exp, c_exp, 1.0, None, ALU.add).then_inc(silu_step, 1)
            dve.wait_ge(silu_step, 1)
            dve.reciprocal(c_exp, c_exp).then_inc(silu_step, 1)
            dve.wait_ge(silu_step, 2)
            dve.tensor_tensor(c_silu, c_in, c_exp, ALU.mult).then_inc(silu_step, 1)
            dve.wait_ge(setup_full, 1)
            dve.tensor_copy(c_T, bank[0][:, 0:B]).then_inc(setup_taken, 1)
            dve.wait_ge(setup_full, 2)
            dve.tensor_copy(vecs_T[:, 0:NVEC], bank[1][:, 0:NVEC]).then_inc(setup_taken, 1)
            dve.wait_ge(setup_full, 4)
            for n in range(2):
                dve.tensor_copy(mods[:, 3 * n:3 * n + 3, :],
                                bank[2 + n][0:B, 0:3 * D].rearrange("b (n d) -> b n d", d=D)).then_inc(mod_step, 1)
            dve.wait_ge(mod_step, 2)
            dve.tensor_scalar(mods[:, 1, :], mods[:, 1, :], 1.0, None, ALU.add).then_inc(mod_step, 1)
            dve.tensor_scalar(mods[:, 4, :], mods[:, 4, :], 1.0, None, ALU.add).then_inc(mods_ready, 1)
            steps = 3
            for n, row in enumerate((2, 5)):
                g = mods[:, row, :]
                if n:
                    dve.wait_ge(mods_ready, 2)
                dve.tensor_scalar(gsign, g, 0.0, 2.0, ALU.is_ge, ALU.mult).then_inc(mod_step, 1)
                dve.tensor_scalar(gabs, g, -1.0, 0.25, ALU.mult, ALU.max).then_inc(mod_step, 1)
                dve.wait_ge(mod_step, steps + 2)
                dve.tensor_tensor(gabs, gabs, g, ALU.max).then_inc(mod_step, 1)
                dve.wait_ge(mod_step, steps + 3)
                dve.scalar_tensor_tensor(g, gsign, -1.0, gabs, ALU.add, ALU.mult).then_inc(mods_ready, 1)
                steps += 3
            dve.wait_ge(setup_full, 6)
            dve.tensor_copy(modT[:].rearrange("p n b -> p (n b)"), bank[0][:, 0:2 * B]).then_inc(setup_taken, 1)
            dve.wait_ge(weights_loaded, 16 * len(WEIGHTS))

            def free(ins, name):
                ins.then_inc(work_free[JOB[name] % 2], 1)

            def bank_of(name):
                return work[JOB[name] % 2]

            def moments(src, st, mv, b, stats, mean):
                for n in range(TPB):
                    dve.bn_stats(st[:, n, :], src(n)).then_inc(stats, 1)
                wait_apart(dve, stats, 2 * b + 2)
                for n in range(TPB):
                    dve.bn_aggr(mv[:, n, :], st[:, n, :]).then_inc(mean, 1)

            def normalise(dst, src, mv, rs, b, rstd, norm):
                dve.wait_ge(rstd, 2 * b + 2)
                for n in range(TPB):
                    dve.tensor_scalar(dst[:, n:n + 1, :], src(n), mv[:, n, 0:1], rs[:, n:n + 1], ALU.subtract, ALU.mult
                                      ).then_inc(norm, 1)

            def iteration(t, r):
                for slot in range(HEADS):
                    if active(t, MAX):
                        b = t - MAX
                        half = slot // HALF
                        if slot % HALF == 0:
                            wait(dve, max_split[half], 4 * b)
                        dve.wait_ge(max_full, b * HEADS + slot + 1)
                        dve.tensor_reduce(neg_max[:, slot // HALF, :, slot % HALF],
                                          max_bank[slot % 2][:].rearrange("p (q k) -> p q k", q=TPB), AX.X, ALU.max,
                                          negate=True).then_inc(max_done, 1)
                    if active(t, FRONT):
                        front(t, slot)
                    if active(t, NORM):
                        norm(t, slot)
                    if active(t, SPREAD):
                        spread(t, slot, (r - SPREAD) % NBUF)
                    if active(t, BACK):
                        back(t, slot)
                    if active(t, LOAD) and slot == SLOT["stats_a"]:
                        wait_apart(dve, x_loaded, 16 * (t - LOAD) + 16)
                        moments(lambda n: tile(res, t, n), st_a, mv_a, t, stats_a, mean_a)
                    if active(t, LOAD) and slot == SLOT["norm_a"]:
                        if active(t, FRONT):
                            full(dve, t, "x_T")
                        normalise(xn, lambda n: tile(res, t, n), mv_a, rs_a, t, rstd_a, norm_a)

            def front(t, slot):
                b = t - FRONT
                if slot == SLOT["qv"]:
                    full(dve, t, "qv")
                    w = bank_of("qv")[:].rearrange("p (n two d) -> p n two d", n=TPB, two=2)
                    dve.tensor_reduce(q_neg[:], w[:, :, 0, :], AX.X, ALU.max, negate=True).then_inc(q_max_ready, 1)
                if slot == SLOT["k"]:
                    full(dve, t, "k")
                    dve.tensor_reduce(k_neg[:], bank_of("k")[:, 0:S], AX.X, ALU.max, negate=True
                                      ).then_inc(k_max_ready, 1)
                if slot == SLOT["recips"]:
                    taken(dve, t, "k")
                    dve.reciprocal(k_rec[:], k_sum[:]).then_inc(recips, 1)
                    dve.reciprocal(q_rec[:], q_sum[:]).then_inc(recips, 1)
                if slot == SLOT["lin_m"]:
                    dve.wait_ge(recips, 2 * b + 2)
                    full(dve, t, "lin_m")
                    free(dve.tensor_scalar(m_lin[:], bank_of("lin_m")[:, 0:D], k_rec[:], LIN_SCALE, ALU.mult, ALU.mult),
                         "lin_m")
                if slot == SLOT["lin_out"]:
                    full(dve, t, "lin_out")
                    for n in range(TPB):
                        last = dve.scalar_tensor_tensor(y_lin[:, n, :], bank_of("lin_out")[:, n * D:(n + 1) * D],
                                                        q_rec[:, n:n + 1], b_lo[:], ALU.mult, ALU.add)
                    free(last, "lin_out")

            def norm(t, slot):
                b = t - NORM
                if slot == SLOT["stats_b"]:
                    wait_apart(dve, x1_ready, b + 1)
                    moments(lambda n: tile(res, b, n), st_b, mv_b, b, stats_b, mean_b)
                if slot == SLOT["norm_b"]:
                    normalise(h_norm, lambda n: tile(res, b, n), mv_b, rs_b, b, rstd_b, norm_b)
                if slot == SLOT["stats_c"]:
                    wait_apart(dve, h2_ready, b + 1)
                    moments(lambda n: tile(keep, b, n), st_c, mv_c, b, stats_c, mean_c)
                if slot == SLOT["norm_c"]:
                    normalise(xc, lambda n: tile(keep, b, n), mv_c, rs_c, b, rstd_c, norm_c)

            def spread(t, slot, buf):
                b = t - SPREAD
                if slot == SLOT["v"]:
                    full(dve, t, "v")
                    wait(dve, pv_done, (b - NBUF + 1) * HEADS)
                    free(dve.tensor_tensor(
                        va[:, buf, :, 0:HEADS * VW].rearrange("p n (h w) -> p n h w", w=VW)[:, :, :, 0:DH],
                        bank_of("v")[:, 0:TPB * D].rearrange("p (n h d) -> p n h d", n=TPB, d=DH),
                        b_v[:].rearrange("p (h d) -> p h d", d=DH).unsqueeze(1).to_broadcast([P, TPB, HEADS, DH]),
                        ALU.add), "v")

            def back(t, slot):
                b = t - BACK
                if slot in (SLOT["ctx_rows0"], SLOT["ctx_rows1"]):
                    n = slot - SLOT["ctx_rows0"]
                    name = f"ctx_rows{n}"
                    full(dve, t, name)
                    w = bank_of(name)[:].rearrange("p (h c) -> p h c", c=32)
                    dve.reciprocal(o_rec[:, n, :], w[:, :, DH]).then_inc(o_rec_ready, 1)
                    dve.wait_ge(o_rec_ready, 2 * b + n + 1)
                    free(dve.tensor_tensor(o_rows[:, n, :].rearrange("p (h d) -> p h d", d=DH), w[:, :, 0:DH],
                                           o_rec[:, n, :].unsqueeze(2).to_broadcast([P, HEADS, DH]), ALU.mult), name)
                if slot == SLOT["att_out"]:
                    full(dve, t, "att_out")
                    dve.wait_ge(h2b_ready, b + 1)
                    wait(dve, x3_scaled, b)
                    free(dve.tensor_tensor(x3[:], bank_of("att_out")[:, 0:TPB * D].rearrange("p (n d) -> p n d", d=D),
                                           h2b[:], ALU.add), "att_out")
                if slot == SLOT["stats_d"]:
                    taken(dve, t, "att_out")
                    moments(lambda n: x3[:, n:n + 1, :], st_d, mv_d, b, stats_d, mean_d)
                if slot == SLOT["norm_d"]:
                    wait(dve, kept, 2 * b)
                    normalise(xm, lambda n: x3[:, n:n + 1, :], mv_d, rs_d, b, rstd_d, norm_d)
                if slot == SLOT["logits"]:
                    full(dve, t, "logits")
                    free(dve.tensor_tensor(batch(logit, b), bank_of("logits")[:, 0:TPB * NL]
                                           .rearrange("p (n d) -> p n d", d=NL),
                                           b_log[:].unsqueeze(1).to_broadcast([P, TPB, NL]), ALU.add), "logits")

            drive(dve, iteration)

            count = [0]

            def step(ins):
                ins.then_inc(route_step, 1)
                count[0] += 1
                dve.wait_ge(route_step, count[0])

            def per_tile(x, n):
                return x.unsqueeze(2).to_broadcast([P, TILES, n])

            def tiles_experts(x):
                return x.rearrange("p (t e) -> p t e", e=E)

            for n in range(2):
                dve.wait_ge(work_free[n], bank_uses(PIPE, n))
            dve.wait_ge(res_ready, B)
            dve.wait_ge(kept, 2 * B)
            dve.memset(ones[:], 1.0).then_inc(ones_set, 1)
            gates = logit[:, :, 0:E]
            step(dve.tensor_reduce(lmax[:, 0, :], gates, AX.X, ALU.max))
            step(dve.tensor_reduce(lmax[:, 1, :], logit[:, :, E:NL], AX.X, ALU.max))
            step(dve.tensor_tensor(shifted[:, :, 0:E], gates, per_tile(lmax[:, 0, :], E), ALU.subtract))
            step(dve.tensor_tensor(shifted[:, :, E:NL], logit[:, :, E:NL], per_tile(lmax[:, 1, :], 2), ALU.subtract))
            key, a, incl, tot = (tiles_experts(route_buf(n, TILES * E)) for n in range(4))
            onehot3 = tiles_experts(onehot[:])
            step(dve.tensor_tensor(key, gates, per_tile(lmax[:, 0, :], E), ALU.is_equal))
            step(dve.tensor_tensor(key, key, order[:].unsqueeze(1).to_broadcast([P, TILES, E]), ALU.mult))
            step(dve.tensor_reduce(w_moe[:], key, AX.X, ALU.max))
            step(dve.tensor_tensor(onehot3, key, per_tile(w_moe[:], E), ALU.is_equal))
            dve.wait_ge(counts_full, 2)
            step(dve.tensor_copy(tot, tiles_experts(bank[3][:])))
            incl = route_buf(2, TILES * E).rearrange("p (e t) -> p e t", t=TILES)
            zero = route_buf(4, TILES)
            step(dve.memset(zero, 0.0))
            for e in range(E):
                dve.tensor_tensor_scan(incl[:, e, :], tot[:, :, e], zero, 0.0, ALU.add, ALU.add).then_inc(route_step, 1)
            count[0] += E
            dve.wait_ge(route_step, count[0])
            tiles_e, ends, base = small[:, 0, :], small[:, 1, :], small[:, 2, :]
            cmp = y_shared[:].rearrange("p n d -> p (n d)").rearrange("p (e t) -> p e t", t=TILES)
            step(dve.tensor_tensor(cmp, tile_first[:].unsqueeze(1).to_broadcast([P, E, TILES]),
                                   incl[:, :, TILES - 1:TILES].to_broadcast([P, E, TILES]), ALU.is_lt))
            step(dve.tensor_reduce(tiles_e, cmp, AX.X, ALU.add))
            step(dve.tensor_tensor_scan(ends, tiles_e, zero[:, 0:E], 0.0, ALU.add, ALU.add))
            step(dve.tensor_tensor(base, ends, tiles_e, ALU.subtract))
            step(dve.tensor_scalar(base, base, float(P), None, ALU.mult))
            step(dve.tensor_tensor(a, incl.rearrange("p e t -> p t e"), tot, ALU.subtract))
            step(dve.tensor_tensor(a, a, tiles_experts(bank[2][:]), ALU.add))
            step(dve.tensor_tensor(a, a, base.unsqueeze(1).to_broadcast([P, TILES, E]), ALU.add))
            step(dve.tensor_tensor(a, a, onehot3, ALU.mult))
            step(dve.tensor_reduce(lmax[:, 0, :], a, AX.X, ALU.add))
            step(dve.tensor_copy(slot_u[:], lmax[:, 0, :]))
            cmp2 = route_buf(0, MAX_TILES * (E - 1)).rearrange("p (t e) -> p t e", e=E - 1)
            step(dve.tensor_tensor(cmp2, ends[:, 0:E - 1].unsqueeze(1).to_broadcast([P, MAX_TILES, E - 1]),
                                   tile_no[:].unsqueeze(2).to_broadcast([P, MAX_TILES, E - 1]), ALU.is_le))
            exp_f = route_buf(4, MAX_TILES)
            step(dve.tensor_reduce(exp_f, cmp2, AX.X, ALU.add))
            step(dve.tensor_copy(expert_u[:], exp_f))
            dve.wait_ge(route_exp, 1)
            step(dve.tensor_reduce(w_moe[:], shifted[:, :, 0:E], AX.X, ALU.add))
            step(dve.tensor_reduce(w_rm[:], shifted[:, :, E:NL], AX.X, ALU.add))
            step(dve.reciprocal(w_moe[:], w_moe[:]))
            step(dve.reciprocal(w_rm[:], w_rm[:]))
            step(dve.tensor_tensor(w_moe[:], w_moe[:], w_rm[:], ALU.mult))
            step(dve.tensor_tensor(token_meta[:, :, 1], w_moe[:], shifted[:, :, E], ALU.mult))
            dve.tensor_tensor(w_rm[:], w_rm[:], shifted[:, :, E + 1], ALU.mult).then_inc(route_ready, 1)
            dve.wait_ge(route_ready, 1)

            dve.wait_ge(experts_loaded, 16 * 3 * E)
            b1_all = vecs_T[:, B1:B1 + E * FC].rearrange("p (e c) -> p e c", c=FC)
            dve.tensor_copy(w_exp[:, :, WB1:WB2], b1_all).then_inc(weight_step, 1)

            def stage_rows(k, n):
                g = 2 * k + n
                group = bass.ds(g * GT, GT)
                if later(k):
                    dve.wait_ge(sorted_sem[n], 16 * GT * k)
                dve.tensor_copy(out_rows[:, n, :, 0:D], keep[:, group, :]).then_inc(scatter_staged, 1)
                dve.tensor_copy(out_rows[:, n, :, D:ROW], token_meta[:, group, :]).then_inc(scatter_staged, 1)
                dve.tensor_copy(out_slots[:, n, :], slot_u[:, group]).then_inc(scatter_staged, 1)

            dve.wait_ge(shared_loaded, 16 * len(SHARED_WEIGHTS))

            def shared_out(k, n):
                g = 2 * k + n
                wn = w_rm[:, bass.ds(g * GT, GT)].unsqueeze(2).to_broadcast([P, GT, D])
                dve.wait_ge(down_full, g + 1)
                wait(dve, shared_added, g)
                dve.tensor_tensor(y_shared[:], bank[6 + n][:].rearrange("p (m d) -> p m d", d=D),
                                  over(w_shared[:, WB2:WCOLS], GT), ALU.add).then_inc(down_taken, 1)
                dve.wait_ge(down_taken, g + 1)
                dve.tensor_tensor(y_shared[:], y_shared[:], wn, ALU.mult).then_inc(shared_step, 1)
                dve.wait_ge(shared_step, 2 * g + 1)
                dve.wait_ge(gb2_loaded, 16 * g + 16)
                y4 = y_shared[:].rearrange("p (b n) d -> p b n d", n=TPB)
                dve.tensor_tensor(y4, y4, gb2[:].unsqueeze(2).to_broadcast([P, GB, TPB, D]), ALU.mult
                                  ).then_inc(shared_step, 1)
                dve.wait_ge(shared_step, 2 * g + 2)
                rows = res[:, bass.ds(g * GT, GT), :]
                dve.tensor_tensor(rows, rows, y_shared[:], ALU.add).then_inc(shared_added, 1)

            last_k = GROUPS // 2 - 1
            for n in range(2):
                stage_rows(0, n)
            for n in range(2):
                shared_out(0, n)
                stage_rows(1, n)
            with dve.Fori(1, last_k) as k:
                for n in range(2):
                    shared_out(k, n)
                    stage_rows(k + 1, n)
            shared_out(last_k, 0)

            dve.wait_ge(weight_step, 1)

            def load_expert(k, n):
                k, n, j = moe_tile(k, n)
                if j is not None:
                    return dve.value_load(expert_u[0:1, bass.ds(j, 1)], min_val=0, max_val=E - 1)

            def stage_weights(k, n, expert):
                k, n, j = moe_tile(k, n)
                if j is not None:
                    wait(dve, moe_y_taken, j - NB + 1)
                    dve.tensor_copy(staged[:, n, :], w_exp[:, bass.ds(expert, 1), :].rearrange("p e w -> p (e w)")
                                    ).then_inc(stage_ready, 1)

            def take_meta(k, n):
                k, n, j = moe_tile(k, n)
                if j is not None:
                    dve.wait_ge(rows_in_loaded[n], 16 * k + 16)
                    wait(dve, y_weighted, 2 * (j - NB + 1))
                    dve.tensor_copy(meta[:, n, :], rows_buf[:, n, D:ROW]).then_inc(meta_taken, 1)

            def moe_out(k, n):
                k, n, j = moe_tile(k, n)
                if j is not None:
                    dve.wait_ge(moe_y_full, j + 1)
                    dve.wait_ge(stage_ready, j + 1)
                    dve.tensor_tensor(y_moe[:, n, :], bank[6 + n % 2][:, 0:D], staged[:, n, WB2:WCOLS], ALU.add
                                      ).then_inc(moe_y_taken, 1)
                    dve.wait_ge(meta_taken, j + 1)
                    if later(k):
                        dve.wait_ge(moe_scattered[n], 16 * k)
                    dve.tensor_copy(meta_slot[:, n:n + 1], meta[:, n, 0:1]).then_inc(y_weighted, 1)
                    dve.wait_ge(moe_y_taken, j + 1)
                    dve.tensor_scalar(y_out[:, n, :], y_moe[:, n, :], meta[:, n, 1:2], None, ALU.mult
                                      ).then_inc(y_weighted, 1)

            def moe_step(k, n):
                take_meta(k, n)
                expert = load_expert(k, n + 2)
                moe_out(k, n - 2)
                stage_weights(k, n + 2, expert)

            dve.wait_ge(up_full, GROUPS * FC)
            for n in range(2):
                stage_weights(0, n, load_expert(0, n))
            shared_out(last_k, 1)
            drive_tiles(dve, moe_step)

            add_experts(dve, [g for g in range(FG) if g not in POOL_GROUPS])

        @block.gpsimd
        def _(pool):
            pool.memset(ident[:], 0.0).then_inc(ident_ready, 1)
            pool.wait_ge(ident_ready, 1)
            pool.affine_select(out=ident[:], in_=ident[:], compare_op=ALU.not_equal, fill=1.0, base=0,
                               pattern=[[-1, P]], channel_multiplier=1).then_inc(ident_ready, 1)
            pool.iota(tile_first[:], [[P, TILES]], base=0, channel_multiplier=0, allow_small_or_imprecise_dtypes=True
                      ).then_inc(consts_ready, 1)
            pool.iota(tile_no[:], [[1, MAX_TILES]], base=0, channel_multiplier=0, allow_small_or_imprecise_dtypes=True
                      ).then_inc(consts_ready, 1)
            pool.iota(order[:], [[-1, E]], base=E, channel_multiplier=0, allow_small_or_imprecise_dtypes=True
                      ).then_inc(consts_ready, 1)
            pool.iota(token_meta[:, :, 0], [[P, TILES]], base=0, channel_multiplier=1,
                      allow_small_or_imprecise_dtypes=True).then_inc(consts_ready, 1)
            pool.memset(slots0[:], 0.0).then_inc(slots_cleared, 1)
            pool.wait_ge(slots_cleared, 1)

            def number_slots(first, n):
                pool.iota(slots0[:, 0:n, D], [[P, n]], base=B * S + first * P, channel_multiplier=1,
                          allow_small_or_imprecise_dtypes=True).then_inc(slots_cleared, 1)

            number_slots(0, CLEAR)
            pool.wait_ge(half_ready, 3)

            def rstd(mv, rs, b, mean, ready):
                wait_apart(pool, mean, 2 * b + 2)
                pool.tensor_scalar(rs[:], mv[:, :, 1], EPS, None, ALU.add).then_inc(ready, 1)
                wait_apart(pool, ready, 2 * b + 1)
                pool.tensor_tensor(rs[:], rs[:], half_neg[:], ALU.pow).then_inc(ready, 1)

            def split_max(b, half):
                left, done = neg_max[:, half], max_split[half]
                for i in range(2):
                    pool.tensor_copy(max_cols[:, half, :, i, :], left).then_inc(done, 1)
                    wait_apart(pool, done, 4 * b + 2 * i + 1)
                    out = left if i == 0 else max_cols[:, half, :, 2, :]
                    pool.tensor_tensor(out, left, max_cols[:, half, :, i, :], ALU.subtract).then_inc(done, 1)
                    if i == 0:
                        wait_apart(pool, done, 4 * b + 2)

            def iteration(t, r):
                if isinstance(t, int) and t == 1:
                    pool.memset(k_all[:], 1.0).then_inc(ones_ready, 1)
                if isinstance(t, int) and t == 4:
                    pool.wait_ge(slots_stored, 16)
                    number_slots(CLEAR, MAX_TILES - CLEAR)
                if isinstance(t, int) and t == BACK:
                    pool.wait_ge(slots_stored, 32)
                if active(t, EXP):
                    b = t - EXP
                    if active(t - 1, EXP):
                        full(pool, t - 1, "max_T_hi", wait_apart)
                    wait_apart(pool, max_done, b * HEADS + HEADS)
                    split_max(b, 1)
                for slot in range(HEADS):
                    if active(t, MAX) and slot == HALF:
                        b = t - MAX
                        if active(t - 1, MAX):
                            full(pool, t - 1, "max_T_lo", wait_apart)
                        wait_apart(pool, max_done, b * HEADS + HALF)
                        split_max(b, 0)
                    if active(t, FRONT):
                        front(t, slot)
                    if active(t, NORM):
                        norm(t, slot)
                    if active(t, BACK):
                        back(t, slot)
                    if active(t, NORM) and slot == SLOT["part0"]:
                        wait_apart(pool, qk_split, 4 * (t - NORM) + 1)
                        pool.tensor_tensor(qkf[:], qkf[:], parts[:, :, 0, :], ALU.subtract).then_inc(qk_split, 1)
                    if active(t, SPREAD) and slot == SLOT["part1"]:
                        wait_apart(pool, qk_split, 4 * (t - SPREAD) + 3)
                        pool.tensor_tensor(parts[:, :, 2, :], qkf[:], parts[:, :, 1, :], ALU.subtract
                                           ).then_inc(qk_split, 1)
                    if active(t, LOAD) and slot == SLOT["stats_a"]:
                        rstd(mv_a, rs_a, t, mean_a, rstd_a)
            def front(t, slot):
                b = t - FRONT
                if slot == SLOT["lin_out"]:
                    taken(pool, t, "lin_out", wait_apart)
                    wait_apart(pool, ga_loaded, 16 * b + 16)
                    pool.tensor_tensor(y_lin[:], y_lin[:], over(mod_ga[:, 0, :], TPB), ALU.mult).then_inc(y_scaled, 1)
                    wait_apart(pool, y_scaled, b + 1)
                    pool.tensor_tensor(batch(res, b), batch(res, b), y_lin[:], ALU.add).then_inc(x1_ready, 1)

            def norm(t, slot):
                b = t - NORM
                if slot == SLOT["stats_b"]:
                    rstd(mv_b, rs_b, b, mean_b, rstd_b)
                if slot == SLOT["norm_b"]:
                    wait_apart(pool, norm_b, 2 * b + 2)
                    wait_apart(pool, modb_loaded, 16 * b + 16)
                    pool.tensor_tensor(h_norm[:], h_norm[:], over(mod_b[:, 0, :], TPB), ALU.mult).then_inc(h_scaled, 1)
                    wait_apart(pool, h_scaled, b + 1)
                    pool.tensor_tensor(batch(keep, b), h_norm[:], over(mod_b[:, 1, :], TPB), ALU.add
                                       ).then_inc(h2_ready, 1)
                if slot == SLOT["stats_c"]:
                    rstd(mv_c, rs_c, b, mean_c, rstd_c)

            def back(t, slot):
                b = t - BACK
                if slot == SLOT["h2b"]:
                    wait_apart(pool, res_ready, b)
                    pool.tensor_tensor(h2b[:], batch(keep, b), over(b_ao[:], TPB), ALU.add).then_inc(h2b_ready, 1)
                if slot == SLOT["stats_d"]:
                    rstd(mv_d, rs_d, b, mean_d, rstd_d)
                    wait_apart(pool, gb_loaded, 16 * b + 16)
                    pool.tensor_tensor(h2b[:], x3[:], mod_gb[:].to_broadcast([P, TPB, D]), ALU.mult
                                       ).then_inc(x3_scaled, 1)
                    wait_apart(pool, x3_scaled, b + 1)
                    pool.tensor_tensor(batch(res, b), batch(res, b), h2b[:], ALU.add).then_inc(res_ready, 1)
                if slot == SLOT["norm_d"]:
                    wait_apart(pool, norm_d, 2 * b + 2)
                    pool.tensor_copy(batch(keep, b), xm[:]).then_inc(kept, 1)
                if slot == SLOT["keep_T"]:
                    taken(pool, t, "moe_in_T", wait_apart)
                    pool.tensor_copy(moe_in_T[:, bass.ds(b * S, S)], xmT[:]).then_inc(kept, 1)

            drive(pool, iteration)

            pool.wait_ge(ones_set, 1)
            pool.affine_select(out=upper[:], in_=ones[:], compare_op=ALU.is_gt, fill=0.0, base=0,
                               pattern=[[1, P]], channel_multiplier=-1).then_inc(consts_ready, 1)

            pool.wait_ge(route_ready, 1)

            def scatter(k, n):
                wait_apart(pool, scatter_staged, 3 * (2 * k + n) + 3)
                for m in range(GT):
                    pool.indirect_dma_start(
                        sorted_dram, bass.IndirectOffsetOnAxis(ap=out_slots[:, n, m:m + 1], axis=0),
                        out_rows[:, n, m, :], None).then_inc(sorted_sem[n], 16)

            drive_groups(pool, scatter)

            def scatter_moe(k, n):
                k, n, j = moe_tile(k, n)
                if j is not None:
                    wait_apart(pool, y_weighted, 2 * j + 2)
                    pool.indirect_dma_start(moe_dram, bass.IndirectOffsetOnAxis(ap=meta_slot[:, n:n + 1], axis=0),
                                            y_out[:, n, :], None).then_inc(moe_scattered[n], 16)

            drive_tiles(pool, scatter_moe)

            add_experts(pool, POOL_GROUPS)


INPUTS = ("x c wmod wqkv_lin wo_lin bo_lin vec wqkv bqk bv wo bo wlog blog w1 b1 w2 b2").split()


def kernel(L0_attn_x, L0_attn_Wq, L0_attn_Wk, L0_attn_Wv, L0_attn_Wo, L0_attn_bo, L0_ffn_ln1_g, L0_ffn_ln1_b,
           L0_ffn_Wqkv, L0_ffn_bqkv, L0_ffn_Wo, L0_ffn_bo, L0_ffn_ln2_g, L0_ffn_ln2_b, L0_ffn_gate_w, L0_ffn_W1,
           L0_ffn_b1, L0_ffn_W2, L0_ffn_b2, L0_ffn_rW1, L0_ffn_rb1, L0_ffn_rW2, L0_ffn_rb2, L0_ffn_coef_w,
           L0_ffn_coef_b, L0_c, L0_wmod):
    import numpy as np
    import concourse.bacc as bacc
    from concourse.bass_utils import run_bass_kernel_spmd

    def heads_last(w):
        w = np.asarray(w)
        return w.reshape(*w.shape[:-1], HEADS, DH).swapaxes(-1, -2).reshape(w.shape)

    wqkv, bqkv = np.asarray(L0_ffn_Wqkv), np.asarray(L0_ffn_bqkv)
    data = {
        "x": L0_attn_x, "c": L0_c, "wmod": L0_wmod,
        "wqkv_lin": np.stack([L0_attn_Wq, L0_attn_Wk, L0_attn_Wv]), "wo_lin": L0_attn_Wo, "bo_lin": L0_attn_bo,
        "vec": np.stack([L0_ffn_ln1_g, L0_ffn_ln1_b, L0_ffn_ln2_g, L0_ffn_ln2_b]),
        "wqkv": np.concatenate([heads_last(wqkv[:, 0:D]), heads_last(wqkv[:, D:2 * D]), wqkv[:, 2 * D:]], 1),
        "bqk": np.stack([heads_last(bqkv[0:D]), heads_last(bqkv[D:2 * D])]), "bv": bqkv[2 * D:],
        "wo": L0_ffn_Wo, "bo": L0_ffn_bo,
        "wlog": np.concatenate([L0_ffn_gate_w, L0_ffn_coef_w], 1),
        "blog": np.concatenate([np.zeros(E, np.float32), L0_ffn_coef_b]),
        "w1": np.concatenate([L0_ffn_W1, np.asarray(L0_ffn_rW1)[None]]),
        "b1": np.concatenate([L0_ffn_b1, np.asarray(L0_ffn_rb1)[None]]).reshape((E + 1) * FC, P),
        "w2": np.concatenate([L0_ffn_W2, np.asarray(L0_ffn_rW2)[None]]),
        "b2": np.concatenate([L0_ffn_b2, np.asarray(L0_ffn_rb2)[None]]),
    }
    nc = bacc.Bacc("TRN2", target_bir_lowering=False, num_devices=1)
    arrays, args = {}, []
    for name in INPUTS:
        a = np.ascontiguousarray(data[name])
        arrays[f"in_{name}"] = a
        args.append(nc.dram_tensor(f"in_{name}", a.shape, mybir.dt.from_np(a.dtype), kind="ExternalInput").ap())
    out = nc.dram_tensor("out", [B, S, D], F32, kind="ExternalOutput").ap()
    adaln_block(nc, *args, out)
    got = run_bass_kernel_spmd(nc, [arrays], core_ids=[0])
    return got.results[0]["out"]
```
